# Optimizing a Trainium2 kernel written in Bass

```python
import numpy as np
import jax
import jax.numpy as jnp

def _softmax(x, axis=-1):
    return jax.nn.softmax(x, axis=axis)

def _gelu(x):
    return jax.nn.gelu(x, approximate=True)

def _silu(x):
    return jax.nn.silu(x)

def _sigmoid(x):
    return jax.nn.sigmoid(x)

def _layernorm(x, axis=-1, eps=1e-05):
    m = jnp.mean(x, axis=axis, keepdims=True)
    v = jnp.var(x, axis=axis, keepdims=True)
    return (x - m) / jnp.sqrt(v + eps)

def _scatter_add(tgt, idx, src, axis=0):
    return tgt.at[idx].add(src)

def _segment_sum(src, seg, n):
    return jax.ops.segment_sum(src, seg, n)
kernel_name = 'mk_adj_ffn_d1_adj_r2_f1433f'

def setup_inputs(seed: int=0):
    np.random.seed(seed)
    _w = jnp.asarray

    def _rec_inputs():
        import jax
        import jax.numpy as jnp
        _gk = jax.random.key(seed)
        x = -0.0001538 + 1 * jax.random.normal(jax.random.fold_in(_gk, 1), (64, 128, 384), jnp.float32)
        _a = jax.random.bernoulli(jax.random.fold_in(_gk, 2), 0.0625, (64, 128, 128))
        _a = jnp.logical_or(_a, jnp.swapaxes(_a, -1, -2))
        _a = jnp.logical_or(_a, jnp.eye(128, dtype=bool))
        _af = _a.astype(jnp.float32)
        _af = _af * jax.random.uniform(jax.random.fold_in(_gk, 3), (64, 128, 128), jnp.float32, 0.05, 5.06092)
        adj = _af
        return (x, adj)
    x, adj = _rec_inputs()

    def _L0_gnn_setup():
        import jax, jax.numpy as jnp
        import numpy as np
        D_MODEL = 384
        NHEADS = 8
        D_FF = 1536
        B, N = (8, 512)
        EPS = 1e-06

        def _rmsnorm(x, alpha, gamma):
            x = x * jax.lax.rsqrt(jnp.mean(x * x, axis=-1, keepdims=True) + EPS)
            return alpha * x + gamma
        key = jax.random.key(seed)
        ks = jax.random.split(key, 10)
        d, f = (D_MODEL, D_FF)
        s = 1.0 / np.sqrt(d)
        inp = {'x': jax.random.normal(ks[0], (B, N, d), dtype=jnp.float32), 'attn_bias': jax.random.normal(ks[1], (B, N, N), dtype=jnp.float32), 'wq': jax.random.normal(ks[2], (d, d), dtype=jnp.float32) * s, 'bq': jnp.zeros((d,), jnp.float32), 'wk': jax.random.normal(ks[3], (d, d), dtype=jnp.float32) * s, 'bk': jnp.zeros((d,), jnp.float32), 'wv': jax.random.normal(ks[4], (d, d), dtype=jnp.float32) * s, 'bv': jnp.zeros((d,), jnp.float32), 'wo': jax.random.normal(ks[5], (d, d), dtype=jnp.float32) * s, 'bo': jnp.zeros((d,), jnp.float32), 'w1': jax.random.normal(ks[6], (d, f), dtype=jnp.float32) * s, 'b1': jnp.zeros((f,), jnp.float32), 'w2': jax.random.normal(ks[7], (f, d), dtype=jnp.float32) * (1.0 / np.sqrt(f)), 'b2': jnp.zeros((d,), jnp.float32), 'alpha1': jnp.ones((d,), jnp.float32), 'gamma1': jnp.ones((d,), jnp.float32), 'alpha2': jnp.ones((d,), jnp.float32), 'gamma2': jnp.ones((d,), jnp.float32)}
        return inp
    _L0_gnn_all = _L0_gnn_setup()
    _L0_gnn_in = {k: v for k, v in _L0_gnn_all.items() if k in ('wq', 'bq', 'wk', 'bk', 'wv', 'bv', 'wo', 'bo', 'w1', 'b1', 'w2', 'b2', 'alpha1', 'gamma1', 'alpha2', 'gamma2')}
    del _L0_gnn_all

    def _L0_ffn_setup():
        import jax, jax.numpy as jnp
        import numpy as np
        DIM = 384
        GROUP = 128
        E1, S1, E2 = (8, 16, 4)
        MULT = 4
        HID = int(DIM * MULT * 2 / 3)
        B, N = (4, 2048)

        def _l2norm(t, eps=1e-06):
            return t * jax.lax.rsqrt(jnp.sum(t * t, axis=-1, keepdims=True) + eps)

        def _forward(x, gamma_in, slots1, gamma2, w_slot2, w1, b1, w2, b2):
            b, n, d = x.shape
            G, g = (n // GROUP, GROUP)
            scale = d ** 0.5
            xn = _l2norm(x) * scale * gamma_in
            xg = xn.reshape(b, G, g, d)
            phi = _l2norm(slots1) * scale
            logits1 = jnp.einsum('bGgd,esd->bGges', xg, phi)
            disp1 = jax.nn.softmax(logits1, axis=2)
            comb1 = jax.nn.softmax(logits1.reshape(b, G, g, E1 * S1), -1)
            slots = jnp.einsum('bGgd,bGges->bGesd', xg, disp1)
            yn = _l2norm(slots) * scale * gamma2[None, None, :, None, :]
            ns = S1 // E2
            m = S1 // ns
            means = yn.reshape(b, G, E1, m, ns, d).mean(axis=4)
            se2 = jnp.einsum('bGkmd,kdf->bGkmf', means, w_slot2)
            se2 = se2.reshape(b, G, E1, m, E2, d).transpose(0, 1, 2, 4, 3, 5)
            se2 = _l2norm(se2) * scale
            logits2 = jnp.einsum('bGksd,bGkemd->bGksem', yn, se2)
            disp2 = jax.nn.softmax(logits2, axis=3)
            comb2 = jax.nn.softmax(logits2.reshape(b, G, E1, S1, E2 * m), -1)
            slots2 = jnp.einsum('bGksd,bGksem->bGkemd', yn, disp2)
            u = jnp.einsum('bGkemd,kedh->bGkemh', slots2, w1) + b1[None, None, :, :, None, :]
            v, gate = jnp.split(u, 2, axis=-1)
            act = v * jax.nn.gelu(gate)
            o = jnp.einsum('bGkemh,kehd->bGkemd', act, w2) + b2[None, None, :, :, None, :]
            out2 = jnp.einsum('bGkpd,bGksp->bGksd', o.reshape(b, G, E1, E2 * m, d), comb2)
            out = jnp.einsum('bGPd,bGgP->bGgd', out2.reshape(b, G, E1 * S1, d), comb1)
            return out.reshape(b, n, d)
        key = jax.random.key(seed)
        ks = jax.random.split(key, 8)
        p = lambda k, shape, s=0.02: jax.random.normal(k, shape, dtype=jnp.float32) * s
        return {'x': jax.random.normal(ks[0], (B, N, DIM), dtype=jnp.float32), 'gamma_in': jnp.ones((DIM,), jnp.float32), 'slots1': p(ks[1], (E1, S1, DIM), 1.0 / DIM ** 0.5), 'gamma2': jnp.ones((E1, DIM), jnp.float32), 'w_slot2': p(ks[2], (E1, DIM, E2 * DIM)), 'w1': p(ks[3], (E1, E2, DIM, 2 * HID)), 'b1': jnp.zeros((E1, E2, 2 * HID), jnp.float32), 'w2': p(ks[4], (E1, E2, HID, DIM)), 'b2': jnp.zeros((E1, E2, DIM), jnp.float32)}
    _L0_ffn_all = _L0_ffn_setup()
    _L0_ffn_in = {k: v for k, v in _L0_ffn_all.items() if k in ('gamma_in', 'slots1', 'gamma2', 'w_slot2', 'w1', 'b1', 'w2', 'b2')}
    del _L0_ffn_all
    return {'x': x, 'adj': adj, 'L0_gnn_wq': _L0_gnn_in['wq'], 'L0_gnn_bq': _L0_gnn_in['bq'], 'L0_gnn_wk': _L0_gnn_in['wk'], 'L0_gnn_bk': _L0_gnn_in['bk'], 'L0_gnn_wv': _L0_gnn_in['wv'], 'L0_gnn_bv': _L0_gnn_in['bv'], 'L0_gnn_wo': _L0_gnn_in['wo'], 'L0_gnn_bo': _L0_gnn_in['bo'], 'L0_gnn_w1': _L0_gnn_in['w1'], 'L0_gnn_b1': _L0_gnn_in['b1'], 'L0_gnn_w2': _L0_gnn_in['w2'], 'L0_gnn_b2': _L0_gnn_in['b2'], 'L0_gnn_alpha1': _L0_gnn_in['alpha1'], 'L0_gnn_gamma1': _L0_gnn_in['gamma1'], 'L0_gnn_alpha2': _L0_gnn_in['alpha2'], 'L0_gnn_gamma2': _L0_gnn_in['gamma2'], 'L0_ffn_gamma_in': _L0_ffn_in['gamma_in'], 'L0_ffn_slots1': _L0_ffn_in['slots1'], 'L0_ffn_gamma2': _L0_ffn_in['gamma2'], 'L0_ffn_w_slot2': _L0_ffn_in['w_slot2'], 'L0_ffn_w1': _L0_ffn_in['w1'], 'L0_ffn_b1': _L0_ffn_in['b1'], 'L0_ffn_w2': _L0_ffn_in['w2'], 'L0_ffn_b2': _L0_ffn_in['b2']}

def reference(x, adj, L0_gnn_wq, L0_gnn_bq, L0_gnn_wk, L0_gnn_bk, L0_gnn_wv, L0_gnn_bv, L0_gnn_wo, L0_gnn_bo, L0_gnn_w1, L0_gnn_b1, L0_gnn_w2, L0_gnn_b2, L0_gnn_alpha1, L0_gnn_gamma1, L0_gnn_alpha2, L0_gnn_gamma2, L0_ffn_gamma_in, L0_ffn_slots1, L0_ffn_gamma2, L0_ffn_w_slot2, L0_ffn_w1, L0_ffn_b1, L0_ffn_w2, L0_ffn_b2):
    import jax
    import jax.numpy as jnp

    def _L0_gnn_ref(x, attn_bias, wq, bq, wk, bk, wv, bv, wo, bo, w1, b1, w2, b2, alpha1, gamma1, alpha2, gamma2):
        import jax, jax.numpy as jnp
        import numpy as np
        D_MODEL = 384
        NHEADS = 8
        D_FF = 1536
        B, N = (8, 512)
        EPS = 1e-06

        def _rmsnorm(x, alpha, gamma):
            x = x * jax.lax.rsqrt(jnp.mean(x * x, axis=-1, keepdims=True) + EPS)
            return alpha * x + gamma
        b, n, d = x.shape
        h = NHEADS
        dh = d // h
        scaling = dh ** (-0.5)

        def split_heads(t):
            return t.reshape(b, n, h, dh).transpose(0, 2, 1, 3)
        q = split_heads(x @ wq + bq)
        k = split_heads(x @ wk + bk)
        v = split_heads(x @ wv + bv)
        scores = jnp.einsum('bhqd,bhkd->bhqk', q, k) * scaling
        scores = scores + attn_bias[:, None, :, :]
        attn = jax.nn.softmax(scores, axis=-1)
        ctx = jnp.einsum('bhij,bhjd->bhid', attn, v)
        ctx = ctx.transpose(0, 2, 1, 3).reshape(b, n, d)
        attn_out = ctx @ wo + bo
        x = _rmsnorm(x + attn_out, alpha1, gamma1)
        ff = jax.nn.silu(x @ w1 + b1) @ w2 + b2
        x = _rmsnorm(x + ff, alpha2, gamma2)
        return x

    def _L0_ffn_ref(x, gamma_in, slots1, gamma2, w_slot2, w1, b1, w2, b2):
        import jax, jax.numpy as jnp
        import numpy as np
        DIM = 384
        GROUP = 128
        E1, S1, E2 = (8, 16, 4)
        MULT = 4
        HID = int(DIM * MULT * 2 / 3)
        B, N = (4, 2048)

        def _l2norm(t, eps=1e-06):
            return t * jax.lax.rsqrt(jnp.sum(t * t, axis=-1, keepdims=True) + eps)

        def _forward(x, gamma_in, slots1, gamma2, w_slot2, w1, b1, w2, b2):
            b, n, d = x.shape
            G, g = (n // GROUP, GROUP)
            scale = d ** 0.5
            xn = _l2norm(x) * scale * gamma_in
            xg = xn.reshape(b, G, g, d)
            phi = _l2norm(slots1) * scale
            logits1 = jnp.einsum('bGgd,esd->bGges', xg, phi)
            disp1 = jax.nn.softmax(logits1, axis=2)
            comb1 = jax.nn.softmax(logits1.reshape(b, G, g, E1 * S1), -1)
            slots = jnp.einsum('bGgd,bGges->bGesd', xg, disp1)
            yn = _l2norm(slots) * scale * gamma2[None, None, :, None, :]
            ns = S1 // E2
            m = S1 // ns
            means = yn.reshape(b, G, E1, m, ns, d).mean(axis=4)
            se2 = jnp.einsum('bGkmd,kdf->bGkmf', means, w_slot2)
            se2 = se2.reshape(b, G, E1, m, E2, d).transpose(0, 1, 2, 4, 3, 5)
            se2 = _l2norm(se2) * scale
            logits2 = jnp.einsum('bGksd,bGkemd->bGksem', yn, se2)
            disp2 = jax.nn.softmax(logits2, axis=3)
            comb2 = jax.nn.softmax(logits2.reshape(b, G, E1, S1, E2 * m), -1)
            slots2 = jnp.einsum('bGksd,bGksem->bGkemd', yn, disp2)
            u = jnp.einsum('bGkemd,kedh->bGkemh', slots2, w1) + b1[None, None, :, :, None, :]
            v, gate = jnp.split(u, 2, axis=-1)
            act = v * jax.nn.gelu(gate)
            o = jnp.einsum('bGkemh,kehd->bGkemd', act, w2) + b2[None, None, :, :, None, :]
            out2 = jnp.einsum('bGkpd,bGksp->bGksd', o.reshape(b, G, E1, E2 * m, d), comb2)
            out = jnp.einsum('bGPd,bGgP->bGgd', out2.reshape(b, G, E1 * S1, d), comb1)
            return out.reshape(b, n, d)
        return _forward(x, gamma_in, slots1, gamma2, w_slot2, w1, b1, w2, b2)
    x = x + _L0_gnn_ref(_layernorm(x, axis=-1), adj, L0_gnn_wq, L0_gnn_bq, L0_gnn_wk, L0_gnn_bk, L0_gnn_wv, L0_gnn_bv, L0_gnn_wo, L0_gnn_bo, L0_gnn_w1, L0_gnn_b1, L0_gnn_w2, L0_gnn_b2, L0_gnn_alpha1, L0_gnn_gamma1, L0_gnn_alpha2, L0_gnn_gamma2)
    x = x + _L0_ffn_ref(_layernorm(x, axis=-1), L0_ffn_gamma_in, L0_ffn_slots1, L0_ffn_gamma2, L0_ffn_w_slot2, L0_ffn_w1, L0_ffn_b1, L0_ffn_w2, L0_ffn_b2)
    return x

_drawn_inputs = setup_inputs


def setup_inputs(seed=0):
    import zlib

    import numpy as np

    out = dict(_drawn_inputs(seed))
    spreads = {'L0_gnn_bq': (0.0, 0.622),
     'L0_gnn_bk': (0.0, 0.8),
     'L0_gnn_bv': (0.0, 0.1),
     'L0_gnn_bo': (0.0, 0.1),
     'L0_gnn_b1': (0.0, 0.395),
     'L0_gnn_b2': (0.0, 0.272),
     'L0_gnn_alpha1': (1.0, 0.2),
     'L0_gnn_gamma1': (1.0, 0.2),
     'L0_gnn_alpha2': (1.0, 0.2),
     'L0_gnn_gamma2': (1.0, 0.2),
     'L0_ffn_gamma_in': (1.0, 0.2),
     'L0_ffn_gamma2': (1.0, 0.581),
     'L0_ffn_b1': (0.0, 0.8),
     'L0_ffn_b2': (0.0, 0.1)}
    factors = {}
    for name, (base, spread) in spreads.items():
        noise = np.random.default_rng([zlib.crc32(name.encode()), seed]).standard_normal(out[name].shape)
        drawn = base * np.exp(spread * noise) if base else spread * noise
        out[name] = jnp.asarray(drawn.astype(out[name].dtype))
    for name, factor in factors.items():
        out[name] = (out[name] * factor).astype(out[name].dtype)
    return out
```

```python
from contextlib import ExitStack

import concourse.bass as bass
from concourse import mybir

F32 = mybir.dt.float32
F32R = mybir.dt.float32r
BF16 = mybir.dt.bfloat16
ALU = mybir.AluOpType
ACT = mybir.ActivationFunctionType
X_AXIS = mybir.AxisListType.X

P = 128
D = 384
DC = D // P
NB = 64
H = 8
DH = D // H
HP = 64
FF = 1536
FC = FF // P
GT = 2
GN = GT * P
NG = NB // GT
PAIRS = FC // 2
E1, S1, E2, M2 = 8, 16, 4, 4
NS = S1 // E2
NX = E1 * E2
HID = 1024
XR = NB * M2
EPS_LN = 1e-5
EPS = 1e-6
SCALE = float(D) ** 0.5
MASKED = -1e30


class Signal:

    def __init__(self, sem, per_step):
        self.sem, self.n = sem, per_step

    def at(self, step, k):
        return step * self.n + k


def past(step, n):
    return not isinstance(step, int) or step >= n


def build(nc, x, adj, wq, bq, wk, bk, wv, bv, wo, bo, w1, b1, w2, b2, alpha1, gamma1, alpha2, gamma2,
          f_gamma_in, f_slots1, f_gamma2, f_w_slot2, f_w1, f_b1, f_w2, f_b2, out):
    names = [0]

    def dram(name, shape):
        return nc.dram_tensor(name, shape, F32, kind="Internal").ap()

    x_rows = x.rearrange("b n d -> (b n) d")
    res_dram = dram("residual", [NB * P, D])
    yn_dram = dram("yn", [NB, P, D])
    comb_dram = dram("comb1T", [NB, P, P])
    se_dram = dram("se2", [E1, NB * M2, E2 * D])
    ct_dram = dram("combT", [NB, P, P])
    o_dram = dram("expert_out", [NB * P, D])

    with ExitStack() as kernel_ctx:
        def sem(ctx, name, per_step=1):
            names[0] += 1
            return Signal(ctx.enter_context(nc.semaphore(f"{name}_{names[0]}")), per_step)

        def sb(ctx, name, shape, dt=F32):
            return ctx.enter_context(nc.sbuf_tensor(name, shape, dt))

        def ps(ctx, name, shape):
            return ctx.enter_context(nc.psum_tensor(name, shape, F32))

        ident = sb(kernel_ctx, "ident", [P, P])
        nhalf = sb(kernel_ctx, "nhalf", [P, 4])
        eps_ln = sb(kernel_ctx, "eps_ln", [P, 4])
        eps = sb(kernel_ctx, "eps", [P, 4])

        with ExitStack() as layer_ctx:
            setup_and_layer(nc, layer_ctx, sb, ps, sem, ident, nhalf, eps_ln, eps, x_rows, adj, wq, bq, wk, bk, wv, bv,
                            wo, bo, w1, b1, w2, b2, alpha1, gamma1, alpha2, gamma2, f_gamma_in, f_slots1,
                            f_gamma2, res_dram, yn_dram, comb_dram)
        with ExitStack() as ctx:
            routes(nc, ctx, sb, ps, sem, ident, nhalf, eps, f_w_slot2, yn_dram, se_dram)
        with ExitStack() as experts_ctx:
            slots2T = sb(experts_ctx, "slots2T", [P, DC, NB, P])
            with ExitStack() as ctx:
                dispatch(nc, ctx, sb, ps, sem, ident, yn_dram, se_dram, comb_dram, ct_dram, slots2T)
            with ExitStack() as ctx:
                experts(nc, ctx, sb, ps, sem, ident, slots2T, f_w1, f_b1, f_w2, f_b2, o_dram)
        with ExitStack() as ctx:
            combine(nc, ctx, sb, ps, sem, ct_dram, o_dram, res_dram, out)


def setup_and_layer(nc, ctx, sb, ps, sem, ident, nhalf, eps_ln, eps, x_rows, adj, wq, bq, wk, bk, wv, bv, wo, bo, w1, b1,
                    w2, b2, alpha1, gamma1, alpha2, gamma2, f_gamma_in, f_slots1, f_gamma2, res_dram,
                    yn_dram, comb_dram):
    def split_pair(name, shape):
        return [sb(ctx, name + "_hi", shape, F32R), sb(ctx, name + "_lo", shape, F32R)]

    wq_s = split_pair("wq", [P, DC, H * HP])
    wk_s = split_pair("wk", [P, DC, H * HP])
    wv_s = split_pair("wv", [P, DC, D])
    wo_s = split_pair("wo", [P, DC, D])
    w1_s = split_pair("w1", [P, DC, FF])
    w2_s = split_pair("w2", [P, FC, D])
    phiT = sb(ctx, "phiT", [P, DC, P])
    bqk = sb(ctx, "bqk", [P, 2, H // 2])
    b1c = sb(ctx, "b1c", [P, FC])
    rows = {n: sb(ctx, "row_" + n, [P, D]) for n in
            ("bv", "bo", "alpha1", "gamma1", "b2", "alpha2", "gamma2", "gin", "g2")}

    with ExitStack() as setup:
        stage = [sb(setup, f"stage{i}", [P, 12 * D]) for i in range(2)]
        phi = sb(setup, "phi", [P, D])
        phi_sq = sb(setup, "phi_sq", [P, D])
        phi_ss = sb(setup, "phi_ss", [P, 4])
        tp = ps(setup, "tp", [P, DC, P])
        staged = [sem(setup, "staged0"), sem(setup, "staged1")]
        zeroed = sem(setup, "zeroed")
        hi_done = sem(setup, "hi_done")
        lo_done = sem(setup, "lo_done")
        small = sem(setup, "small")
        pool_done = sem(setup, "pool_done")
        phi_done = sem(setup, "phi_done")
        phi_T = sem(setup, "phi_T")

        def padded(t):
            return t[:, 0:DC * H * HP].rearrange("p (c h e) -> p c h e", c=DC, h=H)

        weights = []
        for i, (w, parts) in enumerate(((wq, wq_s), (wk, wk_s), (wv, wv_s), (wo, wo_s), (w1, w1_s), (w2, w2_s))):
            s = stage[i % 2]
            if i < 2:
                srcs = [(padded(s)[:, c, :, 0:DH], w[c * P:(c + 1) * P, :].rearrange("p (h e) -> p h e", h=H))
                        for c in range(DC)]
                flat = s[:, 0:DC * H * HP]
            else:
                n = w.shape[0] // P * w.shape[1]
                srcs = [(s[:, 0:n].rearrange("p (c f) -> p c f", c=w.shape[0] // P),
                         w.rearrange("(c p) f -> p c f", p=P))]
                flat = s[:, 0:n]
            weights.append((srcs, flat, [t[:].rearrange("p c f -> p (c f)") for t in parts]))

        landed = [0, 0]
        after = []
        for i, (srcs, _, _) in enumerate(weights):
            landed[i % 2] += 16 * len(srcs)
            after.append(landed[i % 2])
        n_small = [0]

        with nc.Block() as block:
            @block.sync
            def _(sp):
                for i, (srcs, _, _) in enumerate(weights):
                    if i < 2:
                        sp.wait_ge(zeroed.sem, i + 1)
                    else:
                        sp.wait_ge(lo_done.sem, i - 1)
                    for dst, src in srcs:
                        sp.dma_start(dst, src).then_inc(staged[i % 2].sem, 16)

            @block.scalar
            def _(act):
                def small_load(dst, src):
                    act.dma_start(dst, src).then_inc(small.sem, 16)
                    n_small[0] += 16

                small_load(phi[:], f_slots1.rearrange("k s d -> (k s) d"))
                for name, src in (("bv", bv), ("bo", bo), ("alpha1", alpha1), ("gamma1", gamma1), ("b2", b2),
                                  ("alpha2", alpha2), ("gamma2", gamma2), ("gin", f_gamma_in)):
                    small_load(rows[name][:], src.partition_broadcast(P))
                small_load(rows["g2"][:], f_gamma2.rearrange("k (o d) -> k o d", o=1).broadcast_to([E1, S1, D]))
                act.wait_ge(zeroed.sem, 3)
                for n, b in enumerate((bq, bk)):
                    for half in range(2):
                        src = b.rearrange("(m two e) -> two e m", two=2, e=DH)[half]
                        for m in range(H // 2):
                            small_load(bqk[HP * half:HP * half + DH, n, m:m + 1], src[:, m:m + 1])
                for m in range(FC):
                    small_load(b1c[:, m:m + 1], b1[m * P:(m + 1) * P].rearrange("(p o) -> p o", o=1))
                for i, (_, flat, parts) in enumerate(weights):
                    act.wait_ge(staged[i % 2].sem, after[i])
                    nc.scalar.copy(parts[0], flat).then_inc(hi_done.sem, 1)
                act.wait_ge(small.sem, n_small[0])
                nc.scalar.activation(phi_sq[:], phi[:], ACT.Square, accum_out=phi_ss[:, 0:1]).then_inc(phi_done.sem, 1)
                act.wait_ge(phi_T.sem, 1)
                nc.scalar.copy(phiT[:], tp[:]).then_inc(phi_done.sem, 1)

            @block.gpsimd
            def _(pool):
                nc.gpsimd.memset(ident[:], 0.0).then_inc(pool_done.sem, 1)
                nc.gpsimd.memset(eps_ln[:], EPS_LN)
                nc.gpsimd.memset(eps[:], EPS)
                nc.gpsimd.memset(nhalf[:], -0.5).then_inc(pool_done.sem, 1)
                pool.wait_ge(pool_done.sem, 2)
                nc.gpsimd.affine_select(out=ident[:], in_=ident[:], compare_op=ALU.not_equal, fill=1.0, base=0,
                                        pattern=[[-1, P]], channel_multiplier=1).then_inc(pool_done.sem, 1)
                pool.wait_ge(phi_done.sem, 1)
                nc.gpsimd.tensor_scalar(phi_ss[:, 1:2], phi_ss[:, 0:1], EPS, 1.0, ALU.add, ALU.mult).then_inc(pool_done.sem, 1)
                pool.wait_ge(pool_done.sem, 4)
                nc.gpsimd.tensor_tensor(phi_ss[:, 2:3], phi_ss[:, 1:2], nhalf[:, 0:1], ALU.pow).then_inc(pool_done.sem, 1)

            @block.vector
            def _(dve):
                for s in stage:
                    nc.vector.memset(s[:, 0:DC * H * HP], 0.0).then_inc(zeroed.sem, 1)
                nc.vector.memset(bqk[:], 0.0).then_inc(zeroed.sem, 1)
                for i, (_, flat, parts) in enumerate(weights):
                    dve.wait_ge(hi_done.sem, i + 1)
                    nc.vector.tensor_tensor(parts[1], flat, parts[0].bitcast(F32), ALU.subtract).then_inc(lo_done.sem, 1)
                dve.wait_ge(small.sem, n_small[0])
                nc.vector.tensor_scalar(rows["gin"][:], rows["gin"][:], SCALE, None, ALU.mult)
                nc.vector.tensor_scalar(rows["g2"][:], rows["g2"][:], SCALE, None, ALU.mult)
                nc.vector.tensor_scalar(bqk[:, 0, :], bqk[:, 0, :], DH ** -0.5, None, ALU.mult)
                dve.wait_ge(pool_done.sem, 5)
                nc.vector.tensor_scalar(phi[:], phi[:], phi_ss[:, 2:3], SCALE, ALU.mult, ALU.mult).then_inc(lo_done.sem, 1)

            @block.tensor
            def _(pe):
                pe.wait_ge(pool_done.sem, 5)
                pe.wait_ge(lo_done.sem, len(weights) + 1)
                for c in range(DC):
                    mm = pe.transpose(tp[:, c, :], phi[:, c * P:(c + 1) * P], ident[:])
                mm.then_inc(phi_T.sem, 1)

    t_sb = lambda name, shape, dt=F32: sb(ctx, name, shape, dt)
    x_in = t_sb("x_in", [P, GT, D])
    adj_sb = t_sb("adj_sb", [P, GT, P])
    z = t_sb("z", [P, GT, D])
    zT = [t_sb("zT_hi", [P, DC, GN], F32R), t_sb("zT_lo", [P, DC, GN], F32R)]
    qT = t_sb("qT", [P, H // 2, GN])
    kT = t_sb("kT", [P, H // 2, GN])
    v_sb = t_sb("v_sb", [P, GT, D])
    s_sb = [t_sb(f"s_sb{t}", [P, 2, H // 2, P]) for t in range(GT)]
    pT = t_sb("pT", [P, 2, H // 2, P])
    ctx_sb = t_sb("ctx_sb", [P, D])
    cT = [t_sb("cT_hi", [P, DC, P], F32R), t_sb("cT_lo", [P, DC, P], F32R)]
    y = t_sb("y", [P, GT, D])
    yT = [t_sb("yT_hi", [P, DC, GN], F32R), t_sb("yT_lo", [P, DC, GN], F32R)]
    yb = t_sb("yb", [P, GT, D])
    h_tmp = [t_sb(f"h_tmp{i}", [P, 2, GN]) for i in range(2)]
    hT = [[t_sb(f"hT_hi{i}", [P, 2, GN], F32R), t_sb(f"hT_lo{i}", [P, 2, GN], F32R)] for i in range(3)]
    f_sb = t_sb("f_sb", [P, GT, D])
    x_res = t_sb("x_res", [P, GT, D])
    xn = t_sb("xn", [P, GT, D])
    xnT = t_sb("xnT", [P, DC, GN])
    logit = t_sb("logit", [P, GT, P])
    comb = t_sb("comb", [P, GT, P])
    disp = t_sb("disp", [P, GT, P])
    dcT = t_sb("dcT", [P, 2, GT, P])
    yn = t_sb("yn_sb", [P, GT, D])
    squares = {n: t_sb("squares_" + n, [P, GT, D], BF16) for n in ("r", "f")}
    counts = t_sb("counts", [P, GT])
    st = t_sb("st", [P, GT, 6])
    mv = t_sb("mv", [P, GT, 2])
    rstd = t_sb("rstd", [P, 2, GT])
    nmax = t_sb("nmax", [P, GT, H])
    ssum = t_sb("ssum", [P, GT, H])
    rsum = t_sb("rsum", [P, GT, H])
    rms = t_sb("rms", [P, GT, 3])
    fms = t_sb("fms", [P, GT, 3])
    st2 = t_sb("st2", [P, GT, 6])
    mv2 = t_sb("mv2", [P, GT, 2])
    rstd2 = t_sb("rstd2", [P, 2, GT])
    zms = t_sb("zms", [P, GT, 3])
    lmx = t_sb("lmx", [P, 2, GT])
    lsum = t_sb("lsum", [P, 2, GT])
    lrec = t_sb("lrec", [P, 2, GT])
    sms = t_sb("sms", [P, GT, 3])

    a_bank = [ps(ctx, f"a_bank{i}", [P, 512]) for i in range(3)]
    m_bank = [ps(ctx, f"m_bank{i}", [P, 2, GN]) for i in range(2)]
    f_bank = [ps(ctx, f"f_bank{i}", [P, 512]) for i in range(GT)]
    r_bank = ps(ctx, "r_bank", [P, 512])

    S = lambda name, n: sem(ctx, name, n)
    x_landed, adj_landed = S("x_landed", 16), S("adj_landed", 16)
    stats, meanvar, ve, rstd_ok, z_ok = S("stats", 2), S("meanvar", 2), S("ve", 1), S("rstd_ok", 1), S("z_ok", 2)
    zh, zl = S("zT_hi", 2), S("zT_lo", 2)
    q_ok, k_ok, v_ok = S("q", 4), S("k", 4), S("v", 2)
    sc_ok, mx_ok, p_ok, rs_ok = S("scores", 4), S("row_max", 2), S("exp", 16), S("recip", 2)
    pt_ok, ctx_ok, ch, cl = S("pT", 4), S("ctx", 2), S("cT_hi", 2), S("cT_lo", 2)
    r_ok, rb_ok, rss, rve, rrs = S("r", 2), S("r_bias", 2), S("r_ss", 2), S("r_ve", 2), S("r_rs", 2)
    ys, y_ok, yh, yl = S("y_scaled", 2), S("y", 2), S("yT_hi", 2), S("yT_lo", 2)
    a_full = S("a_bank_full", 24)
    res_landed = S("x_res_landed", 16)
    yb_ok, h_ok, hh, hl = S("yb", 2), S("h", 12), S("hT_hi", 6), S("hT_lo", 6)
    f_ok, fss, fve, frs = S("f", 2), S("f_ss", 2), S("f_ve", 2), S("f_rs", 2)
    fs, xg, xo = S("f_scaled", 2), S("x_plus_gamma", 2), S("layer_out", 2)
    m_full, f_full, h_used = S("m_bank_full", 6), S("f_bank_full", 2), S("h_used", PAIRS - 1)
    res_stored = S("res_stored", 16)
    st2_ok, mv2_ok, ve2, rstd2_ok, z2_ok = S("stats2", 2), S("meanvar2", 2), S("ve2", 1), S("rstd2_ok", 1), S("z2", 2)
    zss, zve, zrs, xn_ok = S("z_ss", 2), S("z_ve", 1), S("z_rs", 1), S("xn", 2)
    xt_ok, lg_ok, lm_ok, le_ok, lr_ok, cb_ok = S("xnT", 2), S("logit", 1), S("l_max", 1), S("l_exp", 2), S("l_recip", 1), S("comb", 2)
    dm_ok, de_ok, dr_ok, tt_ok = S("d_max", 1), S("d_exp", 2), S("d_recip", 1), S("dcT", 1)
    sl_ok, sss, sve, srs, yn_ok = S("slots", 2), S("s_ss", 2), S("s_ve", 2), S("s_rs", 2), S("yn", 2)
    r_full = S("r_bank_full", 7)
    yn_stored, comb_stored = S("yn_stored", 16), S("comb_stored", 16)

    U_ZT, U_Q, U_K, U_V, U_S = (0, 1), (2, 3), (4, 5), (6, 7), ((8, 9), (10, 11))
    U_PT, U_CTX, U_CT, U_WO, U_YT = ((12, 13), (15, 16)), (14, 18), (17, 20), (19, 22), (21, 23)
    def tok(t):
        return slice(t * P, (t + 1) * P)

    with nc.Block() as block:
        @block.sync
        def _(sp):
            def body(a, m, r):
                if a is not None:
                    if past(a, 1):
                        sp.wait_ge(z_ok.sem, z_ok.at(a - 1, 2))
                    sp.dma_start(x_in[:], x_rows[bass.ds(a * GN, GN), :].rearrange("(t p) d -> p t d", p=P)
                                 ).then_inc(x_landed.sem, 16)
                    if past(a, 1):
                        sp.wait_ge(sc_ok.sem, sc_ok.at(a - 1, 4))
                    sp.dma_start(adj_sb[:], adj[bass.ds(a * GT, GT)].rearrange("t q k -> q t k")
                                 ).then_inc(adj_landed.sem, 16)
                if m is not None:
                    if past(m, 1):
                        sp.wait_ge(xo.sem, xo.at(m - 1, 2))
                    sp.dma_start(x_res[:], x_rows[bass.ds(m * GN, GN), :].rearrange("(t p) d -> p t d", p=P)
                                 ).then_inc(res_landed.sem, 16)
                if r is not None:
                    sp.wait_ge(tt_ok.sem, tt_ok.at(r, 1))
                    sp.dma_start(comb_dram[bass.ds(r * GT, GT)].rearrange("t p n -> p t n"), dcT[:, 1, :, :]
                                 ).then_inc(comb_stored.sem, 16)
                    sp.wait_ge(yn_ok.sem, yn_ok.at(r, 2))
                    sp.dma_start(yn_dram[bass.ds(r * GT, GT)].rearrange("t p d -> p t d"), yn[:]
                                 ).then_inc(yn_stored.sem, 16)
                if m is not None:
                    sp.wait_ge(xo.sem, xo.at(m, 2))
                    sp.dma_start(res_dram[bass.ds(m * GN, GN), :].rearrange("(t p) d -> p t d", p=P), f_sb[:]
                                 ).then_inc(res_stored.sem, 16)

            run(sp, body)
            sp.wait_ge(res_stored.sem, 16 * NG)
            sp.wait_ge(yn_stored.sem, 16 * NG)
            sp.wait_ge(comb_stored.sem, 16 * NG)

        @block.tensor
        def _(pe):
            def split_mm(dst, lhs, rhs, start=True, stop=True):
                n = len(lhs)
                for c in range(n):
                    (lh, ll), (rh, rl) = lhs[c], rhs[c]
                    for j, (left, right) in enumerate(((lh, rh), (lh, rl), (ll, rh))):
                        mm = pe.matmul(dst, left, right, start=start and c == 0 and j == 0,
                                       stop=stop and c == n - 1 and j == 2)
                return mm

            def zT_step(g, t):
                pe.wait_ge(z_ok.sem, z_ok.at(g, t + 1))
                if t == 0:
                    if past(g, 1):
                        pe.wait_ge(yl.sem, yl.at(g - 1, 1))
                else:
                    if past(g, 1):
                        pe.wait_ge(r_ok.sem, r_ok.at(g - 1, 2))
                bank = a_bank[U_ZT[t] % 3]
                for c in range(DC):
                    mm = pe.transpose(bank[:, tok(c)], z[:, t, tok(c)], ident[:])
                mm.then_inc(a_full.sem, 1)

            def project(g, uses, w, n):
                if w is wq_s and n == 0:
                    pe.wait_ge(zl.sem, zl.at(g, 2))
                    if past(g, 1):
                        pe.wait_ge(yl.sem, yl.at(g - 1, 2))
                if w is wk_s and n == 1:
                    pe.wait_ge(q_ok.sem, q_ok.at(g, 2))
                bank = a_bank[uses[n] % 3]
                for half in range(2):
                    m = 2 * n + half
                    mm = split_mm(bank[:, half * GN:(half + 1) * GN],
                                  [[w[s][:, c, tok(m)] for s in range(2)] for c in range(DC)],
                                  [[zT[s][:, c, :] for s in range(2)] for c in range(DC)])
                mm.then_inc(a_full.sem, 1)

            def values(g, t):
                if t == 0:
                    pe.wait_ge(q_ok.sem, q_ok.at(g, 4))
                else:
                    pe.wait_ge(k_ok.sem, k_ok.at(g, 2))
                bank = a_bank[U_V[t] % 3]
                split_mm(bank[:, 0:D], [[zT[s][:, c, tok(t)] for s in range(2)] for c in range(DC)],
                         [[wv_s[s][:, c, :] for s in range(2)] for c in range(DC)]).then_inc(a_full.sem, 1)

            def scores(g, t):
                pe.wait_ge(q_ok.sem, q_ok.at(g, 4))
                pe.wait_ge(k_ok.sem, k_ok.at(g, 4))
                for par in range(2):
                    held, k = ((k_ok, 4), (v_ok, 1), (v_ok, 2), (sc_ok, 1))[2 * t + par]
                    pe.wait_ge(held.sem, held.at(g, k))
                    bank = a_bank[U_S[t][par] % 3]
                    r = slice(HP * par, HP * par + DH)
                    for m in range(H // 2):
                        mm = pe.matmul(bank[:, tok(m)], qT[r, m, tok(t)], kT[r, m, tok(t)], start=True, stop=True)
                    mm.then_inc(a_full.sem, 1)

            def prob_T(g, t):
                for par in range(2):
                    pe.wait_ge(p_ok.sem, p_ok.at(g, 8 * t + 4 * (par + 1)))
                    held, k = ((sc_ok, 2), (sc_ok, 3), (pt_ok, 1), (pt_ok, 2))[2 * t + par]
                    pe.wait_ge(held.sem, held.at(g, k))
                    bank = a_bank[U_PT[t][par] % 3]
                    for m in range(H // 2):
                        mm = pe.transpose(bank[:, tok(m)], s_sb[t][:, par, m, :], ident[:])
                    mm.then_inc(a_full.sem, 1)

            def context(g, t):
                pe.wait_ge(v_ok.sem, v_ok.at(g, t + 1))
                held, k = ((sc_ok, 4), (pt_ok, 3))[t]
                pe.wait_ge(held.sem, held.at(g, k))
                bank = a_bank[U_CTX[t] % 3]
                for par in range(2):
                    pe.wait_ge(pt_ok.sem, pt_ok.at(g, 2 * t + par + 1))
                    for m in range(H // 2):
                        h = 2 * m + par
                        mm = pe.matmul(bank[:, h * DH:(h + 1) * DH], pT[:, par, m, :],
                                       v_sb[:, t, h * DH:(h + 1) * DH], start=True, stop=True)
                mm.then_inc(a_full.sem, 1)

            def context_T(g, t):
                pe.wait_ge(ctx_ok.sem, ctx_ok.at(g, t + 1))
                if t:
                    pe.wait_ge(cl.sem, cl.at(g, 1))
                bank = a_bank[U_CT[t] % 3]
                for c in range(DC):
                    mm = pe.transpose(bank[:, tok(c)], ctx_sb[:, tok(c)], ident[:])
                mm.then_inc(a_full.sem, 1)

            def project_out(g, t):
                pe.wait_ge(cl.sem, cl.at(g, t + 1))
                held, k = ((pt_ok, 4), (r_ok, 1))[t]
                pe.wait_ge(held.sem, held.at(g, k))
                bank = a_bank[U_WO[t] % 3]
                split_mm(bank[:, 0:D], [[cT[s][:, c, :] for s in range(2)] for c in range(DC)],
                         [[wo_s[s][:, c, :] for s in range(2)] for c in range(DC)]).then_inc(a_full.sem, 1)

            def yT_step(g, t):
                pe.wait_ge(y_ok.sem, y_ok.at(g, t + 1))
                held, k = ((ctx_ok, 2), (cl, 2))[t]
                pe.wait_ge(held.sem, held.at(g, k))
                bank = a_bank[U_YT[t] % 3]
                for c in range(DC):
                    mm = pe.transpose(bank[:, tok(c)], y[:, t, tok(c)], ident[:])
                mm.then_inc(a_full.sem, 1)

            def up(g, i):
                pe.wait_ge(yl.sem, yl.at(g, 2))
                if i >= 2:
                    pe.wait_ge(h_ok.sem, h_ok.at(g, 2 * (i - 1)))
                else:
                    if past(g, 1):
                        pe.wait_ge(h_ok.sem, h_ok.at(g - 1, 12 - 2 * (1 - i)))
                for half in range(2):
                    m = 2 * i + half
                    mm = split_mm(m_bank[i % 2][:, half, :],
                                  [[w1_s[s][:, c, tok(m)] for s in range(2)] for c in range(DC)],
                                  [[yT[s][:, c, :] for s in range(2)] for c in range(DC)])
                mm.then_inc(m_full.sem, 1)

            def down(g, i):
                pe.wait_ge(hh.sem, hh.at(g, i + 1))
                pe.wait_ge(hl.sem, hl.at(g, i + 1))
                for t in range(GT):
                    if i == 0:
                        if past(g, 1):
                            pe.wait_ge(f_ok.sem, f_ok.at(g - 1, t + 1))
                    mm = split_mm(f_bank[t][:, 0:D],
                                  [[hT[i % 3][s][:, half, tok(t)] for s in range(2)] for half in range(2)],
                                  [[w2_s[s][:, 2 * i + half, :] for s in range(2)] for half in range(2)],
                                  start=i == 0, stop=i == PAIRS - 1)
                    if i == PAIRS - 1:
                        mm.then_inc(f_full.sem, 1)
                if i < PAIRS - 1:
                    mm.then_inc(h_used.sem, 1)

            def xnT_step(g, t):
                pe.wait_ge(xn_ok.sem, xn_ok.at(g, t + 1))
                if t == 0:
                    if past(g, 1):
                        pe.wait_ge(sl_ok.sem, sl_ok.at(g - 1, 2))
                else:
                    pe.wait_ge(xt_ok.sem, xt_ok.at(g, 1))
                for c in range(DC):
                    mm = pe.transpose(r_bank[:, tok(c)], xn[:, t, tok(c)], ident[:])
                mm.then_inc(r_full.sem, 1)

            def logits(g):
                pe.wait_ge(xt_ok.sem, xt_ok.at(g, 2))
                for t in range(GT):
                    for c in range(DC):
                        mm = pe.matmul(r_bank[:, tok(t)], xnT[:, c, tok(t)], phiT[:, c, :], start=c == 0, stop=c == DC - 1)
                mm.then_inc(r_full.sem, 1)

            def logits_T(g):
                pe.wait_ge(lg_ok.sem, lg_ok.at(g, 1))
                for t in range(GT):
                    mm = pe.transpose(r_bank[:, tok(t)], logit[:, t, :], ident[:])
                mm.then_inc(r_full.sem, 1)

            def weights_T(g):
                pe.wait_ge(de_ok.sem, de_ok.at(g, 2))
                pe.wait_ge(cb_ok.sem, cb_ok.at(g, 2))
                for n, w in enumerate((disp, comb)):
                    for t in range(GT):
                        mm = pe.transpose(r_bank[:, tok(2 * n + t)], w[:, t, :], ident[:])
                mm.then_inc(r_full.sem, 1)

            def slots(g, t):
                if t == 0:
                    pe.wait_ge(tt_ok.sem, tt_ok.at(g, 1))
                else:
                    pe.wait_ge(sl_ok.sem, sl_ok.at(g, 1))
                pe.matmul(r_bank[:, 0:D], dcT[:, 0, t, :], xn[:, t, :], start=True, stop=True).then_inc(r_full.sem, 1)

            def body(a, m, r):
                A, M, R = a is not None, m is not None, r is not None
                if M: up(m, 0); up(m, 1)
                if A: zT_step(a, 0); zT_step(a, 1)
                if R: xnT_step(r, 0); xnT_step(r, 1)
                if M: up(m, 2); down(m, 0)
                if A: project(a, U_Q, wq_s, 0); project(a, U_Q, wq_s, 1)
                if R: logits(r)
                if A: project(a, U_K, wk_s, 0); project(a, U_K, wk_s, 1)
                if R: logits_T(r)
                if A: values(a, 0); values(a, 1); scores(a, 0); scores(a, 1)
                if M: down(m, 1)
                if R: weights_T(r)
                if M: down(m, 2)
                if A: prob_T(a, 0)
                if M: up(m, 3)
                if A: context(a, 0); prob_T(a, 1)
                if R: slots(r, 0)
                if M: up(m, 4)
                if A: context_T(a, 0); context(a, 1)
                if R: slots(r, 1)
                if M: down(m, 3)
                if A: project_out(a, 0); context_T(a, 1)
                if M: up(m, 5)
                if A: yT_step(a, 0); project_out(a, 1)
                if M: down(m, 4)
                if M: down(m, 5)
                if A: yT_step(a, 1)

            run(pe, body)

        @block.scalar
        def _(act):
            def hi_T(g, t, use, dst, sig):
                act.wait_ge(a_full.sem, a_full.at(g, use[t] + 1))
                nc.scalar.copy(dst, a_bank[use[t] % 3][:, 0:D].rearrange("p (c n) -> p c n", c=DC)).then_inc(sig.sem, 1)

            def query(g):
                for m in range(H // 2):
                    if m % 2 == 0:
                        act.wait_ge(a_full.sem, a_full.at(g, U_Q[m // 2] + 1))
                    bank = a_bank[U_Q[m // 2] % 3]
                    nc.scalar.activation(qT[:, m, :], bank[:, (m % 2) * GN:(m % 2 + 1) * GN], ACT.Identity,
                                         bias=bqk[:, 0, m:m + 1], scale=DH ** -0.5).then_inc(q_ok.sem, 1)

            def exps(g, t):
                act.wait_ge(mx_ok.sem, mx_ok.at(g, t + 1))
                for par in range(2):
                    for m in range(H // 2):
                        h = par * (H // 2) + m
                        s = s_sb[t][:, par, m, :]
                        nc.scalar.activation(s, s, ACT.Exp, bias=nmax[:, t, h:h + 1],
                                             accum_out=ssum[:, t, h:h + 1]).then_inc(p_ok.sem, 1)

            def prob_T(g, t):
                act.wait_ge(a_full.sem, a_full.at(g, U_PT[t][0] + 1))
                if t:
                    act.wait_ge(ctx_ok.sem, ctx_ok.at(g, t))
                else:
                    if past(g, 1):
                        act.wait_ge(ctx_ok.sem, ctx_ok.at(g - 1, 2))
                for par in range(2):
                    act.wait_ge(a_full.sem, a_full.at(g, U_PT[t][par] + 1))
                    nc.scalar.copy(pT[:, par, :, :], a_bank[U_PT[t][par] % 3][:].rearrange("p (m n) -> p m n", n=P)
                                   ).then_inc(pt_ok.sem, 1)

            def square(g, t, name, sig_in, src, dst, sig, scale=1.0):
                act.wait_ge(sig_in.sem, sig_in.at(g, t + 1))
                out, rows_in = squares[name][:, t, :] if name in squares else None, src[:, t, :]
                if name == "z":
                    out, rows_in = xnT[:, :, tok(t)], rows_in.rearrange("p (c n) -> p c n", c=DC)
                if name == "s":
                    out = (comb, disp)[t][:].rearrange("p t n -> p (t n)").bitcast(BF16)[:, 0:D]
                nc.scalar.activation(out, rows_in, ACT.Square, scale=scale, accum_out=dst[:, t, 0:1]).then_inc(sig.sem, 1)

            def silu(g, i):
                act.wait_ge(m_full.sem, m_full.at(g, i + 1))
                if i >= 2:
                    act.wait_ge(hl.sem, hl.at(g, i - 1))
                else:
                    if past(g, 1):
                        act.wait_ge(hl.sem, hl.at(g - 1, PAIRS - 1 + i))
                for half in range(2):
                    nc.scalar.activation(h_tmp[i % 2][:, half, :], m_bank[i % 2][:, half, :], ACT.Silu,
                                         bias=b1c[:, 2 * i + half:2 * i + half + 1]).then_inc(h_ok.sem, 1)

            def xnT_step(g, t):
                act.wait_ge(r_full.sem, r_full.at(g, t + 1))
                nc.scalar.copy(xnT[:, :, tok(t)], r_bank[:, 0:D].rearrange("p (c n) -> p c n", c=DC)).then_inc(xt_ok.sem, 1)

            def logits(g):
                act.wait_ge(r_full.sem, r_full.at(g, 3))
                nc.scalar.copy(logit[:], r_bank[:, 0:GN].rearrange("p (t n) -> p t n", t=GT)).then_inc(lg_ok.sem, 1)

            def comb_exp(g):
                act.wait_ge(lm_ok.sem, lm_ok.at(g, 1))
                for t in range(GT):
                    nc.scalar.activation(comb[:, t, :], logit[:, t, :], ACT.Exp, bias=lmx[:, 0, t:t + 1],
                                         accum_out=lsum[:, 0, t:t + 1]).then_inc(le_ok.sem, 1)

            def disp_exp(g):
                act.wait_ge(dm_ok.sem, dm_ok.at(g, 1))
                for t in range(GT):
                    nc.scalar.activation(disp[:, t, :], r_bank[:, tok(t)], ACT.Exp, bias=lmx[:, 1, t:t + 1],
                                         accum_out=lsum[:, 1, t:t + 1]).then_inc(de_ok.sem, 1)

            def weights_T(g):
                act.wait_ge(r_full.sem, r_full.at(g, 5))
                if past(g, 1):
                    act.wait_ge(comb_stored.sem, comb_stored.at(g - 1, 16))
                nc.scalar.copy(dcT[:].rearrange("p n t k -> p (n t k)"), r_bank[:]).then_inc(tt_ok.sem, 1)

            def body(a, m, r):
                A, M, R = a is not None, m is not None, r is not None
                if R:
                    for t in range(GT): square(r, t, "z", z2_ok, xn, zms, zss)
                if M: silu(m, 0); silu(m, 1)
                if A:
                    for t in range(GT): hi_T(a, t, U_ZT, zT[0][:, :, tok(t)], zh)
                if R: xnT_step(r, 0); xnT_step(r, 1)
                if M: silu(m, 2)
                if A: query(a)
                if R: logits(r); comb_exp(r); disp_exp(r)
                if A: exps(a, 0)
                if R: weights_T(r)
                if A: exps(a, 1); prob_T(a, 0)
                if M: silu(m, 3)
                if A: prob_T(a, 1)
                if R: square(r, 0, "s", sl_ok, yn, sms, sss)
                if M: silu(m, 4)
                if A: hi_T(a, 0, U_CT, cT[0][:], ch)
                if R: square(r, 1, "s", sl_ok, yn, sms, sss)
                if A:
                    square(a, 0, "r", rb_ok, y, rms, rss, D ** -0.5)
                    hi_T(a, 1, U_CT, cT[0][:], ch)
                if M: silu(m, 5)
                if A:
                    hi_T(a, 0, U_YT, yT[0][:, :, tok(0)], yh)
                    square(a, 1, "r", rb_ok, y, rms, rss, D ** -0.5)
                if M:
                    for t in range(GT): square(m, t, "f", f_ok, f_sb, fms, fss, D ** -0.5)
                if A: hi_T(a, 1, U_YT, yT[0][:, :, tok(1)], yh)

            run(act, body)

        @block.vector
        def _(dve):
            def norm_stats(g, landed, k, src, s, v, sig_s, sig_v):
                for t in range(GT):
                    if t == 0 or k < 16:
                        dve.wait_ge(landed.sem, landed.at(g, k + t if k < 16 else k))
                    nc.vector.bn_stats(s[:, t, :], src[:, t, :]).then_inc(sig_s.sem, 1)
                dve.wait_ge(sig_s.sem, sig_s.at(g, GT))
                nc.vector.tensor_copy(counts[:], s[:, :, 0])
                for t in range(GT):
                    nc.vector.bn_aggr(v[:, t, :], s[:, t, :]).then_inc(sig_v.sem, 1)

            def centre(g, src, dst, v, r, sig_r, sig):
                dve.wait_ge(sig_r.sem, sig_r.at(g, 1))
                for t in range(GT):
                    nc.vector.tensor_scalar(dst[:, t, :], src[:, t, :], v[:, t, 0:1], r[:, 1, t:t + 1],
                                            ALU.subtract, ALU.mult).then_inc(sig.sem, 1)

            def z_step(g):
                if past(g, 1):
                    dve.wait_ge(r_ok.sem, r_ok.at(g - 1, 2))
                dve.wait_ge(x_landed.sem, x_landed.at(g, 16))
                centre(g, x_in, z, mv, rstd, rstd_ok, z_ok)

            def lo_T(g, t, use, hi, lo, sig_hi, sig):
                dve.wait_ge(sig_hi.sem, sig_hi.at(g, t + 1))
                nc.vector.tensor_tensor(lo, a_bank[use[t] % 3][:, 0:D].rearrange("p (c n) -> p c n", c=DC),
                                        hi.bitcast(F32), ALU.subtract).then_inc(sig.sem, 1)

            def key(g):
                for m in range(H // 2):
                    if m % 2 == 0:
                        dve.wait_ge(a_full.sem, a_full.at(g, U_K[m // 2] + 1))
                    bank = a_bank[U_K[m // 2] % 3]
                    nc.vector.tensor_scalar(kT[:, m, :], bank[:, (m % 2) * GN:(m % 2 + 1) * GN],
                                            bqk[:, 1, m:m + 1], None, ALU.add).then_inc(k_ok.sem, 1)

            def values(g, t):
                dve.wait_ge(a_full.sem, a_full.at(g, U_V[t] + 1))
                nc.vector.tensor_tensor(v_sb[:, t, :], a_bank[U_V[t] % 3][:, 0:D], rows["bv"][:], ALU.add).then_inc(v_ok.sem, 1)

            def scores(g, t):
                if t == 0:
                    dve.wait_ge(adj_landed.sem, adj_landed.at(g, 16))
                for par in range(2):
                    dve.wait_ge(a_full.sem, a_full.at(g, U_S[t][par] + 1))
                    nc.vector.tensor_tensor(s_sb[t][:, par, :, :], a_bank[U_S[t][par] % 3][:].rearrange("p (m n) -> p m n", n=P),
                                            adj_sb[:, t, :].unsqueeze(1).broadcast_to([P, H // 2, P]), ALU.add).then_inc(sc_ok.sem, 1)
                dve.wait_ge(sc_ok.sem, sc_ok.at(g, 2 * t + 2))
                nc.vector.tensor_reduce(nmax[:, t, :], s_sb[t][:].rearrange("p a m n -> p (a m) n"), X_AXIS, ALU.max,
                                        negate=True).then_inc(mx_ok.sem, 1)

            def recips(g, t):
                dve.wait_ge(p_ok.sem, p_ok.at(g, 8 * (t + 1)))
                nc.vector.reciprocal(rsum[:, t, :], ssum[:, t, :]).then_inc(rs_ok.sem, 1)

            def context(g, t):
                dve.wait_ge(a_full.sem, a_full.at(g, U_CTX[t] + 1))
                dve.wait_ge(rs_ok.sem, rs_ok.at(g, t + 1))
                if t:
                    dve.wait_ge(a_full.sem, a_full.at(g, U_CT[0] + 1))
                else:
                    if past(g, 1):
                        dve.wait_ge(a_full.sem, a_full.at(g - 1, U_CT[1] + 1))
                nc.vector.tensor_tensor(
                    ctx_sb[:].rearrange("p (m a e) -> p m a e", a=2, e=DH),
                    a_bank[U_CTX[t] % 3][:, 0:D].rearrange("p (m a e) -> p m a e", a=2, e=DH),
                    rsum[:, t, :].rearrange("p (a m) -> p m a", a=2).unsqueeze(3).broadcast_to([P, H // 2, 2, DH]),
                    ALU.mult).then_inc(ctx_ok.sem, 1)

            def residual(g, t):
                dve.wait_ge(a_full.sem, a_full.at(g, U_WO[t] + 1))
                if past(g, 1):
                    dve.wait_ge(yb_ok.sem, yb_ok.at(g - 1, t + 1))
                nc.vector.tensor_tensor(y[:, t, :], a_bank[U_WO[t] % 3][:, 0:D], z[:, t, :], ALU.add).then_inc(r_ok.sem, 1)

            def y_scale(g, t):
                dve.wait_ge(rrs.sem, rrs.at(g, t + 1))
                dve.wait_ge(rb_ok.sem, rb_ok.at(g, t + 1))
                nc.vector.scalar_tensor_tensor(out=y[:, t, :], in0=y[:, t, :], scalar=rms[:, t, 2:3],
                                               in1=rows["alpha1"][:], op0=ALU.mult, op1=ALU.mult).then_inc(ys.sem, 1)

            def h_hi(g, i):
                dve.wait_ge(h_ok.sem, h_ok.at(g, 2 * i + 2))
                if i >= 3:
                    dve.wait_ge(h_used.sem, h_used.at(g, i - 2))
                else:
                    if past(g, 1):
                        dve.wait_ge(f_full.sem, f_full.at(g - 1, 2))
                nc.vector.tensor_copy(hT[i % 3][0][:], h_tmp[i % 2][:]).then_inc(hh.sem, 1)

            def f_sum(g, t):
                dve.wait_ge(f_full.sem, f_full.at(g, t + 1))
                dve.wait_ge(yb_ok.sem, yb_ok.at(g, t + 1))
                if past(g, 1):
                    dve.wait_ge(res_stored.sem, res_stored.at(g - 1, 16))
                nc.vector.tensor_tensor(f_sb[:, t, :], f_bank[t][:, 0:D], yb[:, t, :], ALU.add).then_inc(f_ok.sem, 1)

            def f_scale(g, t):
                dve.wait_ge(frs.sem, frs.at(g, t + 1))
                dve.wait_ge(f_ok.sem, f_ok.at(g, t + 1))
                nc.vector.scalar_tensor_tensor(out=f_sb[:, t, :], in0=f_sb[:, t, :], scalar=fms[:, t, 2:3],
                                               in1=rows["alpha2"][:], op0=ALU.mult, op1=ALU.mult).then_inc(fs.sem, 1)
                dve.wait_ge(fs.sem, fs.at(g, t + 1))
                dve.wait_ge(xg.sem, xg.at(g, t + 1))
                nc.vector.tensor_tensor(f_sb[:, t, :], f_sb[:, t, :], x_res[:, t, :], ALU.add).then_inc(xo.sem, 1)

            def r_scale(g):
                dve.wait_ge(zrs.sem, zrs.at(g, 1))
                dve.wait_ge(z2_ok.sem, z2_ok.at(g, 2))
                for t in range(GT):
                    nc.vector.scalar_tensor_tensor(out=xn[:, t, :], in0=xn[:, t, :], scalar=zms[:, t, 2:3],
                                                   in1=rows["gin"][:], op0=ALU.mult, op1=ALU.mult).then_inc(xn_ok.sem, 1)

            def row_max(g):
                dve.wait_ge(lg_ok.sem, lg_ok.at(g, 1))
                nc.vector.tensor_reduce(lmx[:, 0, :], logit[:], X_AXIS, ALU.max, negate=True).then_inc(lm_ok.sem, 1)

            def comb_norm(g):
                dve.wait_ge(le_ok.sem, le_ok.at(g, 2))
                nc.vector.reciprocal(lrec[:, 0, :], lsum[:, 0, :]).then_inc(lr_ok.sem, 1)
                dve.wait_ge(lr_ok.sem, lr_ok.at(g, 1))
                for t in range(GT):
                    nc.vector.tensor_scalar(comb[:, t, :], comb[:, t, :], lrec[:, 0, t:t + 1], None, ALU.mult).then_inc(cb_ok.sem, 1)

            def slot_max(g):
                dve.wait_ge(r_full.sem, r_full.at(g, 4))
                nc.vector.tensor_reduce(lmx[:, 1, :], r_bank[:, 0:GN].rearrange("p (t n) -> p t n", t=GT), X_AXIS,
                                        ALU.max, negate=True).then_inc(dm_ok.sem, 1)

            def disp_recip(g):
                dve.wait_ge(de_ok.sem, de_ok.at(g, 2))
                nc.vector.reciprocal(lrec[:, 1, :], lsum[:, 1, :]).then_inc(dr_ok.sem, 1)

            def slot_rows(g, t):
                dve.wait_ge(r_full.sem, r_full.at(g, 6 + t))
                dve.wait_ge(dr_ok.sem, dr_ok.at(g, 1))
                if past(g, 1):
                    dve.wait_ge(yn_stored.sem, yn_stored.at(g - 1, 16))
                nc.vector.tensor_scalar(yn[:, t, :], r_bank[:, 0:D], lrec[:, 1, t:t + 1], None, ALU.mult).then_inc(sl_ok.sem, 1)

            def yn_scale(g, t):
                dve.wait_ge(srs.sem, srs.at(g, t + 1))
                dve.wait_ge(sl_ok.sem, sl_ok.at(g, t + 1))
                nc.vector.scalar_tensor_tensor(out=yn[:, t, :], in0=yn[:, t, :], scalar=sms[:, t, 2:3],
                                               in1=rows["g2"][:], op0=ALU.mult, op1=ALU.mult).then_inc(yn_ok.sem, 1)

            def body(a, m, r):
                A, M, R = a is not None, m is not None, r is not None
                if A: norm_stats(a, x_landed, 16, x_in, st, mv, stats, meanvar)
                if R: norm_stats(r, xo, 1, f_sb, st2, mv2, st2_ok, mv2_ok)
                if A: z_step(a)
                if R:
                    if past(r, 1):
                        dve.wait_ge(r_full.sem, r_full.at(r - 1, 7))
                    centre(r, f_sb, xn, mv2, rstd2, rstd2_ok, z2_ok)
                if M: h_hi(m, 0)
                if R: r_scale(r)
                if M: h_hi(m, 1)
                if A:
                    for t in range(GT): lo_T(a, t, U_ZT, zT[0][:, :, tok(t)], zT[1][:, :, tok(t)], zh, zl)
                if M: h_hi(m, 2)
                if R: row_max(r)
                if A: key(a)
                if R: slot_max(r); comb_norm(r); disp_recip(r)
                if A: values(a, 0); values(a, 1); scores(a, 0); scores(a, 1); recips(a, 0)
                if M: h_hi(m, 3)
                if A: context(a, 0); recips(a, 1)
                if R: slot_rows(r, 0)
                if M: h_hi(m, 4)
                if A: lo_T(a, 0, U_CT, cT[0][:], cT[1][:], ch, cl); context(a, 1)
                if R: yn_scale(r, 0); slot_rows(r, 1)
                if A: residual(a, 0); lo_T(a, 1, U_CT, cT[0][:], cT[1][:], ch, cl)
                if A: y_scale(a, 0)
                if R: yn_scale(r, 1)
                if M: h_hi(m, 5)
                if A:
                    lo_T(a, 0, U_YT, yT[0][:, :, tok(0)], yT[1][:, :, tok(0)], yh, yl)
                    residual(a, 1); y_scale(a, 1)
                if M:
                    for t in range(GT): f_sum(m, t)
                if A: lo_T(a, 1, U_YT, yT[0][:, :, tok(1)], yT[1][:, :, tok(1)], yh, yl)
                if M:
                    for t in range(GT): f_scale(m, t)

            run(dve, body)

        @block.gpsimd
        def _(pool):
            def power(g, k, sig_in, src, small, mid, dst, sig_mid, sig_out, kk):
                n = src.shape[1]
                pool.wait_ge(sig_in.sem, sig_in.at(g, k))
                nc.gpsimd.tensor_tensor(mid, src, small[:, 0:n], ALU.add).then_inc(sig_mid.sem, 1)
                pool.wait_ge(sig_mid.sem, sig_mid.at(g, kk))
                nc.gpsimd.tensor_tensor(dst, mid, nhalf[:, 0:n], ALU.pow).then_inc(sig_out.sem, 1)

            def h_lo(g, i):
                pool.wait_ge(hh.sem, hh.at(g, i + 1))
                nc.gpsimd.tensor_tensor(hT[i % 3][1][:], h_tmp[i % 2][:], hT[i % 3][0][:].bitcast(F32),
                                        ALU.subtract).then_inc(hl.sem, 1)

            def r_bias(g, t):
                pool.wait_ge(r_ok.sem, r_ok.at(g, t + 1))
                nc.gpsimd.tensor_tensor(y[:, t, :], y[:, t, :], rows["bo"][:], ALU.add).then_inc(rb_ok.sem, 1)

            def y_shift(g, t):
                pool.wait_ge(ys.sem, ys.at(g, t + 1))
                nc.gpsimd.tensor_tensor(y[:, t, :], y[:, t, :], rows["gamma1"][:], ALU.add).then_inc(y_ok.sem, 1)

            def body(a, m, r):
                A, M, R = a is not None, m is not None, r is not None
                if A: power(a, 2, meanvar, mv[:, :, 1], eps_ln, rstd[:, 0, :], rstd[:, 1, :], ve, rstd_ok, 1)
                if R: power(r, 2, mv2_ok, mv2[:, :, 1], eps_ln, rstd2[:, 0, :], rstd2[:, 1, :], ve2, rstd2_ok, 1)
                if M:
                    for t in range(GT):
                        pool.wait_ge(y_ok.sem, y_ok.at(m, t + 1))
                        if past(m, 1):
                            pool.wait_ge(f_ok.sem, f_ok.at(m - 1, t + 1))
                        nc.gpsimd.tensor_tensor(yb[:, t, :], y[:, t, :], rows["b2"][:], ALU.add).then_inc(yb_ok.sem, 1)
                if R: power(r, 2, zss, zms[:, :, 0], eps, zms[:, :, 1], zms[:, :, 2], zve, zrs, 1)
                if M: h_lo(m, 0); h_lo(m, 1); h_lo(m, 2)
                if M:
                    pool.wait_ge(res_landed.sem, res_landed.at(m, 16))
                    for t in range(GT):
                        nc.gpsimd.tensor_tensor(x_res[:, t, :], x_res[:, t, :], rows["gamma2"][:], ALU.add).then_inc(xg.sem, 1)
                if M: h_lo(m, 3)
                if R: power(r, 1, sss, sms[:, 0, 0:1], eps, sms[:, 0, 1:2], sms[:, 0, 2:3], sve, srs, 1)
                if M: h_lo(m, 4)
                if R: power(r, 2, sss, sms[:, 1, 0:1], eps, sms[:, 1, 1:2], sms[:, 1, 2:3], sve, srs, 2)
                if A:
                    r_bias(a, 0)
                    power(a, 1, rss, rms[:, 0, 0:1], eps, rms[:, 0, 1:2], rms[:, 0, 2:3], rve, rrs, 1)
                    y_shift(a, 0)
                if M: h_lo(m, 5)
                if A:
                    r_bias(a, 1)
                    power(a, 2, rss, rms[:, 1, 0:1], eps, rms[:, 1, 1:2], rms[:, 1, 2:3], rve, rrs, 2)
                    y_shift(a, 1)
                if M:
                    for t in range(GT):
                        power(m, t + 1, fss, fms[:, t, 0:1], eps, fms[:, t, 1:2], fms[:, t, 2:3], fve, frs, t + 1)

            run(pool, body)


def run(eng, body):
    body(0, None, None)
    body(1, 0, None)
    with eng.Fori(2, NG) as g:
        body(g, g - 1, g - 2)
    body(None, NG - 1, NG - 2)
    body(None, None, NG - 1)


def routes(nc, ctx, sb, ps, sem, ident, nhalf, eps, w_slot2, yn_dram, se_dram):
    HB = 2
    HC = E2 * D // 2
    raw = sb(ctx, "ws_raw", [P, DC, E2 * D])
    ws = [sb(ctx, "ws_hi", [P, DC, E2 * D], F32R), sb(ctx, "ws_lo", [P, DC, E2 * D], F32R)]
    yk = [sb(ctx, f"yk{i}", [P, NS, D]) for i in range(HB)]
    mean = [sb(ctx, f"mean{i}", [P, D]) for i in range(HB)]
    mT = [sb(ctx, "mT_hi", [P, DC, HB, P], F32R), sb(ctx, "mT_lo", [P, DC, HB, P], F32R)]
    se = [sb(ctx, f"se{i}", [P, E2, D]) for i in range(HB)]
    squares = sb(ctx, "se_squares", [P, HB, E2, D], mybir.dt.bfloat16)
    ms = sb(ctx, "r_ms", [P, HB, 3, E2])
    t_bank = [ps(ctx, f"rt_bank{i}", [P, DC, P]) for i in range(HB)]
    bank = [ps(ctx, f"rs_bank{i}", [P, 512]) for i in range(4)]
    w_landed = sem(ctx, "ws_landed", 16)
    y_landed = [sem(ctx, f"yk_landed{i}", 16) for i in range(HB)]
    w_hi, w_lo = sem(ctx, "ws_hi", 2), sem(ctx, "ws_lo", 2)
    added, t_full, m_hi, m_lo = sem(ctx, "added", 6), sem(ctx, "mT_full", 2), sem(ctx, "mT_hi", 2), sem(ctx, "mT_lo", 2)
    full, sq, ve, rs, scaled = (sem(ctx, n, c) for n, c in (("se_full", 8), ("se_ss", 8), ("se_ve", 2), ("se_rs", 2), ("se_ok", 8)))
    stored = [sem(ctx, f"se_stored{i}", 16) for i in range(HB)]
    yn_by_k = yn_dram.rearrange("b (k m n) d -> b k m (n d)", k=E1, n=NS)

    def loop(eng, body):
        body(0)
        with eng.Fori(1, E1) as k:
            body(k)

    with nc.Block() as block:
        @block.sync
        def _(sp):
            def body(k):
                if past(k, 1):
                    sp.wait_ge(w_lo.sem, w_lo.at(k - 1, 2))
                sp.dma_start(raw[:], w_slot2[bass.ds(k, 1)].rearrange("o (c p) f -> p (o c) f", p=P)).then_inc(w_landed.sem, 16)
                for i in range(HB):
                    if past(k, 1):
                        sp.wait_ge(added.sem, added.at(k - 1, 3 * (i + 1)))
                    sp.dma_start(yk[i][:].rearrange("p n d -> p (n d)"),
                                 yn_by_k[i * NB // HB:(i + 1) * NB // HB, bass.ds(k, 1)].rearrange("b o m q -> (b o) m q")
                                 ).then_inc(y_landed[i].sem, 16)
            loop(sp, body)

        @block.tensor
        def _(pe):
            def body(k):
                for i in range(HB):
                    pe.wait_ge(added.sem, added.at(k, 3 * (i + 1)))
                    if past(k, 1):
                        pe.wait_ge(m_lo.sem, m_lo.at(k - 1, i + 1))
                    for c in range(DC):
                        mm = pe.transpose(t_bank[i][:, c, :], mean[i][:, c * P:(c + 1) * P], ident[:])
                    mm.then_inc(t_full.sem, 1)
                pe.wait_ge(m_lo.sem, m_lo.at(k, 2))
                for i in range(HB):
                    for e in range(E2):
                        pe.wait_ge(w_lo.sem, w_lo.at(k, 1 + e // 2))
                        if i:
                            pe.wait_ge(scaled.sem, scaled.at(k, e + 1))
                        else:
                            if past(k, 1):
                                pe.wait_ge(scaled.sem, scaled.at(k - 1, 4 + e + 1))
                        for c in range(DC):
                            for j, (a, b) in enumerate(((0, 0), (0, 1), (1, 0))):
                                mm = pe.matmul(bank[e][:, 0:D], mT[a][:, c, i, :], ws[b][:, c, e * D:(e + 1) * D],
                                               start=c == 0 and j == 0, stop=c == DC - 1 and j == 2)
                        mm.then_inc(full.sem, 1)
            loop(pe, body)

        @block.scalar
        def _(act):
            def body(k):
                act.wait_ge(w_landed.sem, w_landed.at(k, 16))
                if past(k, 1):
                    act.wait_ge(full.sem, full.at(k - 1, 8))
                for n in range(2):
                    nc.scalar.copy(ws[0][:, :, n * HC:(n + 1) * HC], raw[:, :, n * HC:(n + 1) * HC]).then_inc(w_hi.sem, 1)
                for i in range(HB):
                    act.wait_ge(t_full.sem, t_full.at(k, i + 1))
                    nc.scalar.activation(mT[0][:, :, i, :], t_bank[i][:], ACT.Identity, scale=1.0 / NS).then_inc(m_hi.sem, 1)
                for i in range(HB):
                    for e in range(E2):
                        act.wait_ge(full.sem, full.at(k, i * E2 + e + 1))
                        nc.scalar.activation(squares[:, i, e, :], bank[e][:, 0:D], ACT.Square, accum_out=ms[:, i, 0, e:e + 1]).then_inc(sq.sem, 1)
                    act.wait_ge(scaled.sem, scaled.at(k, E2 * (i + 1)))
                    act.dma_start(se_dram[bass.ds(k, 1), i * P:(i + 1) * P, :].rearrange("o r q -> (o r) q"),
                                  se[i][:].rearrange("p e d -> p (e d)")).then_inc(stored[i].sem, 16)
            loop(act, body)
            for s in stored:
                act.wait_ge(s.sem, 16 * E1)

        @block.vector
        def _(dve):
            def body(k):
                for i in range(HB):
                    dve.wait_ge(y_landed[i].sem, y_landed[i].at(k, 16))
                    if past(k, 1):
                        dve.wait_ge(t_full.sem, t_full.at(k - 1, i + 1))
                    nc.vector.tensor_tensor(mean[i][:], yk[i][:, 0, :], yk[i][:, 1, :], ALU.add).then_inc(added.sem, 1)
                    for n in range(2, NS):
                        dve.wait_ge(added.sem, added.at(k, 3 * i + n - 1))
                        nc.vector.tensor_tensor(mean[i][:], mean[i][:], yk[i][:, n, :], ALU.add).then_inc(added.sem, 1)
                for n in range(2):
                    dve.wait_ge(w_hi.sem, w_hi.at(k, n + 1))
                    nc.vector.tensor_tensor(ws[1][:, :, n * HC:(n + 1) * HC], raw[:, :, n * HC:(n + 1) * HC],
                                            ws[0][:, :, n * HC:(n + 1) * HC].bitcast(F32), ALU.subtract).then_inc(w_lo.sem, 1)
                for i in range(HB):
                    dve.wait_ge(m_hi.sem, m_hi.at(k, i + 1))
                    nc.vector.scalar_tensor_tensor(out=mT[1][:, :, i, :], in0=t_bank[i][:], scalar=1.0 / NS,
                                                   in1=mT[0][:, :, i, :].bitcast(F32), op0=ALU.mult,
                                                   op1=ALU.subtract).then_inc(m_lo.sem, 1)
                for i in range(HB):
                    dve.wait_ge(rs.sem, rs.at(k, i + 1))
                    if past(k, 1):
                        dve.wait_ge(stored[i].sem, stored[i].at(k - 1, 16))
                    for e in range(E2):
                        nc.vector.tensor_scalar(se[i][:, e, :], bank[e][:, 0:D], ms[:, i, 2, e:e + 1], SCALE,
                                                ALU.mult, ALU.mult).then_inc(scaled.sem, 1)
            loop(dve, body)

        @block.gpsimd
        def _(pool):
            def body(k):
                for i in range(HB):
                    pool.wait_ge(sq.sem, sq.at(k, E2 * (i + 1)))
                    nc.gpsimd.tensor_tensor(ms[:, i, 1, :], ms[:, i, 0, :], eps[:], ALU.add).then_inc(ve.sem, 1)
                    pool.wait_ge(ve.sem, ve.at(k, i + 1))
                    nc.gpsimd.tensor_tensor(ms[:, i, 2, :], ms[:, i, 1, :], nhalf[:], ALU.pow).then_inc(rs.sem, 1)
            loop(pool, body)


def dispatch(nc, ctx, sb, ps, sem, ident, yn_dram, se_dram, comb_dram, ct_dram, slots2T):
    BUF = 2
    yn = [sb(ctx, f"d_yn{i}", [P, D]) for i in range(BUF)]
    se = [sb(ctx, f"d_se{i}", [P, D]) for i in range(BUF)]
    cb = [sb(ctx, f"d_cb{i}", [P, P]) for i in range(BUF)]
    ynT = [sb(ctx, f"d_ynT{i}", [P, D]) for i in range(BUF)]
    seT = [sb(ctx, f"d_seT{i}", [P, D]) for i in range(BUF)]
    lg = [sb(ctx, f"d_lg{i}", [P, 2, P]) for i in range(BUF)]
    dT = [sb(ctx, f"d_dT{i}", [P, P]) for i in range(BUF)]
    ct = [sb(ctx, f"d_ct{i}", [P, P]) for i in range(BUF)]
    mx = sb(ctx, "d_mx", [P, BUF, 2])
    sm = sb(ctx, "d_sm", [P, BUF, 2])
    rc = sb(ctx, "d_rc", [P, BUF, 2])
    mask = sb(ctx, "d_mask", [P, P])
    tb = [ps(ctx, f"d_tb{i}", [P, 512]) for i in range(4)]
    lb = [ps(ctx, f"d_lb{i}", [P, 2, P]) for i in range(1)]
    db = ps(ctx, "d_db", [P, P])
    sb2 = ps(ctx, "d_sb", [P, D])
    cbk = ps(ctx, "d_cbk", [P, P])
    landed = [sem(ctx, f"d_landed{i}", 48) for i in range(BUF)]
    stored = [sem(ctx, f"d_stored{i}", 16) for i in range(BUF)]
    n2 = lambda name: sem(ctx, name, 1)
    t_full, ynT_ok, seT_ok, lg_full, lg_ok, mx_ok, ex_ok, rc_ok, nd_ok, nc_ok = (
        sem(ctx, n, c) for n, c in (("d_t_full", 2), ("d_ynT", 1), ("d_seT", 1), ("d_lg_full", 1), ("d_lg", 1),
                                    ("d_max", 1), ("d_exp", 2), ("d_recip", 1), ("d_disp", 1), ("d_comb", 1)))
    dT_full, dT_ok, s_full, s_ok, c_full, ct_ok, mask_ok = (n2(n) for n in (
        "d_dT_full", "d_dT", "d_s_full", "d_s", "d_c_full", "d_ct", "d_mask"))
    se_by_b = se_dram.rearrange("k (b m) (e d) -> b k (m e) d", m=M2, e=E2)

    def over_pairs(eng, body):
        body(1)
        with eng.Fori(2, NB // 2) as i:
            body(i)

    with nc.Block() as block:
        @block.sync
        def _(sp):
            def load(b, p):
                if past(b, 2):
                    sp.wait_ge(s_full.sem, s_full.at(b - 2, 1))
                sp.dma_start(yn[p][:], yn_dram[bass.ds(b, 1)].rearrange("o p d -> (o p) d")).then_inc(landed[p].sem, 16)
                sp.dma_start(se[p][:], se_by_b[bass.ds(b, 1)].rearrange("o k r d -> (o k) r d")).then_inc(landed[p].sem, 16)
                sp.dma_start(cb[p][:], comb_dram[bass.ds(b, 1)].rearrange("o p d -> (o p) d")).then_inc(landed[p].sem, 16)

            def store(b, p):
                sp.wait_ge(ct_ok.sem, ct_ok.at(b, 1))
                sp.dma_start(ct_dram[bass.ds(b, 1)].rearrange("o p d -> (o p) d"), ct[p][:]).then_inc(stored[p].sem, 16)

            load(0, 0)
            load(1, 1)
            def pair(i):
                load(2 * i, 0)
                store(2 * i - 2, 0)
                load(2 * i + 1, 1)
                store(2 * i - 1, 1)

            over_pairs(sp, pair)
            store(NB - 2, 0)
            store(NB - 1, 1)
            for s in stored:
                sp.wait_ge(s.sem, 16 * NB // 2)

        @block.tensor
        def _(pe):
            def front(b, p, n):
                pe.wait_ge(landed[p].sem, n * 48 + 48)
                if past(b, 2):
                    pe.wait_ge(ynT_ok.sem, ynT_ok.at(b - 2, 1))
                if past(b, 2):
                    pe.wait_ge(seT_ok.sem, seT_ok.at(b - 2, 1))
                for k, (src, bank) in enumerate(((yn[p], tb[2 * p]), (se[p], tb[2 * p + 1]))):
                    for c in range(DC):
                        mm = pe.transpose(bank[:, c * P:(c + 1) * P], src[:, c * P:(c + 1) * P], ident[:])
                    mm.then_inc(t_full.sem, 1)

            def logits(b, p):
                pe.wait_ge(ynT_ok.sem, ynT_ok.at(b, 1))
                pe.wait_ge(seT_ok.sem, seT_ok.at(b, 1))
                if past(b, 1):
                    pe.wait_ge(lg_ok.sem, lg_ok.at(b - 1, 1))
                for k, (left, right) in enumerate(((ynT[p], seT[p]), (seT[p], ynT[p]))):
                    for c in range(DC):
                        mm = pe.matmul(lb[0][:, k, :], left[:, c * P:(c + 1) * P], right[:, c * P:(c + 1) * P],
                                       start=c == 0, stop=c == DC - 1)
                mm.then_inc(lg_full.sem, 1)

            def disp_T(b, p):
                pe.wait_ge(nd_ok.sem, nd_ok.at(b, 1))
                if past(b, 1):
                    pe.wait_ge(dT_ok.sem, dT_ok.at(b - 1, 1))
                pe.transpose(db[:], lg[p][:, 1, :], ident[:]).then_inc(dT_full.sem, 1)

            def back(b, p):
                pe.wait_ge(nc_ok.sem, nc_ok.at(b, 1))
                if past(b, 1):
                    pe.wait_ge(ct_ok.sem, ct_ok.at(b - 1, 1))
                pe.matmul(cbk[:], lg[p][:, 0, :], cb[p][:], start=True, stop=True).then_inc(c_full.sem, 1)
                pe.wait_ge(dT_ok.sem, dT_ok.at(b, 1))
                if past(b, 1):
                    pe.wait_ge(s_ok.sem, s_ok.at(b - 1, 1))
                for c in range(DC):
                    mm = pe.matmul(sb2[:, c * P:(c + 1) * P], yn[p][:, c * P:(c + 1) * P], dT[p][:], start=True, stop=True)
                mm.then_inc(s_full.sem, 1)

            front(0, 0, 0)
            logits(0, 0)
            front(1, 1, 0)

            def pair(i):
                disp_T(2 * i - 2, 0)
                logits(2 * i - 1, 1)
                back(2 * i - 2, 0)
                front(2 * i, 0, i)
                disp_T(2 * i - 1, 1)
                logits(2 * i, 0)
                back(2 * i - 1, 1)
                front(2 * i + 1, 1, i)

            over_pairs(pe, pair)
            disp_T(NB - 2, 0)
            logits(NB - 1, 1)
            back(NB - 2, 0)
            disp_T(NB - 1, 1)
            back(NB - 1, 1)

        @block.scalar
        def _(act):
            def front(b, p):
                act.wait_ge(t_full.sem, t_full.at(b, 1))
                if past(b, 2):
                    act.wait_ge(lg_full.sem, lg_full.at(b - 2, 1))
                nc.scalar.copy(ynT[p][:], tb[2 * p][:, 0:D]).then_inc(ynT_ok.sem, 1)

            def exps(b, p):
                act.wait_ge(mx_ok.sem, mx_ok.at(b, 1))
                for k in range(2):
                    nc.scalar.activation(lg[p][:, k, :], lg[p][:, k, :], ACT.Exp, bias=mx[:, p, k:k + 1],
                                         accum_out=sm[:, p, k:k + 1]).then_inc(ex_ok.sem, 1)

            def back(b, p):
                act.wait_ge(dT_full.sem, dT_full.at(b, 1))
                if past(b, 2):
                    act.wait_ge(s_full.sem, s_full.at(b - 2, 1))
                nc.scalar.copy(dT[p][:], db[:]).then_inc(dT_ok.sem, 1)
                act.wait_ge(s_full.sem, s_full.at(b, 1))
                nc.scalar.copy(slots2T[:, :, bass.ds(b, 1), :].rearrange("p c o n -> p c (o n)"),
                               sb2[:].rearrange("p (c n) -> p c n", c=DC)).then_inc(s_ok.sem, 1)

            front(0, 0)
            exps(0, 0)
            front(1, 1)
            def pair(i):
                back(2 * i - 2, 0)
                front(2 * i, 0)
                exps(2 * i - 1, 1)
                back(2 * i - 1, 1)
                front(2 * i + 1, 1)
                exps(2 * i, 0)

            over_pairs(act, pair)
            back(NB - 2, 0)
            exps(NB - 1, 1)
            back(NB - 1, 1)

        @block.vector
        def _(dve):
            def front(b, p):
                dve.wait_ge(t_full.sem, t_full.at(b, 2))
                if past(b, 2):
                    dve.wait_ge(lg_full.sem, lg_full.at(b - 2, 1))
                nc.vector.tensor_copy(seT[p][:], tb[2 * p + 1][:, 0:D]).then_inc(seT_ok.sem, 1)

            def logits(b, p):
                dve.wait_ge(lg_full.sem, lg_full.at(b, 1))
                if past(b, 2):
                    dve.wait_ge(c_full.sem, c_full.at(b - 2, 1))
                nc.vector.tensor_tensor(lg[p][:], lb[0][:], mask[:].unsqueeze(1).broadcast_to([P, 2, P]), ALU.add).then_inc(lg_ok.sem, 1)
                dve.wait_ge(lg_ok.sem, lg_ok.at(b, 1))
                nc.vector.tensor_reduce(mx[:, p, :], lg[p][:], X_AXIS, ALU.max, negate=True).then_inc(mx_ok.sem, 1)

            def norms(b, p):
                dve.wait_ge(ex_ok.sem, ex_ok.at(b, 2))
                nc.vector.reciprocal(rc[:, p, :], sm[:, p, :]).then_inc(rc_ok.sem, 1)
                dve.wait_ge(rc_ok.sem, rc_ok.at(b, 1))
                nc.vector.tensor_scalar(lg[p][:, 1, :], lg[p][:, 1, :], rc[:, p, 1:2], None, ALU.mult).then_inc(nd_ok.sem, 1)
                nc.vector.tensor_scalar(lg[p][:, 0, :], lg[p][:, 0, :], rc[:, p, 0:1], None, ALU.mult).then_inc(nc_ok.sem, 1)

            def back(b, p, n):
                dve.wait_ge(c_full.sem, c_full.at(b, 1))
                if past(n, 1):
                    dve.wait_ge(stored[p].sem, stored[p].at(n - 1, 16))
                nc.vector.tensor_copy(ct[p][:], cbk[:]).then_inc(ct_ok.sem, 1)

            dve.wait_ge(mask_ok.sem, 3)
            front(0, 0)
            logits(0, 0)
            norms(0, 0)
            front(1, 1)
            def pair(i):
                logits(2 * i - 1, 1)
                back(2 * i - 2, 0, i - 1)
                norms(2 * i - 1, 1)
                front(2 * i, 0)
                logits(2 * i, 0)
                back(2 * i - 1, 1, i - 1)
                norms(2 * i, 0)
                front(2 * i + 1, 1)

            over_pairs(dve, pair)
            logits(NB - 1, 1)
            back(NB - 2, 0, NB // 2 - 1)
            norms(NB - 1, 1)
            back(NB - 1, 1, NB // 2 - 1)

        @block.gpsimd
        def _(pool):
            nc.gpsimd.memset(mask[:], 0.0).then_inc(mask_ok.sem, 1)
            pool.wait_ge(mask_ok.sem, 1)
            blocks = mask[:].rearrange("p (k j) -> p k j", k=E1)
            nc.gpsimd.affine_select(out=blocks, in_=blocks, compare_op=ALU.is_ge, fill=MASKED, base=0,
                                    pattern=[[-S1, E1], [0, S1]], channel_multiplier=1).then_inc(mask_ok.sem, 1)
            pool.wait_ge(mask_ok.sem, 2)
            nc.gpsimd.affine_select(out=blocks, in_=blocks, compare_op=ALU.is_ge, fill=MASKED, base=S1 - 1,
                                    pattern=[[S1, E1], [0, S1]], channel_multiplier=-1).then_inc(mask_ok.sem, 1)



def experts(nc, ctx, sb, ps, sem, ident, slots2T, w1, b1, w2, b2, o_dram):
    PIECES = 4
    CH = HID // P // PIECES
    W = CH * P
    RAW, SPL = 3, 2
    raw1 = [sb(ctx, f"raw1_{i}", [P, DC, 2, W]) for i in range(PIECES)]
    raw2 = [sb(ctx, f"raw2_{i}", [P, CH, D]) for i in range(PIECES)]
    w1s = [[sb(ctx, f"x_w1_{i}_{s}", [P, DC, 2, W], F32R) for s in range(2)] for i in range(SPL)]
    w2s = [[sb(ctx, f"x_w2_{i}_{s}", [P, CH, D], F32R) for s in range(2)] for i in range(SPL)]
    xT = [sb(ctx, f"x_in_{s}", [P, DC, XR], F32R) for s in range(2)]
    gel = sb(ctx, "x_gelu", [P, CH, XR])
    aT = [sb(ctx, f"x_act", [P, CH, XR])]
    aTs = [[sb(ctx, f"x_aT_{i}_{s}", [P, CH, XR], F32R) for s in range(2)] for i in range(2)]
    o_sb = sb(ctx, "x_o", [P, 2, D])
    b1r = sb(ctx, "x_b1r", [NX, 2 * HID])
    b1T = sb(ctx, "x_b1T", [P, 2 * HID // P, NX])
    b2r = sb(ctx, "x_b2r", [P, D])
    u_bank = [ps(ctx, f"u_bank{i}", [P, 2, XR]) for i in range(4)]
    o_bank = [[ps(ctx, f"o_bank{i}{t}", [P, 512]) for t in range(2)] for i in range(2)]

    raw_landed = [sem(ctx, f"raw_landed{i}", 48) for i in range(PIECES)]
    b1_landed, b2_landed = sem(ctx, "b1_landed", 16), sem(ctx, "b2_landed", 16)
    b1_T, b1_ok = sem(ctx, "b1_T"), sem(ctx, "b1_ok")
    h1, h2, l1, l2 = (sem(ctx, n, PIECES) for n in ("w1_hi", "w2_hi", "w1_lo", "w2_lo"))
    xh, xl = sem(ctx, "x_hi"), sem(ctx, "x_lo")
    u_full, g_ok, a_ok = (sem(ctx, n, PIECES * CH) for n in ("u_full", "gelu_ok", "act_ok"))
    ah, al = sem(ctx, "act_hi", PIECES), sem(ctx, "act_lo", PIECES)
    down_done, o_ok = sem(ctx, "down_done", PIECES), sem(ctx, "o_ok", 2)
    o_stored = sem(ctx, "o_stored", 32)
    w1x = w1.rearrange("k e (c p) (g h) -> (k e) p c g h", p=P, g=2)
    w2x = w2.rearrange("k e (c p) d -> (k e) p c d", p=P)
    b2x = b2.rearrange("k e d -> (k e) d")
    o_rows = o_dram.rearrange("(b k m e) d -> k e b m d", k=E1, m=M2, e=E2)
    slots_of = slots2T[:].rearrange("p c b (k m e) -> p c b m k e", k=E1, m=M2)

    def loop(eng, body):
        body(0, 0, 0)
        with eng.Fori(0, E1) as k:
            for e in range(E2):
                body(k, e, None)

    with nc.Block() as block:
        def over_experts(eng, body):
            for e in range(E2):
                body(e, 0, e, e == 0)
            with eng.Fori(1, E1) as k:
                for e in range(E2):
                    body(k * E2 + e, k, e, False)

        @block.sync
        def _(sp):
            sp.dma_start(b1r[:], b1.rearrange("k e h -> (k e) h")).then_inc(b1_landed.sem, 16)

            def store(x, k, e):
                sp.wait_ge(o_ok.sem, o_ok.at(x, 2))
                for t in range(2):
                    sp.dma_start(o_rows[bass.ds(k, 1), e, t * NB // 2:(t + 1) * NB // 2].rearrange("o b m d -> (o b) m d"),
                                 o_sb[:, t, :]).then_inc(o_stored.sem, 16)

            def body(x, k, e, first):
                for i in range(PIECES):
                    if past(x, 1):
                        sp.wait_ge(l1.sem, l1.at(x - 1, i + 1))
                    if past(x, 1):
                        sp.wait_ge(l2.sem, l2.at(x - 1, i + 1))
                    for g in range(2):
                        sp.dma_start(raw1[i][:, :, g, :], w1x[bass.ds(x, 1), :, :, g, i * W:(i + 1) * W].rearrange(
                            "o p c h -> (o p) c h")).then_inc(raw_landed[i].sem, 16)
                    sp.dma_start(raw2[i][:], w2x[bass.ds(x, 1), :, i * CH:(i + 1) * CH, :].rearrange(
                        "o p c d -> (o p) c d")).then_inc(raw_landed[i].sem, 16)
                if not first:
                    store(x - 1, k if e else k - 1, (e - 1) % E2)
                if past(x, 1):
                    sp.wait_ge(o_ok.sem, o_ok.at(x - 1, 2))
                sp.dma_start(b2r[:], b2x[bass.ds(x, 1)].rearrange("o d -> (o d)").partition_broadcast(P)
                             ).then_inc(b2_landed.sem, 16)
            over_experts(sp, body)
            store(NX - 1, E1 - 1, E2 - 1)
            sp.wait_ge(o_stored.sem, o_stored.n * NX)

        @block.tensor
        def _(pe):
            pe.wait_ge(b1_landed.sem, 16)
            for j in range(2 * HID // P):
                mm = pe.transpose(u_bank[0][:].rearrange("p a b -> p (a b)")[:, j * NX:(j + 1) * NX],
                                  b1r[:, j * P:(j + 1) * P], ident[0:NX, 0:NX])
            mm.then_inc(b1_T.sem, 1)
            pe.wait_ge(b1_ok.sem, 1)

            def up(x, i):
                if i == 0:
                    pe.wait_ge(xl.sem, xl.at(x, 1))
                pe.wait_ge(l1.sem, l1.at(x, i + 1))
                for c2 in range(CH):
                    n = i * CH + c2
                    if n >= 4:
                        pe.wait_ge(a_ok.sem, a_ok.at(x, n - 3))
                    else:
                        if past(x, 1):
                            pe.wait_ge(a_ok.sem, a_ok.at(x - 1, PIECES * CH - 3 + n))
                    for g in range(2):
                        for c in range(DC):
                            for j, (a, b) in enumerate(((0, 0), (0, 1), (1, 0))):
                                mm = pe.matmul(u_bank[n % 4][:, g, :], w1s[i % 2][a][:, c, g, c2 * P:(c2 + 1) * P],
                                               xT[b][:, c, :], start=c == 0 and j == 0, stop=c == DC - 1 and j == 2)
                    mm.then_inc(u_full.sem, 1)

            def down(x, e, i):
                pe.wait_ge(l2.sem, l2.at(x, i + 1))
                pe.wait_ge(al.sem, al.at(x, i + 1))
                if i == 0:
                    if past(x, 2):
                        pe.wait_ge(o_ok.sem, o_ok.at(x - 2, 2))
                for t in range(2):
                    for c2 in range(CH):
                        for j, (a, b) in enumerate(((0, 0), (0, 1), (1, 0))):
                            mm = pe.matmul(o_bank[e % 2][t][:, 0:D], aTs[i % 2][a][:, c2, t * P:(t + 1) * P],
                                           w2s[i % 2][b][:, c2, :], start=i == 0 and c2 == 0 and j == 0,
                                           stop=i == PIECES - 1 and c2 == CH - 1 and j == 2)
                mm.then_inc(down_done.sem, 1)

            def body(x, k, e, first):
                up(x, 0)
                if not first:
                    down(x - 1, (e - 1) % 2, PIECES - 1)
                for i in range(1, PIECES):
                    up(x, i)
                    down(x, e, i - 1)
            over_experts(pe, body)
            down(NX - 1, (E2 - 1) % 2, PIECES - 1)

        @block.scalar
        def _(act):
            act.wait_ge(b1_T.sem, 1)
            nc.scalar.copy(b1T[:].rearrange("p j x -> p (j x)"), u_bank[0][:].rearrange("p a b -> p (a b)")).then_inc(b1_ok.sem, 1)
            act.wait_ge(b1_ok.sem, 1)

            def split(x, k, e, i):
                act.wait_ge(raw_landed[i].sem, x * 48 + 48)
                if i >= 2:
                    act.wait_ge(down_done.sem, down_done.at(x, i - 1))
                else:
                    if past(x, 1):
                        act.wait_ge(down_done.sem, down_done.at(x - 1, i + 3))
                nc.scalar.copy(w1s[i % 2][0][:], raw1[i][:]).then_inc(h1.sem, 1)

            def rows_hi(x, k, e):
                if past(x, 1):
                    act.wait_ge(u_full.sem, u_full.at(x - 1, PIECES * CH))
                src = slots_of[:, :, :, :, bass.ds(k, 1), e]
                nc.scalar.copy(xT[0][:].rearrange("p c (b m) -> p c b m", m=M2),
                               src.rearrange("p c b m o -> p c b (m o)")).then_inc(xh.sem, 1)

            def gelu(x, i):
                for c2 in range(CH):
                    n = i * CH + c2
                    act.wait_ge(u_full.sem, u_full.at(x, n + 1))
                    if c2 == 0:
                        if i:
                            act.wait_ge(a_ok.sem, a_ok.at(x, i * CH))
                        else:
                            if past(x, 1):
                                act.wait_ge(a_ok.sem, a_ok.at(x - 1, PIECES * CH))
                    nc.scalar.activation(gel[:, c2, :], u_bank[n % 4][:, 1, :], ACT.Gelu_apprx_tanh,
                                         bias=b1T[:, HID // P + n, bass.ds(x, 1)]).then_inc(g_ok.sem, 1)

            def act_hi(x, i):
                act.wait_ge(a_ok.sem, a_ok.at(x, (i + 1) * CH))
                if i >= 2:
                    act.wait_ge(down_done.sem, down_done.at(x, i - 1))
                else:
                    if past(x, 1):
                        act.wait_ge(down_done.sem, down_done.at(x - 1, i + 3))
                nc.scalar.copy(aTs[i % 2][0][:], aT[0][:]).then_inc(ah.sem, 1)

            def body(x, k, e, first):
                rows_hi(x, k, e)
                split(x, k, e, 0)
                if not first:
                    gelu(x - 1, PIECES - 1)
                    act_hi(x - 1, PIECES - 1)
                for i in range(PIECES - 1):
                    split(x, k, e, i + 1)
                    gelu(x, i)
                    act_hi(x, i)
            over_experts(act, body)
            gelu(NX - 1, PIECES - 1)
            act_hi(NX - 1, PIECES - 1)

        @block.vector
        def _(dve):
            dve.wait_ge(b1_ok.sem, 1)

            def split(x, i):
                dve.wait_ge(raw_landed[i].sem, x * 48 + 48)
                if i >= 2:
                    dve.wait_ge(down_done.sem, down_done.at(x, i - 1))
                else:
                    if past(x, 1):
                        dve.wait_ge(down_done.sem, down_done.at(x - 1, i + 3))
                nc.vector.tensor_copy(w2s[i % 2][0][:], raw2[i][:]).then_inc(h2.sem, 1)
                dve.wait_ge(h1.sem, h1.at(x, i + 1))
                nc.vector.tensor_tensor(w1s[i % 2][1][:], raw1[i][:], w1s[i % 2][0][:].bitcast(F32), ALU.subtract).then_inc(l1.sem, 1)

            def rows_lo(x, k, e):
                dve.wait_ge(xh.sem, xh.at(x, 1))
                src = slots_of[:, :, :, :, bass.ds(k, 1), e].rearrange("p c b m o -> p c b (m o)")
                nc.vector.tensor_tensor(xT[1][:].rearrange("p c (b m) -> p c b m", m=M2), src,
                                        xT[0][:].bitcast(F32).rearrange("p c (b m) -> p c b m", m=M2),
                                        ALU.subtract).then_inc(xl.sem, 1)

            def gate(x, i):
                for c2 in range(CH):
                    n = i * CH + c2
                    dve.wait_ge(g_ok.sem, g_ok.at(x, n + 1))
                    if c2 == 0:
                        if i:
                            dve.wait_ge(al.sem, al.at(x, i))
                        else:
                            if past(x, 1):
                                dve.wait_ge(al.sem, al.at(x - 1, PIECES))
                    nc.vector.scalar_tensor_tensor(out=aT[0][:, c2, :], in0=u_bank[n % 4][:, 0, :],
                                                   scalar=b1T[:, n, bass.ds(x, 1)], in1=gel[:, c2, :],
                                                   op0=ALU.add, op1=ALU.mult).then_inc(a_ok.sem, 1)

            def rows_out(x, e):
                dve.wait_ge(down_done.sem, down_done.at(x, PIECES))
                dve.wait_ge(b2_landed.sem, 16 * x + 16)
                if past(x, 1):
                    dve.wait_ge(o_stored.sem, o_stored.at(x - 1, 32))
                for t in range(2):
                    nc.vector.tensor_tensor(o_sb[:, t, :], o_bank[e % 2][t][:, 0:D], b2r[:], ALU.add).then_inc(o_ok.sem, 1)

            def body(x, k, e, first):
                rows_lo(x, k, e)
                split(x, 0)
                if not first:
                    gate(x - 1, PIECES - 1)
                for i in range(PIECES - 1):
                    split(x, i + 1)
                    gate(x, i)
                    if i == 0 and not first:
                        rows_out(x - 1, (e - 1) % 2)
            over_experts(dve, body)
            gate(NX - 1, PIECES - 1)
            rows_out(NX - 1, (E2 - 1) % 2)

        @block.gpsimd
        def _(pool):
            def split(x, i):
                pool.wait_ge(h2.sem, h2.at(x, i + 1))
                nc.gpsimd.tensor_tensor(w2s[i % 2][1][:], raw2[i][:], w2s[i % 2][0][:].bitcast(F32), ALU.subtract).then_inc(l2.sem, 1)

            def act_lo(x, i):
                pool.wait_ge(ah.sem, ah.at(x, i + 1))
                nc.gpsimd.tensor_tensor(aTs[i % 2][1][:], aT[0][:], aTs[i % 2][0][:].bitcast(F32), ALU.subtract).then_inc(al.sem, 1)

            def body(x, k, e, first):
                split(x, 0)
                if not first:
                    act_lo(x - 1, PIECES - 1)
                for i in range(PIECES - 1):
                    split(x, i + 1)
                    act_lo(x, i)
            over_experts(pool, body)
            act_lo(NX - 1, PIECES - 1)


def combine(nc, ctx, sb, ps, sem, ct_dram, o_dram, res_dram, out):
    BUF = 4
    o_sb = [sb(ctx, f"c_o{i}", [P, D]) for i in range(BUF)]
    ct = [sb(ctx, f"c_ct{i}", [P, P]) for i in range(BUF)]
    res = [sb(ctx, f"c_res{i}", [P, D]) for i in range(BUF)]
    y = [sb(ctx, f"c_y{i}", [P, D]) for i in range(BUF)]
    bank = [ps(ctx, f"c_bank{i}", [P, 512]) for i in range(BUF)]
    landed = [sem(ctx, f"c_landed{i}", 48) for i in range(BUF)]
    stored = [sem(ctx, f"c_stored{i}", 16) for i in range(BUF)]
    full, added = sem(ctx, "c_full", BUF), sem(ctx, "c_added", BUF)
    out_rows = out.rearrange("b n d -> (b n) d")

    def loop(eng, body):
        for i in range(BUF):
            body(0, i)
        with eng.Fori(1, NB // BUF) as r:
            for i in range(BUF):
                body(r, i)

    with nc.Block() as block:
        @block.sync
        def _(sp):
            def body(r, i):
                if past(r, 1):
                    sp.wait_ge(added.sem, added.at(r - 1, i + 1))
                rows = bass.ds(r * BUF * P + i * P, P)
                sp.dma_start(o_sb[i][:], o_dram[rows, :]).then_inc(landed[i].sem, 16)
                sp.dma_start(ct[i][:], ct_dram[bass.ds(r * BUF + i, 1)].rearrange("o p n -> (o p) n")).then_inc(landed[i].sem, 16)
                sp.dma_start(res[i][:], res_dram[rows, :]).then_inc(landed[i].sem, 16)
            loop(sp, body)

        @block.tensor
        def _(pe):
            def body(r, i):
                pe.wait_ge(landed[i].sem, r * 48 + 48)
                if past(r, 1):
                    pe.wait_ge(added.sem, added.at(r - 1, i + 1))
                pe.matmul(bank[i][:, 0:D], ct[i][:], o_sb[i][:], start=True, stop=True).then_inc(full.sem, 1)
            loop(pe, body)

        @block.vector
        def _(dve):
            def body(r, i):
                dve.wait_ge(full.sem, full.at(r, i + 1))
                if past(r, 1):
                    dve.wait_ge(stored[i].sem, stored[i].at(r - 1, 16))
                nc.vector.tensor_tensor(y[i][:], bank[i][:, 0:D], res[i][:], ALU.add).then_inc(added.sem, 1)
            loop(dve, body)

        @block.scalar
        def _(act):
            def body(r, i):
                act.wait_ge(added.sem, added.at(r, i + 1))
                act.dma_start(out_rows[bass.ds(r * BUF * P + i * P, P), :], y[i][:]).then_inc(stored[i].sem, 16)
            loop(act, body)
            for s in stored:
                act.wait_ge(s.sem, 16 * NB // BUF)


_INS = ['x', 'adj', 'L0_gnn_wq', 'L0_gnn_bq', 'L0_gnn_wk', 'L0_gnn_bk', 'L0_gnn_wv', 'L0_gnn_bv', 'L0_gnn_wo',
        'L0_gnn_bo', 'L0_gnn_w1', 'L0_gnn_b1', 'L0_gnn_w2', 'L0_gnn_b2', 'L0_gnn_alpha1', 'L0_gnn_gamma1',
        'L0_gnn_alpha2', 'L0_gnn_gamma2', 'L0_ffn_gamma_in', 'L0_ffn_slots1', 'L0_ffn_gamma2', 'L0_ffn_w_slot2',
        'L0_ffn_w1', 'L0_ffn_b1', 'L0_ffn_w2', 'L0_ffn_b2']


def kernel(**inputs):
    import numpy as _np
    import concourse.bacc as _bacc
    from concourse import mybir as _mybir
    from concourse.bass_utils import run_bass_kernel_spmd as _run

    nc = _bacc.Bacc("TRN2", target_bir_lowering=False, num_devices=1, dynamic_dma_scratch_size=1024)
    arrays, args = {}, []
    for name in _INS:
        a = _np.ascontiguousarray(inputs[name])
        arrays[f"in_{name}_dram"] = a
        args.append(nc.dram_tensor(f"in_{name}_dram", a.shape, _mybir.dt.from_np(a.dtype), kind="ExternalInput").ap())
    args.append(nc.dram_tensor("out_0_dram", (NB, P, D), F32, kind="ExternalOutput").ap())
    build(nc, *args)
    r = _run(nc, [arrays], core_ids=[0])
    return r.results[0]["out_0_dram"]
```

```python
from contextlib import ExitStack

import concourse.bass as bass
from concourse import mybir

F32 = mybir.dt.float32
F32R = mybir.dt.float32r
BF16 = mybir.dt.bfloat16
ALU = mybir.AluOpType
ACT = mybir.ActivationFunctionType
X_AXIS = mybir.AxisListType.X

P = 128
D = 384
DC = D // P
NB = 64
H = 8
DH = D // H
HP = 64
FF = 1536
FC = FF // P
GT = 2
GN = GT * P
NG = NB // GT
PAIRS = FC // 2
E1, S1, E2, M2 = 8, 16, 4, 4
NS = S1 // E2
NX = E1 * E2
HID = 1024
XR = NB * M2
EPS_LN = 1e-5
EPS = 1e-6
SCALE = float(D) ** 0.5
MASKED = -1e30


class Signal:

    def __init__(self, sem, per_step):
        self.sem, self.n = sem, per_step

    def at(self, step, k):
        return step * self.n + k


def past(step, n):
    return not isinstance(step, int) or step >= n


def build(nc, x, adj, wq, bq, wk, bk, wv, bv, wo, bo, w1, b1, w2, b2, alpha1, gamma1, alpha2, gamma2,
          f_gamma_in, f_slots1, f_gamma2, f_w_slot2, f_w1, f_b1, f_w2, f_b2, out):
    names, taken = [0], []

    def dram(name, shape):
        return nc.dram_tensor(name, shape, F32, kind="Internal").ap()

    x_rows = x.rearrange("b n d -> (b n) d")
    res_dram = dram("residual", [NB * P, D])
    yn_dram = dram("yn", [NB, P, D])
    comb_dram = dram("comb1T", [NB, P, P])
    se_dram = dram("se2", [E1, NB * M2, E2 * D])
    ct_dram = dram("combT", [NB, P, P])
    o_dram = dram("expert_out", [NB * P, D])

    with ExitStack() as kernel_ctx:
        def sem(ctx, name, per_step=1):
            names[0] += 1
            handle = nc.alloc_semaphore(name=f"{name}_{names[0]}")
            taken.append(handle)
            return Signal(handle, per_step)

        def free_semaphores():
            nc.clear_and_free_semaphores(list(taken))
            taken.clear()
            nc.all_engine_barrier()

        def sb(ctx, name, shape, dt=F32):
            return ctx.enter_context(nc.sbuf_tensor(name, shape, dt))

        def ps(ctx, name, shape):
            return ctx.enter_context(nc.psum_tensor(name, shape, F32))

        ident = sb(kernel_ctx, "ident", [P, P])
        nhalf = sb(kernel_ctx, "nhalf", [P, 4])
        eps_ln = sb(kernel_ctx, "eps_ln", [P, 4])
        eps = sb(kernel_ctx, "eps", [P, 4])

        with ExitStack() as layer_ctx:
            setup_and_layer(nc, layer_ctx, sb, ps, sem, ident, nhalf, eps_ln, eps, x_rows, adj, wq, bq, wk, bk, wv, bv,
                            wo, bo, w1, b1, w2, b2, alpha1, gamma1, alpha2, gamma2, f_gamma_in, f_slots1,
                            f_gamma2, res_dram, yn_dram, comb_dram)
        free_semaphores()
        with ExitStack() as ctx:
            routes(nc, ctx, sb, ps, sem, ident, nhalf, eps, f_w_slot2, yn_dram, se_dram)
        with ExitStack() as experts_ctx:
            slots2T = sb(experts_ctx, "slots2T", [P, DC, NB, P])
            with ExitStack() as ctx:
                dispatch(nc, ctx, sb, ps, sem, ident, yn_dram, se_dram, comb_dram, ct_dram, slots2T)
            with ExitStack() as ctx:
                experts(nc, ctx, sb, ps, sem, ident, slots2T, f_w1, f_b1, f_w2, f_b2, o_dram)
        with ExitStack() as ctx:
            combine(nc, ctx, sb, ps, sem, ct_dram, o_dram, res_dram, out)


def setup_and_layer(nc, ctx, sb, ps, sem, ident, nhalf, eps_ln, eps, x_rows, adj, wq, bq, wk, bk, wv, bv, wo, bo, w1, b1,
                    w2, b2, alpha1, gamma1, alpha2, gamma2, f_gamma_in, f_slots1, f_gamma2, res_dram,
                    yn_dram, comb_dram):
    def split_pair(name, shape):
        return [sb(ctx, name + "_hi", shape, F32R), sb(ctx, name + "_lo", shape, F32R)]

    wq_s = split_pair("wq", [P, DC, H * HP])
    wk_s = split_pair("wk", [P, DC, H * HP])
    wv_s = split_pair("wv", [P, DC, D])
    wo_s = split_pair("wo", [P, DC, D])
    w1_s = split_pair("w1", [P, DC, FF])
    w2_s = split_pair("w2", [P, FC, D])
    phiT = sb(ctx, "phiT", [P, DC, P])
    bqk = sb(ctx, "bqk", [P, 2, H // 2])
    b1c = sb(ctx, "b1c", [P, FC])
    rows = {n: sb(ctx, "row_" + n, [P, D]) for n in
            ("bv", "bo", "alpha1", "gamma1", "b2", "alpha2", "gamma2", "gin", "g2")}

    with ExitStack() as setup:
        stage = [sb(setup, f"stage{i}", [P, 12 * D]) for i in range(2)]
        phi = sb(setup, "phi", [P, D])
        phi_sq = sb(setup, "phi_sq", [P, D])
        phi_ss = sb(setup, "phi_ss", [P, 4])
        tp = ps(setup, "tp", [P, DC, P])
        staged = [sem(setup, "staged0"), sem(setup, "staged1")]
        zeroed = sem(setup, "zeroed")
        hi_done = sem(setup, "hi_done")
        lo_done = sem(setup, "lo_done")
        small = sem(setup, "small")
        pool_done = sem(setup, "pool_done")
        phi_done = sem(setup, "phi_done")
        phi_T = sem(setup, "phi_T")

        def padded(t):
            return t[:, 0:DC * H * HP].rearrange("p (c h e) -> p c h e", c=DC, h=H)

        weights = []
        for i, (w, parts) in enumerate(((wq, wq_s), (wk, wk_s), (wv, wv_s), (wo, wo_s), (w1, w1_s), (w2, w2_s))):
            s = stage[i % 2]
            if i < 2:
                srcs = [(padded(s)[:, c, :, 0:DH], w[c * P:(c + 1) * P, :].rearrange("p (h e) -> p h e", h=H))
                        for c in range(DC)]
                flat = s[:, 0:DC * H * HP]
            else:
                n = w.shape[0] // P * w.shape[1]
                srcs = [(s[:, 0:n].rearrange("p (c f) -> p c f", c=w.shape[0] // P),
                         w.rearrange("(c p) f -> p c f", p=P))]
                flat = s[:, 0:n]
            weights.append((srcs, flat, [t[:].rearrange("p c f -> p (c f)") for t in parts]))

        landed = [0, 0]
        after = []
        for i, (srcs, _, _) in enumerate(weights):
            landed[i % 2] += 16 * len(srcs)
            after.append(landed[i % 2])
        n_small = [0]

        with nc.Block() as block:
            @block.sync
            def _(sp):
                for i, (srcs, _, _) in enumerate(weights):
                    if i < 2:
                        sp.wait_ge(zeroed.sem, i + 1)
                    else:
                        sp.wait_ge(lo_done.sem, i - 1)
                    for dst, src in srcs:
                        sp.dma_start(dst, src).then_inc(staged[i % 2].sem, 16)

            @block.scalar
            def _(act):
                def small_load(dst, src):
                    act.dma_start(dst, src).then_inc(small.sem, 16)
                    n_small[0] += 16

                small_load(phi[:], f_slots1.rearrange("k s d -> (k s) d"))
                for name, src in (("bv", bv), ("bo", bo), ("alpha1", alpha1), ("gamma1", gamma1), ("b2", b2),
                                  ("alpha2", alpha2), ("gamma2", gamma2), ("gin", f_gamma_in)):
                    small_load(rows[name][:], src.partition_broadcast(P))
                small_load(rows["g2"][:], f_gamma2.rearrange("k (o d) -> k o d", o=1).broadcast_to([E1, S1, D]))
                act.wait_ge(zeroed.sem, 3)
                for n, b in enumerate((bq, bk)):
                    for half in range(2):
                        src = b.rearrange("(m two e) -> two e m", two=2, e=DH)[half]
                        for m in range(H // 2):
                            small_load(bqk[HP * half:HP * half + DH, n, m:m + 1], src[:, m:m + 1])
                for m in range(FC):
                    small_load(b1c[:, m:m + 1], b1[m * P:(m + 1) * P].rearrange("(p o) -> p o", o=1))
                for i, (_, flat, parts) in enumerate(weights):
                    act.wait_ge(staged[i % 2].sem, after[i])
                    nc.scalar.copy(parts[0], flat).then_inc(hi_done.sem, 1)
                act.wait_ge(small.sem, n_small[0])
                nc.scalar.activation(phi_sq[:], phi[:], ACT.Square, accum_out=phi_ss[:, 0:1]).then_inc(phi_done.sem, 1)
                act.wait_ge(phi_T.sem, 1)
                nc.scalar.copy(phiT[:], tp[:]).then_inc(phi_done.sem, 1)

            @block.gpsimd
            def _(pool):
                nc.gpsimd.memset(ident[:], 0.0).then_inc(pool_done.sem, 1)
                nc.gpsimd.memset(eps_ln[:], EPS_LN)
                nc.gpsimd.memset(eps[:], EPS)
                nc.gpsimd.memset(nhalf[:], -0.5).then_inc(pool_done.sem, 1)
                pool.wait_ge(pool_done.sem, 2)
                nc.gpsimd.affine_select(out=ident[:], in_=ident[:], compare_op=ALU.not_equal, fill=1.0, base=0,
                                        pattern=[[-1, P]], channel_multiplier=1).then_inc(pool_done.sem, 1)
                pool.wait_ge(phi_done.sem, 1)
                nc.gpsimd.tensor_scalar(phi_ss[:, 1:2], phi_ss[:, 0:1], EPS, 1.0, ALU.add, ALU.mult).then_inc(pool_done.sem, 1)
                pool.wait_ge(pool_done.sem, 4)
                nc.gpsimd.tensor_tensor(phi_ss[:, 2:3], phi_ss[:, 1:2], nhalf[:, 0:1], ALU.pow).then_inc(pool_done.sem, 1)

            @block.vector
            def _(dve):
                for s in stage:
                    nc.vector.memset(s[:, 0:DC * H * HP], 0.0).then_inc(zeroed.sem, 1)
                nc.vector.memset(bqk[:], 0.0).then_inc(zeroed.sem, 1)
                for i, (_, flat, parts) in enumerate(weights):
                    dve.wait_ge(hi_done.sem, i + 1)
                    nc.vector.tensor_tensor(parts[1], flat, parts[0].bitcast(F32), ALU.subtract).then_inc(lo_done.sem, 1)
                dve.wait_ge(small.sem, n_small[0])
                nc.vector.tensor_scalar(rows["gin"][:], rows["gin"][:], SCALE, None, ALU.mult)
                nc.vector.tensor_scalar(rows["g2"][:], rows["g2"][:], SCALE, None, ALU.mult)
                nc.vector.tensor_scalar(bqk[:, 0, :], bqk[:, 0, :], DH ** -0.5, None, ALU.mult)
                dve.wait_ge(pool_done.sem, 5)
                nc.vector.tensor_scalar(phi[:], phi[:], phi_ss[:, 2:3], SCALE, ALU.mult, ALU.mult).then_inc(lo_done.sem, 1)

            @block.tensor
            def _(pe):
                pe.wait_ge(pool_done.sem, 5)
                pe.wait_ge(lo_done.sem, len(weights) + 1)
                for c in range(DC):
                    mm = pe.transpose(tp[:, c, :], phi[:, c * P:(c + 1) * P], ident[:])
                mm.then_inc(phi_T.sem, 1)

    t_sb = lambda name, shape, dt=F32: sb(ctx, name, shape, dt)
    x_in = t_sb("x_in", [P, GT, D])
    adj_sb = t_sb("adj_sb", [P, GT, P])
    z = t_sb("z", [P, GT, D])
    zT = [t_sb("zT_hi", [P, DC, GN], F32R), t_sb("zT_lo", [P, DC, GN], F32R)]
    qT = t_sb("qT", [P, H // 2, GN])
    kT = t_sb("kT", [P, H // 2, GN])
    v_sb = t_sb("v_sb", [P, GT, D])
    s_sb = [t_sb(f"s_sb{t}", [P, 2, H // 2, P]) for t in range(GT)]
    pT = t_sb("pT", [P, 2, H // 2, P])
    ctx_sb = t_sb("ctx_sb", [P, D])
    cT = [t_sb("cT_hi", [P, DC, P], F32R), t_sb("cT_lo", [P, DC, P], F32R)]
    y = t_sb("y", [P, GT, D])
    yT = [t_sb("yT_hi", [P, DC, GN], F32R), t_sb("yT_lo", [P, DC, GN], F32R)]
    yb = t_sb("yb", [P, GT, D])
    h_tmp = [t_sb(f"h_tmp{i}", [P, 2, GN]) for i in range(2)]
    hT = [[t_sb(f"hT_hi{i}", [P, 2, GN], F32R), t_sb(f"hT_lo{i}", [P, 2, GN], F32R)] for i in range(3)]
    f_sb = t_sb("f_sb", [P, GT, D])
    x_res = t_sb("x_res", [P, GT, D])
    xn = t_sb("xn", [P, GT, D])
    xnT = t_sb("xnT", [P, DC, GN])
    logit = t_sb("logit", [P, GT, P])
    comb = t_sb("comb", [P, GT, P])
    disp = t_sb("disp", [P, GT, P])
    dcT = t_sb("dcT", [P, 2, GT, P])
    yn = t_sb("yn_sb", [P, GT, D])
    squares = {n: t_sb("squares_" + n, [P, GT, D], BF16) for n in ("r", "f")}
    counts = t_sb("counts", [P, GT])
    st = t_sb("st", [P, GT, 6])
    mv = t_sb("mv", [P, GT, 2])
    rstd = t_sb("rstd", [P, 2, GT])
    nmax = t_sb("nmax", [P, GT, H])
    ssum = t_sb("ssum", [P, GT, H])
    rsum = t_sb("rsum", [P, GT, H])
    rms = t_sb("rms", [P, GT, 3])
    fms = t_sb("fms", [P, GT, 3])
    st2 = t_sb("st2", [P, GT, 6])
    mv2 = t_sb("mv2", [P, GT, 2])
    rstd2 = t_sb("rstd2", [P, 2, GT])
    zms = t_sb("zms", [P, GT, 3])
    lmx = t_sb("lmx", [P, 2, GT])
    lsum = t_sb("lsum", [P, 2, GT])
    lrec = t_sb("lrec", [P, 2, GT])
    sms = t_sb("sms", [P, GT, 3])

    a_bank = [ps(ctx, f"a_bank{i}", [P, 512]) for i in range(3)]
    m_bank = [ps(ctx, f"m_bank{i}", [P, 2, GN]) for i in range(2)]
    f_bank = [ps(ctx, f"f_bank{i}", [P, 512]) for i in range(GT)]
    r_bank = ps(ctx, "r_bank", [P, 512])

    S = lambda name, n: sem(ctx, name, n)
    x_landed, adj_landed = S("x_landed", 16), S("adj_landed", 16)
    stats, meanvar, ve, rstd_ok, z_ok = S("stats", 2), S("meanvar", 2), S("ve", 1), S("rstd_ok", 1), S("z_ok", 2)
    zh, zl = S("zT_hi", 2), S("zT_lo", 2)
    q_ok, k_ok, v_ok = S("q", 4), S("k", 4), S("v", 2)
    sc_ok, mx_ok, p_ok, rs_ok = S("scores", 4), S("row_max", 2), S("exp", 16), S("recip", 2)
    pt_ok, ctx_ok, ch, cl = S("pT", 4), S("ctx", 2), S("cT_hi", 2), S("cT_lo", 2)
    r_ok, rb_ok, rss, rve, rrs = S("r", 2), S("r_bias", 2), S("r_ss", 2), S("r_ve", 2), S("r_rs", 2)
    ys, y_ok, yh, yl = S("y_scaled", 2), S("y", 2), S("yT_hi", 2), S("yT_lo", 2)
    a_full, zt_full = S("a_bank_full", 22), S("zT_full", 2)
    res_landed = S("x_res_landed", 16)
    yb_ok, h_ok, hh, hl = S("yb", 2), S("h", 12), S("hT_hi", 6), S("hT_lo", 6)
    f_ok, fss, fve, frs = S("f", 2), S("f_ss", 2), S("f_ve", 2), S("f_rs", 2)
    fs, xg, xo = S("f_scaled", 2), S("x_plus_gamma", 2), S("layer_out", 2)
    m_full, f_full, h_used = S("m_bank_full", 6), S("f_bank_full", 2), S("h_used", PAIRS - 1)
    res_stored = S("res_stored", 16)
    st2_ok, mv2_ok, ve2, rstd2_ok, z2_ok = S("stats2", 2), S("meanvar2", 2), S("ve2", 1), S("rstd2_ok", 1), S("z2", 2)
    zss, zve, zrs, xn_ok = S("z_ss", 2), S("z_ve", 1), S("z_rs", 1), S("xn", 2)
    xt_ok, lg_ok, lm_ok, le_ok, lr_ok, cb_ok = S("xnT", 2), S("logit", 1), S("l_max", 1), S("l_exp", 2), S("l_recip", 1), S("comb", 2)
    dm_ok, de_ok, dr_ok, tt_ok = S("d_max", 1), S("d_exp", 2), S("d_recip", 1), S("dcT", 1)
    sl_ok, sss, sve, srs, yn_ok = S("slots", 2), S("s_ss", 2), S("s_ve", 2), S("s_rs", 2), S("yn", 2)
    r_full = S("r_bank_full", 7)
    yn_stored, comb_stored = S("yn_stored", 16), S("comb_stored", 16)

    U_Q, U_K, U_V, U_S = (0, 1), (2, 3), (4, 5), ((6, 7), (8, 9))
    U_PT, U_CTX, U_CT, U_WO, U_YT = ((10, 11), (13, 14)), (12, 16), (15, 18), (17, 19), (20, 21)
    A_BANK = [a_bank[u % 3] for u in range(20)] + [a_bank[0], a_bank[2]]
    ZT_BANK = [a_bank[2], a_bank[1]]

    def tok(t):
        return slice(t * P, (t + 1) * P)

    with nc.Block() as block:
        @block.sync
        def _(sp):
            def body(a, m, r, n):
                if n is not None:
                    if past(n, 1):
                        sp.wait_ge(z_ok.sem, z_ok.at(n - 1, 2))
                    sp.dma_start(x_in[:], x_rows[bass.ds(n * GN, GN), :].rearrange("(t p) d -> p t d", p=P)
                                 ).then_inc(x_landed.sem, 16)
                if a is not None:
                    if past(a, 1):
                        sp.wait_ge(sc_ok.sem, sc_ok.at(a - 1, 4))
                    sp.dma_start(adj_sb[:], adj[bass.ds(a * GT, GT)].rearrange("t q k -> q t k")
                                 ).then_inc(adj_landed.sem, 16)
                if m is not None:
                    if past(m, 1):
                        sp.wait_ge(xo.sem, xo.at(m - 1, 2))
                    sp.dma_start(x_res[:], x_rows[bass.ds(m * GN, GN), :].rearrange("(t p) d -> p t d", p=P)
                                 ).then_inc(res_landed.sem, 16)
                if r is not None:
                    sp.wait_ge(tt_ok.sem, tt_ok.at(r, 1))
                    sp.dma_start(comb_dram[bass.ds(r * GT, GT)].rearrange("t p n -> p t n"), dcT[:, 1, :, :]
                                 ).then_inc(comb_stored.sem, 16)
                    sp.wait_ge(yn_ok.sem, yn_ok.at(r, 2))
                    sp.dma_start(yn_dram[bass.ds(r * GT, GT)].rearrange("t p d -> p t d"), yn[:]
                                 ).then_inc(yn_stored.sem, 16)
                if m is not None:
                    sp.wait_ge(xo.sem, xo.at(m, 2))
                    sp.dma_start(res_dram[bass.ds(m * GN, GN), :].rearrange("(t p) d -> p t d", p=P), f_sb[:]
                                 ).then_inc(res_stored.sem, 16)

            run(sp, body)
            sp.wait_ge(res_stored.sem, 16 * NG)
            sp.wait_ge(yn_stored.sem, 16 * NG)
            sp.wait_ge(comb_stored.sem, 16 * NG)

        @block.tensor
        def _(pe):
            def split_mm(dst, lhs, rhs, start=True, stop=True):
                n = len(lhs)
                for c in range(n):
                    (lh, ll), (rh, rl) = lhs[c], rhs[c]
                    for j, (left, right) in enumerate(((lh, rh), (lh, rl), (ll, rh))):
                        mm = pe.matmul(dst, left, right, start=start and c == 0 and j == 0,
                                       stop=stop and c == n - 1 and j == 2)
                return mm

            def zT_step(g, t):
                pe.wait_ge(z_ok.sem, z_ok.at(g, t + 1))
                if past(g, 1):
                    pe.wait_ge(r_ok.sem, r_ok.at(g - 1, t + 1))
                for c in range(DC):
                    mm = pe.transpose(ZT_BANK[t][:, tok(c)], z[:, t, tok(c)], ident[:])
                mm.then_inc(zt_full.sem, 1)

            def project(g, uses, w, n):
                if w is wq_s and n == 0:
                    pe.wait_ge(zl.sem, zl.at(g, 2))
                    if past(g, 1):
                        pe.wait_ge(yl.sem, yl.at(g - 1, 1))
                if w is wk_s and n == 0:
                    if past(g, 1):
                        pe.wait_ge(yl.sem, yl.at(g - 1, 2))
                if w is wk_s and n == 1:
                    pe.wait_ge(q_ok.sem, q_ok.at(g, 2))
                bank = A_BANK[uses[n]]
                for half in range(2):
                    m = 2 * n + half
                    mm = split_mm(bank[:, half * GN:(half + 1) * GN],
                                  [[w[s][:, c, tok(m)] for s in range(2)] for c in range(DC)],
                                  [[zT[s][:, c, :] for s in range(2)] for c in range(DC)])
                mm.then_inc(a_full.sem, 1)

            def values(g, t):
                if t == 0:
                    pe.wait_ge(q_ok.sem, q_ok.at(g, 4))
                else:
                    pe.wait_ge(k_ok.sem, k_ok.at(g, 2))
                bank = A_BANK[U_V[t]]
                split_mm(bank[:, 0:D], [[zT[s][:, c, tok(t)] for s in range(2)] for c in range(DC)],
                         [[wv_s[s][:, c, :] for s in range(2)] for c in range(DC)]).then_inc(a_full.sem, 1)

            def scores(g, t):
                pe.wait_ge(q_ok.sem, q_ok.at(g, 4))
                pe.wait_ge(k_ok.sem, k_ok.at(g, 4))
                for par in range(2):
                    held, k = ((k_ok, 4), (v_ok, 1), (v_ok, 2), (sc_ok, 1))[2 * t + par]
                    pe.wait_ge(held.sem, held.at(g, k))
                    bank = A_BANK[U_S[t][par]]
                    r = slice(HP * par, HP * par + DH)
                    for m in range(H // 2):
                        mm = pe.matmul(bank[:, tok(m)], qT[r, m, tok(t)], kT[r, m, tok(t)], start=True, stop=True)
                    mm.then_inc(a_full.sem, 1)

            def prob_T(g, t):
                for par in range(2):
                    pe.wait_ge(p_ok.sem, p_ok.at(g, 8 * t + 4 * (par + 1)))
                    held, k = ((sc_ok, 2), (sc_ok, 3), (pt_ok, 1), (pt_ok, 2))[2 * t + par]
                    pe.wait_ge(held.sem, held.at(g, k))
                    bank = A_BANK[U_PT[t][par]]
                    for m in range(H // 2):
                        mm = pe.transpose(bank[:, tok(m)], s_sb[t][:, par, m, :], ident[:])
                    mm.then_inc(a_full.sem, 1)

            def context(g, t):
                pe.wait_ge(v_ok.sem, v_ok.at(g, t + 1))
                held, k = ((sc_ok, 4), (pt_ok, 3))[t]
                pe.wait_ge(held.sem, held.at(g, k))
                bank = A_BANK[U_CTX[t]]
                for par in range(2):
                    pe.wait_ge(pt_ok.sem, pt_ok.at(g, 2 * t + par + 1))
                    for m in range(H // 2):
                        h = 2 * m + par
                        mm = pe.matmul(bank[:, h * DH:(h + 1) * DH], pT[:, par, m, :],
                                       v_sb[:, t, h * DH:(h + 1) * DH], start=True, stop=True)
                mm.then_inc(a_full.sem, 1)

            def context_T(g, t):
                pe.wait_ge(ctx_ok.sem, ctx_ok.at(g, t + 1))
                if t:
                    pe.wait_ge(cl.sem, cl.at(g, 1))
                bank = A_BANK[U_CT[t]]
                for c in range(DC):
                    mm = pe.transpose(bank[:, tok(c)], ctx_sb[:, tok(c)], ident[:])
                mm.then_inc(a_full.sem, 1)

            def project_out(g, t):
                pe.wait_ge(cl.sem, cl.at(g, t + 1))
                held, k = ((pt_ok, 4), (ctx_ok, 2))[t]
                pe.wait_ge(held.sem, held.at(g, k))
                bank = A_BANK[U_WO[t]]
                split_mm(bank[:, 0:D], [[cT[s][:, c, :] for s in range(2)] for c in range(DC)],
                         [[wo_s[s][:, c, :] for s in range(2)] for c in range(DC)]).then_inc(a_full.sem, 1)

            def yT_step(g, t):
                pe.wait_ge(y_ok.sem, y_ok.at(g, t + 1))
                if t == 0:
                    pe.wait_ge(cl.sem, cl.at(g, 2))
                elif not (isinstance(g, int) and g == NG - 1):
                    pe.wait_ge(zl.sem, zl.at(g + 1, 1))
                bank = A_BANK[U_YT[t]]
                for c in range(DC):
                    mm = pe.transpose(bank[:, tok(c)], y[:, t, tok(c)], ident[:])
                mm.then_inc(a_full.sem, 1)

            def up(g, i):
                pe.wait_ge(yl.sem, yl.at(g, 2))
                if i >= 2:
                    pe.wait_ge(h_ok.sem, h_ok.at(g, 2 * (i - 1)))
                else:
                    if past(g, 1):
                        pe.wait_ge(h_ok.sem, h_ok.at(g - 1, 12 - 2 * (1 - i)))
                for half in range(2):
                    m = 2 * i + half
                    mm = split_mm(m_bank[i % 2][:, half, :],
                                  [[w1_s[s][:, c, tok(m)] for s in range(2)] for c in range(DC)],
                                  [[yT[s][:, c, :] for s in range(2)] for c in range(DC)])
                mm.then_inc(m_full.sem, 1)

            def down(g, i):
                pe.wait_ge(hh.sem, hh.at(g, i + 1))
                pe.wait_ge(hl.sem, hl.at(g, i + 1))
                for t in range(GT):
                    if i == 0:
                        if past(g, 1):
                            pe.wait_ge(f_ok.sem, f_ok.at(g - 1, t + 1))
                    mm = split_mm(f_bank[t][:, 0:D],
                                  [[hT[i % 3][s][:, half, tok(t)] for s in range(2)] for half in range(2)],
                                  [[w2_s[s][:, 2 * i + half, :] for s in range(2)] for half in range(2)],
                                  start=i == 0, stop=i == PAIRS - 1)
                    if i == PAIRS - 1:
                        mm.then_inc(f_full.sem, 1)
                if i < PAIRS - 1:
                    mm.then_inc(h_used.sem, 1)

            def xnT_step(g, t):
                pe.wait_ge(xn_ok.sem, xn_ok.at(g, t + 1))
                if t == 0:
                    if past(g, 1):
                        pe.wait_ge(sl_ok.sem, sl_ok.at(g - 1, 2))
                else:
                    pe.wait_ge(xt_ok.sem, xt_ok.at(g, 1))
                for c in range(DC):
                    mm = pe.transpose(r_bank[:, tok(c)], xn[:, t, tok(c)], ident[:])
                mm.then_inc(r_full.sem, 1)

            def logits(g):
                pe.wait_ge(xt_ok.sem, xt_ok.at(g, 2))
                for t in range(GT):
                    for c in range(DC):
                        mm = pe.matmul(r_bank[:, tok(t)], xnT[:, c, tok(t)], phiT[:, c, :], start=c == 0, stop=c == DC - 1)
                mm.then_inc(r_full.sem, 1)

            def logits_T(g):
                pe.wait_ge(lg_ok.sem, lg_ok.at(g, 1))
                for t in range(GT):
                    mm = pe.transpose(r_bank[:, tok(t)], logit[:, t, :], ident[:])
                mm.then_inc(r_full.sem, 1)

            def weights_T(g):
                pe.wait_ge(de_ok.sem, de_ok.at(g, 2))
                pe.wait_ge(cb_ok.sem, cb_ok.at(g, 2))
                for n, w in enumerate((disp, comb)):
                    for t in range(GT):
                        mm = pe.transpose(r_bank[:, tok(2 * n + t)], w[:, t, :], ident[:])
                mm.then_inc(r_full.sem, 1)

            def slots(g, t):
                if t == 0:
                    pe.wait_ge(tt_ok.sem, tt_ok.at(g, 1))
                else:
                    pe.wait_ge(sl_ok.sem, sl_ok.at(g, 1))
                pe.matmul(r_bank[:, 0:D], dcT[:, 0, t, :], xn[:, t, :], start=True, stop=True).then_inc(r_full.sem, 1)

            def body(a, m, r, n):
                A, M, R, N = (v is not None for v in (a, m, r, n))
                if A: project(a, U_Q, wq_s, 0); project(a, U_Q, wq_s, 1)
                if M: up(m, 0)
                if A: project(a, U_K, wk_s, 0); project(a, U_K, wk_s, 1)
                if M: up(m, 1)
                if A: values(a, 0); values(a, 1); scores(a, 0)
                if R: xnT_step(r, 0)
                if A: scores(a, 1)
                if R: xnT_step(r, 1)
                if M: down(m, 0)
                if A: prob_T(a, 0)
                if R: logits(r)
                if M: down(m, 1)
                if A: context(a, 0); prob_T(a, 1)
                if R: logits_T(r)
                if M: up(m, 2)
                if A: context_T(a, 0); context(a, 1)
                if M: up(m, 3)
                if A: project_out(a, 0); context_T(a, 1)
                if R: weights_T(r)
                if M: down(m, 2)
                if A: project_out(a, 1)
                if M: up(m, 4); down(m, 3)
                if N: zT_step(n, 0)
                if R: slots(r, 0)
                if M: up(m, 5)
                if A: yT_step(a, 0)
                if N: zT_step(n, 1)
                if M: down(m, 4)
                if A: yT_step(a, 1)
                if R: slots(r, 1)
                if M: down(m, 5)

            run(pe, body)

        @block.scalar
        def _(act):
            def hi_zT(g, t):
                act.wait_ge(zt_full.sem, zt_full.at(g, t + 1))
                if past(g, 1):
                    act.wait_ge(a_full.sem, a_full.at(g - 1, U_V[1] + 1))
                nc.scalar.copy(zT[0][:, :, tok(t)], ZT_BANK[t][:, 0:D].rearrange("p (c n) -> p c n", c=DC)).then_inc(zh.sem, 1)

            def hi_yT(g, t):
                if past(g, 1):
                    act.wait_ge(m_full.sem, m_full.at(g - 1, PAIRS))
                hi_T(g, t, U_YT, yT[0][:, :, tok(t)], yh)

            def hi_T(g, t, use, dst, sig):
                act.wait_ge(a_full.sem, a_full.at(g, use[t] + 1))
                nc.scalar.copy(dst, A_BANK[use[t]][:, 0:D].rearrange("p (c n) -> p c n", c=DC)).then_inc(sig.sem, 1)

            def query(g, half):
                for m in (2 * half, 2 * half + 1):
                    if m % 2 == 0:
                        act.wait_ge(a_full.sem, a_full.at(g, U_Q[m // 2] + 1))
                    bank = A_BANK[U_Q[m // 2]]
                    nc.scalar.activation(qT[:, m, :], bank[:, (m % 2) * GN:(m % 2 + 1) * GN], ACT.Identity,
                                         bias=bqk[:, 0, m:m + 1], scale=DH ** -0.5).then_inc(q_ok.sem, 1)

            def exps(g, t):
                act.wait_ge(mx_ok.sem, mx_ok.at(g, t + 1))
                for par in range(2):
                    for m in range(H // 2):
                        h = par * (H // 2) + m
                        s = s_sb[t][:, par, m, :]
                        nc.scalar.activation(s, s, ACT.Exp, bias=nmax[:, t, h:h + 1],
                                             accum_out=ssum[:, t, h:h + 1]).then_inc(p_ok.sem, 1)

            def prob_T(g, t):
                act.wait_ge(a_full.sem, a_full.at(g, U_PT[t][0] + 1))
                if t:
                    act.wait_ge(ctx_ok.sem, ctx_ok.at(g, t))
                else:
                    if past(g, 1):
                        act.wait_ge(ctx_ok.sem, ctx_ok.at(g - 1, 2))
                for par in range(2):
                    act.wait_ge(a_full.sem, a_full.at(g, U_PT[t][par] + 1))
                    nc.scalar.copy(pT[:, par, :, :], A_BANK[U_PT[t][par]][:].rearrange("p (m n) -> p m n", n=P)
                                   ).then_inc(pt_ok.sem, 1)

            def square(g, t, name, sig_in, src, dst, sig, scale=1.0):
                act.wait_ge(sig_in.sem, sig_in.at(g, t + 1))
                out, rows_in = squares[name][:, t, :] if name in squares else None, src[:, t, :]
                if name == "z":
                    out, rows_in = xnT[:, :, tok(t)], rows_in.rearrange("p (c n) -> p c n", c=DC)
                if name == "s":
                    out = (comb, disp)[t][:].rearrange("p t n -> p (t n)").bitcast(BF16)[:, 0:D]
                nc.scalar.activation(out, rows_in, ACT.Square, scale=scale, accum_out=dst[:, t, 0:1]).then_inc(sig.sem, 1)

            def silu(g, i):
                act.wait_ge(m_full.sem, m_full.at(g, i + 1))
                if i >= 2:
                    act.wait_ge(hl.sem, hl.at(g, i - 1))
                else:
                    if past(g, 1):
                        act.wait_ge(hl.sem, hl.at(g - 1, PAIRS - 1 + i))
                for half in range(2):
                    nc.scalar.activation(h_tmp[i % 2][:, half, :], m_bank[i % 2][:, half, :], ACT.Silu,
                                         bias=b1c[:, 2 * i + half:2 * i + half + 1]).then_inc(h_ok.sem, 1)

            def xnT_step(g, t):
                act.wait_ge(r_full.sem, r_full.at(g, t + 1))
                nc.scalar.copy(xnT[:, :, tok(t)], r_bank[:, 0:D].rearrange("p (c n) -> p c n", c=DC)).then_inc(xt_ok.sem, 1)

            def logits(g):
                act.wait_ge(r_full.sem, r_full.at(g, 3))
                nc.scalar.copy(logit[:], r_bank[:, 0:GN].rearrange("p (t n) -> p t n", t=GT)).then_inc(lg_ok.sem, 1)

            def comb_exp(g):
                act.wait_ge(lm_ok.sem, lm_ok.at(g, 1))
                for t in range(GT):
                    nc.scalar.activation(comb[:, t, :], logit[:, t, :], ACT.Exp, bias=lmx[:, 0, t:t + 1],
                                         accum_out=lsum[:, 0, t:t + 1]).then_inc(le_ok.sem, 1)

            def disp_exp(g):
                act.wait_ge(dm_ok.sem, dm_ok.at(g, 1))
                for t in range(GT):
                    nc.scalar.activation(disp[:, t, :], r_bank[:, tok(t)], ACT.Exp, bias=lmx[:, 1, t:t + 1],
                                         accum_out=lsum[:, 1, t:t + 1]).then_inc(de_ok.sem, 1)

            def weights_T(g):
                act.wait_ge(r_full.sem, r_full.at(g, 5))
                if past(g, 1):
                    act.wait_ge(comb_stored.sem, comb_stored.at(g - 1, 16))
                nc.scalar.copy(dcT[:].rearrange("p n t k -> p (n t k)"), r_bank[:]).then_inc(tt_ok.sem, 1)

            def body(a, m, r, n):
                A, M, R, N = (v is not None for v in (a, m, r, n))
                if A: query(a, 0); query(a, 1)
                if M: silu(m, 0)
                if R: square(r, 0, "z", z2_ok, xn, zms, zss); square(r, 1, "z", z2_ok, xn, zms, zss)
                if M: silu(m, 1)
                if R: xnT_step(r, 0)
                if A: exps(a, 0)
                if R: xnT_step(r, 1)
                if A: exps(a, 1); prob_T(a, 0)
                if R: logits(r); comb_exp(r)
                if A: prob_T(a, 1)
                if R: disp_exp(r)
                if A: hi_T(a, 0, U_CT, cT[0][:], ch)
                if M: silu(m, 2); silu(m, 3)
                if A: hi_T(a, 1, U_CT, cT[0][:], ch)
                if R: weights_T(r)
                if A: square(a, 0, "r", rb_ok, y, rms, rss, D ** -0.5)
                if M: silu(m, 4)
                if A: square(a, 1, "r", rb_ok, y, rms, rss, D ** -0.5)
                if N: hi_zT(n, 0)
                if R: square(r, 0, "s", sl_ok, yn, sms, sss)
                if M: silu(m, 5)
                if A: hi_yT(a, 0)
                if N: hi_zT(n, 1)
                if A: hi_yT(a, 1)
                if R: square(r, 1, "s", sl_ok, yn, sms, sss)
                if M: square(m, 0, "f", f_ok, f_sb, fms, fss, D ** -0.5); square(m, 1, "f", f_ok, f_sb, fms, fss, D ** -0.5)

            run(act, body)

        @block.vector
        def _(dve):
            def norm_stats(g, landed, k, src, s, v, sig_s, sig_v):
                for t in range(GT):
                    if t == 0 or k < 16:
                        dve.wait_ge(landed.sem, landed.at(g, k + t if k < 16 else k))
                    nc.vector.bn_stats(s[:, t, :], src[:, t, :]).then_inc(sig_s.sem, 1)
                dve.wait_ge(sig_s.sem, sig_s.at(g, GT))
                nc.vector.tensor_copy(counts[:], s[:, :, 0])
                for t in range(GT):
                    nc.vector.bn_aggr(v[:, t, :], s[:, t, :]).then_inc(sig_v.sem, 1)

            def centre(g, t, src, dst, v, r, sig_r, sig):
                dve.wait_ge(sig_r.sem, sig_r.at(g, 1))
                nc.vector.tensor_scalar(dst[:, t, :], src[:, t, :], v[:, t, 0:1], r[:, 1, t:t + 1],
                                        ALU.subtract, ALU.mult).then_inc(sig.sem, 1)

            def z_step(g, t):
                if past(g, 1):
                    dve.wait_ge(r_ok.sem, r_ok.at(g - 1, t + 1))
                dve.wait_ge(x_landed.sem, x_landed.at(g, 16))
                centre(g, t, x_in, z, mv, rstd, rstd_ok, z_ok)

            def lo_zT(g, t):
                dve.wait_ge(zh.sem, zh.at(g, t + 1))
                nc.vector.tensor_tensor(zT[1][:, :, tok(t)], ZT_BANK[t][:, 0:D].rearrange("p (c n) -> p c n", c=DC),
                                        zT[0][:, :, tok(t)].bitcast(F32), ALU.subtract).then_inc(zl.sem, 1)

            def lo_T(g, t, use, hi, lo, sig_hi, sig):
                dve.wait_ge(sig_hi.sem, sig_hi.at(g, t + 1))
                nc.vector.tensor_tensor(lo, A_BANK[use[t]][:, 0:D].rearrange("p (c n) -> p c n", c=DC),
                                        hi.bitcast(F32), ALU.subtract).then_inc(sig.sem, 1)

            def key(g, half):
                for m in (2 * half, 2 * half + 1):
                    if m % 2 == 0:
                        dve.wait_ge(a_full.sem, a_full.at(g, U_K[m // 2] + 1))
                    bank = A_BANK[U_K[m // 2]]
                    nc.vector.tensor_scalar(kT[:, m, :], bank[:, (m % 2) * GN:(m % 2 + 1) * GN],
                                            bqk[:, 1, m:m + 1], None, ALU.add).then_inc(k_ok.sem, 1)

            def values(g, t):
                dve.wait_ge(a_full.sem, a_full.at(g, U_V[t] + 1))
                nc.vector.tensor_tensor(v_sb[:, t, :], A_BANK[U_V[t]][:, 0:D], rows["bv"][:], ALU.add).then_inc(v_ok.sem, 1)

            def scores(g, t):
                if t == 0:
                    dve.wait_ge(adj_landed.sem, adj_landed.at(g, 16))
                for par in range(2):
                    dve.wait_ge(a_full.sem, a_full.at(g, U_S[t][par] + 1))
                    nc.vector.tensor_tensor(s_sb[t][:, par, :, :], A_BANK[U_S[t][par]][:].rearrange("p (m n) -> p m n", n=P),
                                            adj_sb[:, t, :].unsqueeze(1).broadcast_to([P, H // 2, P]), ALU.add).then_inc(sc_ok.sem, 1)
                dve.wait_ge(sc_ok.sem, sc_ok.at(g, 2 * t + 2))
                nc.vector.tensor_reduce(nmax[:, t, :], s_sb[t][:].rearrange("p a m n -> p (a m) n"), X_AXIS, ALU.max,
                                        negate=True).then_inc(mx_ok.sem, 1)

            def recips(g, t):
                dve.wait_ge(p_ok.sem, p_ok.at(g, 8 * (t + 1)))
                nc.vector.reciprocal(rsum[:, t, :], ssum[:, t, :]).then_inc(rs_ok.sem, 1)

            def context(g, t):
                dve.wait_ge(a_full.sem, a_full.at(g, U_CTX[t] + 1))
                dve.wait_ge(rs_ok.sem, rs_ok.at(g, t + 1))
                if t:
                    dve.wait_ge(a_full.sem, a_full.at(g, U_CT[0] + 1))
                else:
                    if past(g, 1):
                        dve.wait_ge(a_full.sem, a_full.at(g - 1, U_CT[1] + 1))
                nc.vector.tensor_tensor(
                    ctx_sb[:].rearrange("p (m a e) -> p m a e", a=2, e=DH),
                    A_BANK[U_CTX[t]][:, 0:D].rearrange("p (m a e) -> p m a e", a=2, e=DH),
                    rsum[:, t, :].rearrange("p (a m) -> p m a", a=2).unsqueeze(3).broadcast_to([P, H // 2, 2, DH]),
                    ALU.mult).then_inc(ctx_ok.sem, 1)

            def residual(g, t):
                dve.wait_ge(a_full.sem, a_full.at(g, U_WO[t] + 1))
                if past(g, 1):
                    dve.wait_ge(yb_ok.sem, yb_ok.at(g - 1, t + 1))
                nc.vector.tensor_tensor(y[:, t, :], A_BANK[U_WO[t]][:, 0:D], z[:, t, :], ALU.add).then_inc(r_ok.sem, 1)

            def y_scale(g, t):
                dve.wait_ge(rrs.sem, rrs.at(g, t + 1))
                dve.wait_ge(rb_ok.sem, rb_ok.at(g, t + 1))
                nc.vector.scalar_tensor_tensor(out=y[:, t, :], in0=y[:, t, :], scalar=rms[:, t, 2:3],
                                               in1=rows["alpha1"][:], op0=ALU.mult, op1=ALU.mult).then_inc(ys.sem, 1)

            def h_hi(g, i):
                dve.wait_ge(h_ok.sem, h_ok.at(g, 2 * i + 2))
                if i >= 3:
                    dve.wait_ge(h_used.sem, h_used.at(g, i - 2))
                else:
                    if past(g, 1):
                        dve.wait_ge(f_full.sem, f_full.at(g - 1, 2))
                nc.vector.tensor_copy(hT[i % 3][0][:], h_tmp[i % 2][:]).then_inc(hh.sem, 1)

            def f_sum(g, t):
                dve.wait_ge(f_full.sem, f_full.at(g, t + 1))
                dve.wait_ge(yb_ok.sem, yb_ok.at(g, t + 1))
                if past(g, 1):
                    dve.wait_ge(res_stored.sem, res_stored.at(g - 1, 16))
                nc.vector.tensor_tensor(f_sb[:, t, :], f_bank[t][:, 0:D], yb[:, t, :], ALU.add).then_inc(f_ok.sem, 1)

            def f_scale(g, t):
                dve.wait_ge(frs.sem, frs.at(g, t + 1))
                dve.wait_ge(f_ok.sem, f_ok.at(g, t + 1))
                nc.vector.scalar_tensor_tensor(out=f_sb[:, t, :], in0=f_sb[:, t, :], scalar=fms[:, t, 2:3],
                                               in1=rows["alpha2"][:], op0=ALU.mult, op1=ALU.mult).then_inc(fs.sem, 1)
                dve.wait_ge(fs.sem, fs.at(g, t + 1))
                dve.wait_ge(xg.sem, xg.at(g, t + 1))
                nc.vector.tensor_tensor(f_sb[:, t, :], f_sb[:, t, :], x_res[:, t, :], ALU.add).then_inc(xo.sem, 1)

            def r_scale(g):
                dve.wait_ge(zrs.sem, zrs.at(g, 1))
                dve.wait_ge(z2_ok.sem, z2_ok.at(g, 2))
                for t in range(GT):
                    nc.vector.scalar_tensor_tensor(out=xn[:, t, :], in0=xn[:, t, :], scalar=zms[:, t, 2:3],
                                                   in1=rows["gin"][:], op0=ALU.mult, op1=ALU.mult).then_inc(xn_ok.sem, 1)

            def row_max(g):
                dve.wait_ge(lg_ok.sem, lg_ok.at(g, 1))
                nc.vector.tensor_reduce(lmx[:, 0, :], logit[:], X_AXIS, ALU.max, negate=True).then_inc(lm_ok.sem, 1)

            def comb_norm(g):
                dve.wait_ge(le_ok.sem, le_ok.at(g, 2))
                nc.vector.reciprocal(lrec[:, 0, :], lsum[:, 0, :]).then_inc(lr_ok.sem, 1)
                dve.wait_ge(lr_ok.sem, lr_ok.at(g, 1))
                for t in range(GT):
                    nc.vector.tensor_scalar(comb[:, t, :], comb[:, t, :], lrec[:, 0, t:t + 1], None, ALU.mult).then_inc(cb_ok.sem, 1)

            def slot_max(g):
                dve.wait_ge(r_full.sem, r_full.at(g, 4))
                nc.vector.tensor_reduce(lmx[:, 1, :], r_bank[:, 0:GN].rearrange("p (t n) -> p t n", t=GT), X_AXIS,
                                        ALU.max, negate=True).then_inc(dm_ok.sem, 1)

            def disp_recip(g):
                dve.wait_ge(de_ok.sem, de_ok.at(g, 2))
                nc.vector.reciprocal(lrec[:, 1, :], lsum[:, 1, :]).then_inc(dr_ok.sem, 1)

            def slot_rows(g, t):
                dve.wait_ge(r_full.sem, r_full.at(g, 6 + t))
                dve.wait_ge(dr_ok.sem, dr_ok.at(g, 1))
                if past(g, 1):
                    dve.wait_ge(yn_stored.sem, yn_stored.at(g - 1, 16))
                nc.vector.tensor_scalar(yn[:, t, :], r_bank[:, 0:D], lrec[:, 1, t:t + 1], None, ALU.mult).then_inc(sl_ok.sem, 1)

            def yn_scale(g, t):
                dve.wait_ge(srs.sem, srs.at(g, t + 1))
                dve.wait_ge(sl_ok.sem, sl_ok.at(g, t + 1))
                nc.vector.scalar_tensor_tensor(out=yn[:, t, :], in0=yn[:, t, :], scalar=sms[:, t, 2:3],
                                               in1=rows["g2"][:], op0=ALU.mult, op1=ALU.mult).then_inc(yn_ok.sem, 1)

            def body(a, m, r, n):
                A, M, R, N = (v is not None for v in (a, m, r, n))
                if R:
                    norm_stats(r, xo, 1, f_sb, st2, mv2, st2_ok, mv2_ok)
                    if past(r, 1):
                        dve.wait_ge(r_full.sem, r_full.at(r - 1, 7))
                    for t in range(GT): centre(r, t, f_sb, xn, mv2, rstd2, rstd2_ok, z2_ok)
                if A: key(a, 0)
                if M: h_hi(m, 0)
                if A: key(a, 1)
                if R: r_scale(r)
                if M: h_hi(m, 1)
                if A: values(a, 0); values(a, 1); scores(a, 0); scores(a, 1); recips(a, 0)
                if N: norm_stats(n, x_landed, 16, x_in, st, mv, stats, meanvar)
                if R: row_max(r)
                if A: context(a, 0); recips(a, 1)
                if R: slot_max(r); comb_norm(r)
                if A: lo_T(a, 0, U_CT, cT[0][:], cT[1][:], ch, cl)
                if R: disp_recip(r)
                if M: h_hi(m, 2)
                if A: context(a, 1)
                if M: h_hi(m, 3)
                if A: residual(a, 0); lo_T(a, 1, U_CT, cT[0][:], cT[1][:], ch, cl)
                if N: z_step(n, 0)
                if A: y_scale(a, 0); residual(a, 1)
                if N: z_step(n, 1)
                if M: h_hi(m, 4)
                if A: y_scale(a, 1)
                if N: lo_zT(n, 0)
                if R: slot_rows(r, 0)
                if M: h_hi(m, 5)
                if A: lo_T(a, 0, U_YT, yT[0][:, :, tok(0)], yT[1][:, :, tok(0)], yh, yl)
                if N: lo_zT(n, 1)
                if R: yn_scale(r, 0)
                if A: lo_T(a, 1, U_YT, yT[0][:, :, tok(1)], yT[1][:, :, tok(1)], yh, yl)
                if R: slot_rows(r, 1)
                if M: f_sum(m, 0); f_sum(m, 1)
                if R: yn_scale(r, 1)
                if M: f_scale(m, 0); f_scale(m, 1)

            run(dve, body)

        @block.gpsimd
        def _(pool):
            def power(g, k, sig_in, src, small, mid, dst, sig_mid, sig_out, kk):
                n = src.shape[1]
                pool.wait_ge(sig_in.sem, sig_in.at(g, k))
                nc.gpsimd.tensor_tensor(mid, src, small[:, 0:n], ALU.add).then_inc(sig_mid.sem, 1)
                pool.wait_ge(sig_mid.sem, sig_mid.at(g, kk))
                nc.gpsimd.tensor_tensor(dst, mid, nhalf[:, 0:n], ALU.pow).then_inc(sig_out.sem, 1)

            def h_lo(g, i):
                pool.wait_ge(hh.sem, hh.at(g, i + 1))
                nc.gpsimd.tensor_tensor(hT[i % 3][1][:], h_tmp[i % 2][:], hT[i % 3][0][:].bitcast(F32),
                                        ALU.subtract).then_inc(hl.sem, 1)

            def r_bias(g, t):
                pool.wait_ge(r_ok.sem, r_ok.at(g, t + 1))
                nc.gpsimd.tensor_tensor(y[:, t, :], y[:, t, :], rows["bo"][:], ALU.add).then_inc(rb_ok.sem, 1)

            def y_shift(g, t):
                pool.wait_ge(ys.sem, ys.at(g, t + 1))
                nc.gpsimd.tensor_tensor(y[:, t, :], y[:, t, :], rows["gamma1"][:], ALU.add).then_inc(y_ok.sem, 1)

            def body(a, m, r, n):
                A, M, R, N = (v is not None for v in (a, m, r, n))
                if R: power(r, 2, mv2_ok, mv2[:, :, 1], eps_ln, rstd2[:, 0, :], rstd2[:, 1, :], ve2, rstd2_ok, 1)
                if M:
                    for t in range(GT):
                        pool.wait_ge(y_ok.sem, y_ok.at(m, t + 1))
                        if past(m, 1):
                            pool.wait_ge(f_ok.sem, f_ok.at(m - 1, t + 1))
                        nc.gpsimd.tensor_tensor(yb[:, t, :], y[:, t, :], rows["b2"][:], ALU.add).then_inc(yb_ok.sem, 1)
                if R: power(r, 2, zss, zms[:, :, 0], eps, zms[:, :, 1], zms[:, :, 2], zve, zrs, 1)
                if M:
                    h_lo(m, 0); h_lo(m, 1)
                    pool.wait_ge(res_landed.sem, res_landed.at(m, 16))
                    for t in range(GT):
                        nc.gpsimd.tensor_tensor(x_res[:, t, :], x_res[:, t, :], rows["gamma2"][:], ALU.add).then_inc(xg.sem, 1)
                if N: power(n, 2, meanvar, mv[:, :, 1], eps_ln, rstd[:, 0, :], rstd[:, 1, :], ve, rstd_ok, 1)
                if M: h_lo(m, 2); h_lo(m, 3)
                if A:
                    r_bias(a, 0)
                    power(a, 1, rss, rms[:, 0, 0:1], eps, rms[:, 0, 1:2], rms[:, 0, 2:3], rve, rrs, 1)
                    y_shift(a, 0)
                    r_bias(a, 1)
                    power(a, 2, rss, rms[:, 1, 0:1], eps, rms[:, 1, 1:2], rms[:, 1, 2:3], rve, rrs, 2)
                if M: h_lo(m, 4)
                if A: y_shift(a, 1)
                if R: power(r, 1, sss, sms[:, 0, 0:1], eps, sms[:, 0, 1:2], sms[:, 0, 2:3], sve, srs, 1)
                if M: h_lo(m, 5)
                if R: power(r, 2, sss, sms[:, 1, 0:1], eps, sms[:, 1, 1:2], sms[:, 1, 2:3], sve, srs, 2)
                if M:
                    for t in range(GT):
                        power(m, t + 1, fss, fms[:, t, 0:1], eps, fms[:, t, 1:2], fms[:, t, 2:3], fve, frs, t + 1)

            run(pool, body)


def run(eng, body):
    body(None, None, None, 0)
    body(0, None, None, 1)
    body(1, 0, None, 2)
    with eng.Fori(2, NG - 1) as g:
        body(g, g - 1, g - 2, g + 1)
    body(NG - 1, NG - 2, NG - 3, None)
    body(None, NG - 1, NG - 2, None)
    body(None, None, NG - 1, None)


def routes(nc, ctx, sb, ps, sem, ident, nhalf, eps, w_slot2, yn_dram, se_dram):
    HB = 2
    HC = E2 * D // 2
    raw = sb(ctx, "ws_raw", [P, DC, E2 * D])
    ws = [sb(ctx, "ws_hi", [P, DC, E2 * D], F32R), sb(ctx, "ws_lo", [P, DC, E2 * D], F32R)]
    yk = [sb(ctx, f"yk{i}", [P, NS, D]) for i in range(HB)]
    mean = [sb(ctx, f"mean{i}", [P, D]) for i in range(HB)]
    mT = [sb(ctx, "mT_hi", [P, DC, HB, P], F32R), sb(ctx, "mT_lo", [P, DC, HB, P], F32R)]
    se = [sb(ctx, f"se{i}", [P, E2, D]) for i in range(HB)]
    squares = sb(ctx, "se_squares", [P, HB, E2, D], mybir.dt.bfloat16)
    ms = sb(ctx, "r_ms", [P, HB, 3, E2])
    t_bank = [ps(ctx, f"rt_bank{i}", [P, DC, P]) for i in range(HB)]
    bank = [ps(ctx, f"rs_bank{i}", [P, 512]) for i in range(4)]
    w_landed = sem(ctx, "ws_landed", 16)
    y_landed = [sem(ctx, f"yk_landed{i}", 16) for i in range(HB)]
    w_hi, w_lo = sem(ctx, "ws_hi", 2), sem(ctx, "ws_lo", 2)
    added, t_full, m_hi, m_lo = sem(ctx, "added", 6), sem(ctx, "mT_full", 2), sem(ctx, "mT_hi", 2), sem(ctx, "mT_lo", 2)
    full, sq, ve, rs, scaled = (sem(ctx, n, c) for n, c in (("se_full", 8), ("se_ss", 8), ("se_ve", 2), ("se_rs", 2), ("se_ok", 8)))
    stored = [sem(ctx, f"se_stored{i}", 16) for i in range(HB)]
    yn_by_k = yn_dram.rearrange("b (k m n) d -> b k m (n d)", k=E1, n=NS)

    def loop(eng, body):
        body(0)
        with eng.Fori(1, E1) as k:
            body(k)

    with nc.Block() as block:
        @block.sync
        def _(sp):
            def body(k):
                if past(k, 1):
                    sp.wait_ge(w_lo.sem, w_lo.at(k - 1, 2))
                sp.dma_start(raw[:], w_slot2[bass.ds(k, 1)].rearrange("o (c p) f -> p (o c) f", p=P)).then_inc(w_landed.sem, 16)
                for i in range(HB):
                    if past(k, 1):
                        sp.wait_ge(added.sem, added.at(k - 1, 3 * (i + 1)))
                    sp.dma_start(yk[i][:].rearrange("p n d -> p (n d)"),
                                 yn_by_k[i * NB // HB:(i + 1) * NB // HB, bass.ds(k, 1)].rearrange("b o m q -> (b o) m q")
                                 ).then_inc(y_landed[i].sem, 16)
            loop(sp, body)

        @block.tensor
        def _(pe):
            def body(k):
                for i in range(HB):
                    pe.wait_ge(added.sem, added.at(k, 3 * (i + 1)))
                    if past(k, 1):
                        pe.wait_ge(m_lo.sem, m_lo.at(k - 1, i + 1))
                    for c in range(DC):
                        mm = pe.transpose(t_bank[i][:, c, :], mean[i][:, c * P:(c + 1) * P], ident[:])
                    mm.then_inc(t_full.sem, 1)
                pe.wait_ge(m_lo.sem, m_lo.at(k, 2))
                for i in range(HB):
                    for e in range(E2):
                        pe.wait_ge(w_lo.sem, w_lo.at(k, 1 + e // 2))
                        if i:
                            pe.wait_ge(scaled.sem, scaled.at(k, e + 1))
                        else:
                            if past(k, 1):
                                pe.wait_ge(scaled.sem, scaled.at(k - 1, 4 + e + 1))
                        for c in range(DC):
                            for j, (a, b) in enumerate(((0, 0), (0, 1), (1, 0))):
                                mm = pe.matmul(bank[e][:, 0:D], mT[a][:, c, i, :], ws[b][:, c, e * D:(e + 1) * D],
                                               start=c == 0 and j == 0, stop=c == DC - 1 and j == 2)
                        mm.then_inc(full.sem, 1)
            loop(pe, body)

        @block.scalar
        def _(act):
            def body(k):
                act.wait_ge(w_landed.sem, w_landed.at(k, 16))
                if past(k, 1):
                    act.wait_ge(full.sem, full.at(k - 1, 8))
                for n in range(2):
                    nc.scalar.copy(ws[0][:, :, n * HC:(n + 1) * HC], raw[:, :, n * HC:(n + 1) * HC]).then_inc(w_hi.sem, 1)
                for i in range(HB):
                    act.wait_ge(t_full.sem, t_full.at(k, i + 1))
                    nc.scalar.activation(mT[0][:, :, i, :], t_bank[i][:], ACT.Identity, scale=1.0 / NS).then_inc(m_hi.sem, 1)
                for i in range(HB):
                    for e in range(E2):
                        act.wait_ge(full.sem, full.at(k, i * E2 + e + 1))
                        nc.scalar.activation(squares[:, i, e, :], bank[e][:, 0:D], ACT.Square, accum_out=ms[:, i, 0, e:e + 1]).then_inc(sq.sem, 1)
                    act.wait_ge(scaled.sem, scaled.at(k, E2 * (i + 1)))
                    act.dma_start(se_dram[bass.ds(k, 1), i * P:(i + 1) * P, :].rearrange("o r q -> (o r) q"),
                                  se[i][:].rearrange("p e d -> p (e d)")).then_inc(stored[i].sem, 16)
            loop(act, body)
            for s in stored:
                act.wait_ge(s.sem, 16 * E1)

        @block.vector
        def _(dve):
            def body(k):
                for i in range(HB):
                    dve.wait_ge(y_landed[i].sem, y_landed[i].at(k, 16))
                    if past(k, 1):
                        dve.wait_ge(t_full.sem, t_full.at(k - 1, i + 1))
                    nc.vector.tensor_tensor(mean[i][:], yk[i][:, 0, :], yk[i][:, 1, :], ALU.add).then_inc(added.sem, 1)
                    for n in range(2, NS):
                        dve.wait_ge(added.sem, added.at(k, 3 * i + n - 1))
                        nc.vector.tensor_tensor(mean[i][:], mean[i][:], yk[i][:, n, :], ALU.add).then_inc(added.sem, 1)
                for n in range(2):
                    dve.wait_ge(w_hi.sem, w_hi.at(k, n + 1))
                    nc.vector.tensor_tensor(ws[1][:, :, n * HC:(n + 1) * HC], raw[:, :, n * HC:(n + 1) * HC],
                                            ws[0][:, :, n * HC:(n + 1) * HC].bitcast(F32), ALU.subtract).then_inc(w_lo.sem, 1)
                for i in range(HB):
                    dve.wait_ge(m_hi.sem, m_hi.at(k, i + 1))
                    nc.vector.scalar_tensor_tensor(out=mT[1][:, :, i, :], in0=t_bank[i][:], scalar=1.0 / NS,
                                                   in1=mT[0][:, :, i, :].bitcast(F32), op0=ALU.mult,
                                                   op1=ALU.subtract).then_inc(m_lo.sem, 1)
                for i in range(HB):
                    dve.wait_ge(rs.sem, rs.at(k, i + 1))
                    if past(k, 1):
                        dve.wait_ge(stored[i].sem, stored[i].at(k - 1, 16))
                    for e in range(E2):
                        nc.vector.tensor_scalar(se[i][:, e, :], bank[e][:, 0:D], ms[:, i, 2, e:e + 1], SCALE,
                                                ALU.mult, ALU.mult).then_inc(scaled.sem, 1)
            loop(dve, body)

        @block.gpsimd
        def _(pool):
            def body(k):
                for i in range(HB):
                    pool.wait_ge(sq.sem, sq.at(k, E2 * (i + 1)))
                    nc.gpsimd.tensor_tensor(ms[:, i, 1, :], ms[:, i, 0, :], eps[:], ALU.add).then_inc(ve.sem, 1)
                    pool.wait_ge(ve.sem, ve.at(k, i + 1))
                    nc.gpsimd.tensor_tensor(ms[:, i, 2, :], ms[:, i, 1, :], nhalf[:], ALU.pow).then_inc(rs.sem, 1)
            loop(pool, body)


def dispatch(nc, ctx, sb, ps, sem, ident, yn_dram, se_dram, comb_dram, ct_dram, slots2T):
    G = 2
    NP = NB // G
    RING = 4
    yn = [sb(ctx, f"d_yn{i}", [P, G, D]) for i in range(RING)]
    se = [sb(ctx, f"d_se{i}", [P, G, D]) for i in range(RING)]
    cb = [sb(ctx, f"d_cb{i}", [P, G, P]) for i in range(RING)]
    ynT = [sb(ctx, f"d_ynT{i}", [P, G, D]) for i in range(2)]
    seT = [sb(ctx, f"d_seT{i}", [P, G, D]) for i in range(2)]
    lg = [sb(ctx, f"d_lg{i}", [P, G, 2, P]) for i in range(2)]
    dT = [sb(ctx, f"d_dT{i}", [P, G, P]) for i in range(2)]
    ct = [sb(ctx, f"d_ct{i}", [P, G, P]) for i in range(2)]
    mx = sb(ctx, "d_mx", [P, 2, G, 2])
    sm = sb(ctx, "d_sm", [P, 2, G, 2])
    rc = sb(ctx, "d_rc", [P, 2, G, 2])
    mask = sb(ctx, "d_mask", [P, P])
    yb = [ps(ctx, f"d_yb{g}", [P, 512]) for g in range(G)]
    eb = [ps(ctx, f"d_eb{g}", [P, 512]) for g in range(G)]
    lb = ps(ctx, "d_lb", [P, G, 2, P])
    wb = ps(ctx, "d_wb", [P, G, P])
    ob = [ps(ctx, f"d_ob{g}", [P, 512]) for g in range(G)]
    landed = [sem(ctx, f"d_landed{i}", 64) for i in range(RING)]
    stored = [sem(ctx, f"d_stored{i}", 16) for i in range(2)]
    y_full, e_full, l_full, w_full, s_full, c_full = (sem(ctx, n, c) for n, c in (
        ("d_y_full", G), ("d_e_full", G), ("d_l_full", 1), ("d_w_full", 1), ("d_s_full", G), ("d_c_full", 1)))
    ynT_ok, seT_ok, lg_ok, mx_ok, ex_ok, rc_ok, nm_ok, dT_ok, s_ok, ct_ok, mask_ok = (sem(ctx, n, c) for n, c in (
        ("d_ynT", G), ("d_seT", G), ("d_lg", 1), ("d_max", 1), ("d_exp", 4), ("d_recip", 1), ("d_norm", 1),
        ("d_dT", 1), ("d_s", G), ("d_ct", 1), ("d_mask", 1)))
    se_by_b = se_dram.rearrange("k (b m) (e d) -> b k (m e) d", m=M2, e=E2)

    def over_steps(eng, body):
        for i in range(RING):
            body(0, i)
        with eng.Fori(1, NP // RING) as r:
            for i in range(RING):
                body(r, i)
        for i in range(2):
            body(NP // RING, i)

    def before(r, i, lag):
        pair = (r, i - lag) if i >= lag else (r - 1, i - lag + RING)
        there = not isinstance(r, int) or 0 <= pair[0] * RING + pair[1] < NP
        return pair if there else None

    with nc.Block() as block:
        @block.sync
        def _(sp):
            def load(r, i):
                first = r * (RING * G) + i * G
                if past(r, 1):
                    sp.wait_ge(s_full.sem, s_full.at(r * RING - RING + i, G))
                sp.dma_start(yn[i][:], yn_dram[bass.ds(first, G)].rearrange("g p d -> p g d")).then_inc(landed[i].sem, 16)
                for g in range(G):
                    sp.dma_start(se[i][:, g, :], se_by_b[bass.ds(first + g, 1)].rearrange("o k r d -> (o k) r d")
                                 ).then_inc(landed[i].sem, 16)
                if past(r, 1):
                    sp.wait_ge(c_full.sem, c_full.at(r * RING - RING + i, 1))
                sp.dma_start(cb[i][:], comb_dram[bass.ds(first, G)].rearrange("g p d -> p g d")).then_inc(landed[i].sem, 16)

            def store(r, i):
                sp.wait_ge(ct_ok.sem, ct_ok.at(r * RING + i, 1))
                sp.dma_start(ct_dram[bass.ds(r * (RING * G) + i * G, G)].rearrange("g p d -> p g d"), ct[i % 2][:]
                             ).then_inc(stored[i % 2].sem, 16)

            for i in range(RING):
                load(0, i)
            with sp.Fori(1, NP // RING) as r:
                for i in range(RING):
                    load(r, i)
                    store(r - 1, i)
            for i in range(RING):
                store(NP // RING - 1, i)
            for s in stored:
                sp.wait_ge(s.sem, 16 * NP // 2)

        @block.gpsimd
        def _(pool):
            nc.gpsimd.memset(mask[:], 0.0).then_inc(mask_ok.sem, 1)
            pool.wait_ge(mask_ok.sem, 1)
            blocks = mask[:].rearrange("p (k j) -> p k j", k=E1)
            nc.gpsimd.affine_select(out=blocks, in_=blocks, compare_op=ALU.is_ge, fill=MASKED, base=0,
                                    pattern=[[-S1, E1], [0, S1]], channel_multiplier=1).then_inc(mask_ok.sem, 1)
            pool.wait_ge(mask_ok.sem, 2)
            nc.gpsimd.affine_select(out=blocks, in_=blocks, compare_op=ALU.is_ge, fill=MASKED, base=S1 - 1,
                                    pattern=[[S1, E1], [0, S1]], channel_multiplier=-1).then_inc(mask_ok.sem, 1)

        @block.tensor
        def _(pe):
            def turn(r, i):
                n = r * RING + i
                pe.wait_ge(landed[i].sem, landed[i].at(r, 64))
                for src, bank, full, read in ((yn[i], yb, y_full, ynT_ok), (se[i], eb, e_full, seT_ok)):
                    for g in range(G):
                        if past(n, 1):
                            pe.wait_ge(read.sem, read.at(n - 1, g + 1))
                        for c in range(DC):
                            mm = pe.transpose(bank[g][:, c * P:(c + 1) * P], src[:, g, c * P:(c + 1) * P], ident[:])
                        mm.then_inc(full.sem, 1)

            def logits(r, i):
                n = r * RING + i
                pe.wait_ge(ynT_ok.sem, ynT_ok.at(n, G))
                pe.wait_ge(seT_ok.sem, seT_ok.at(n, G))
                if past(n, 1):
                    pe.wait_ge(lg_ok.sem, lg_ok.at(n - 1, 1))
                for g in range(G):
                    for k, (left, right) in enumerate(((ynT[i % 2], seT[i % 2]), (seT[i % 2], ynT[i % 2]))):
                        for c in range(DC):
                            mm = pe.matmul(lb[:, g, k, :], left[:, g, c * P:(c + 1) * P], right[:, g, c * P:(c + 1) * P],
                                           start=c == 0, stop=c == DC - 1)
                mm.then_inc(l_full.sem, 1)

            def disp_T(r, i):
                n = r * RING + i
                pe.wait_ge(nm_ok.sem, nm_ok.at(n, 1))
                if past(n, 1):
                    pe.wait_ge(ct_ok.sem, ct_ok.at(n - 1, 1))
                for g in range(G):
                    mm = pe.transpose(wb[:, g, :], lg[i % 2][:, g, 1, :], ident[:])
                mm.then_inc(w_full.sem, 1)

            def back(r, i):
                n = r * RING + i
                pe.wait_ge(dT_ok.sem, dT_ok.at(n, 1))
                for g in range(G):
                    mm = pe.matmul(wb[:, g, :], lg[i % 2][:, g, 0, :], cb[i][:, g, :], start=True, stop=True)
                mm.then_inc(c_full.sem, 1)
                for g in range(G):
                    if past(n, 1):
                        pe.wait_ge(s_ok.sem, s_ok.at(n - 1, g + 1))
                    for c in range(DC):
                        mm = pe.matmul(ob[g][:, c * P:(c + 1) * P], yn[i][:, g, c * P:(c + 1) * P], dT[i % 2][:, g, :],
                                       start=True, stop=True)
                    mm.then_inc(s_full.sem, 1)

            def body(r, i):
                this, last, last2 = before(r, i, 0), before(r, i, 1), before(r, i, 2)
                if last2:
                    disp_T(*last2)
                if this:
                    turn(*this)
                if last:
                    logits(*last)
                if last2:
                    back(*last2)

            over_steps(pe, body)

        @block.scalar
        def _(act):
            def turn(r, i):
                n = r * RING + i
                for g in range(G):
                    act.wait_ge(y_full.sem, y_full.at(n, g + 1))
                    if past(n, 2):
                        act.wait_ge(l_full.sem, l_full.at(n - 2, 1))
                    nc.scalar.copy(ynT[i % 2][:, g, :], yb[g][:, 0:D]).then_inc(ynT_ok.sem, 1)

            def exps(r, i):
                n = r * RING + i
                act.wait_ge(mx_ok.sem, mx_ok.at(n, 1))
                for g in range(G):
                    for k in range(2):
                        nc.scalar.activation(lg[i % 2][:, g, k, :], lg[i % 2][:, g, k, :], ACT.Exp,
                                             bias=mx[:, i % 2, g, k:k + 1],
                                             accum_out=sm[:, i % 2, g, k:k + 1]).then_inc(ex_ok.sem, 1)

            def disp_T(r, i):
                n = r * RING + i
                act.wait_ge(w_full.sem, w_full.at(n, 1))
                if past(n, 2):
                    act.wait_ge(s_full.sem, s_full.at(n - 2, G))
                nc.scalar.copy(dT[i % 2][:], wb[:]).then_inc(dT_ok.sem, 1)

            def back(r, i):
                n = r * RING + i
                for g in range(G):
                    act.wait_ge(s_full.sem, s_full.at(n, g + 1))
                    nc.scalar.copy(slots2T[:, :, bass.ds(n * G + g, 1), :].rearrange("p c o n -> p c (o n)"),
                                   ob[g][:, 0:D].rearrange("p (c n) -> p c n", c=DC)).then_inc(s_ok.sem, 1)

            def body(r, i):
                this, last, last2 = before(r, i, 0), before(r, i, 1), before(r, i, 2)
                if last2:
                    disp_T(*last2)
                if this:
                    turn(*this)
                if last:
                    exps(*last)
                if last2:
                    back(*last2)

            over_steps(act, body)

        @block.vector
        def _(dve):
            def turn(r, i):
                n = r * RING + i
                for g in range(G):
                    dve.wait_ge(e_full.sem, e_full.at(n, g + 1))
                    if past(n, 2):
                        dve.wait_ge(l_full.sem, l_full.at(n - 2, 1))
                    nc.vector.tensor_copy(seT[i % 2][:, g, :], eb[g][:, 0:D]).then_inc(seT_ok.sem, 1)

            def logits(r, i):
                n = r * RING + i
                dve.wait_ge(l_full.sem, l_full.at(n, 1))
                if past(n, 2):
                    dve.wait_ge(c_full.sem, c_full.at(n - 2, 1))
                flat = lg[i % 2][:].rearrange("p g k n -> p (g k) n")
                nc.vector.tensor_tensor(flat, lb[:].rearrange("p g k n -> p (g k) n"),
                                        mask[:].unsqueeze(1).broadcast_to([P, 2 * G, P]), ALU.add).then_inc(lg_ok.sem, 1)
                dve.wait_ge(lg_ok.sem, lg_ok.at(n, 1))
                nc.vector.tensor_reduce(mx[:, i % 2].rearrange("p g k -> p (g k)"), flat, X_AXIS, ALU.max,
                                        negate=True).then_inc(mx_ok.sem, 1)

            def norms(r, i):
                n = r * RING + i
                dve.wait_ge(ex_ok.sem, ex_ok.at(n, 4))
                nc.vector.reciprocal(rc[:, i % 2].rearrange("p g k -> p (g k)"),
                                     sm[:, i % 2].rearrange("p g k -> p (g k)")).then_inc(rc_ok.sem, 1)
                dve.wait_ge(rc_ok.sem, rc_ok.at(n, 1))
                flat = lg[i % 2][:].rearrange("p g k n -> p (g k) n")
                nc.vector.tensor_tensor(flat, flat, rc[:, i % 2].rearrange("p g k -> p (g k)").unsqueeze(2).broadcast_to(
                    [P, 2 * G, P]), ALU.mult).then_inc(nm_ok.sem, 1)

            def back(r, i):
                n = r * RING + i
                dve.wait_ge(c_full.sem, c_full.at(n, 1))
                if past(n, 2):
                    dve.wait_ge(stored[i % 2].sem, 16 * (r * (RING // 2) + i // 2))
                nc.vector.tensor_copy(ct[i % 2][:], wb[:]).then_inc(ct_ok.sem, 1)

            def body(r, i):
                this, last, last2 = before(r, i, 0), before(r, i, 1), before(r, i, 2)
                if this:
                    turn(*this)
                if last:
                    logits(*last)
                if last2:
                    back(*last2)
                if last:
                    norms(*last)

            dve.wait_ge(mask_ok.sem, 3)
            over_steps(dve, body)


def experts(nc, ctx, sb, ps, sem, ident, slots2T, w1, b1, w2, b2, o_dram):
    PIECES = 4
    CH = HID // P // PIECES
    W = CH * P
    BANKS = 4
    raw1 = [sb(ctx, f"raw1_{i}", [P, DC, 2, W]) for i in range(PIECES)]
    raw2 = [sb(ctx, f"raw2_{i}", [P, CH, D]) for i in range(PIECES)]
    w1s = [[sb(ctx, f"x_w1_{i}_{s}", [P, DC, 2, W], F32R) for s in range(2)] for i in range(2)]
    w2s = [[sb(ctx, f"x_w2_{i}_{s}", [P, CH, D], F32R) for s in range(2)] for i in range(2)]
    xT = [[sb(ctx, f"x_in_{i}_{s}", [P, DC, XR], F32R) for s in range(2)] for i in range(2)]
    gel = sb(ctx, "x_gelu", [P, CH, XR])
    aT = [sb(ctx, f"x_act_{i}", [P, CH, XR]) for i in range(2)]
    aTs = [[sb(ctx, f"x_aT_{i}_{s}", [P, CH, XR], F32R) for s in range(2)] for i in range(2)]
    o_sb = sb(ctx, "x_o", [P, 2, D])
    b1r = sb(ctx, "x_b1r", [NX, 2 * HID])
    b1T = sb(ctx, "x_b1T", [P, 2 * HID // P, NX])
    b2r = [sb(ctx, f"x_b2r{i}", [P, D]) for i in range(2)]
    u_bank = [ps(ctx, f"u_bank{i}", [P, 2, XR]) for i in range(BANKS)]
    o_bank = [[ps(ctx, f"o_bank{i}{t}", [P, 512]) for t in range(2)] for i in range(2)]

    raw1_landed = [sem(ctx, f"raw1_landed{i}", 32) for i in range(PIECES)]
    raw2_landed = [sem(ctx, f"raw2_landed{i}", 16) for i in range(PIECES)]
    b1_landed, b2_landed = sem(ctx, "b1_landed", 16), [sem(ctx, f"b2_landed{i}", 16) for i in range(2)]
    b1_T, b1_ok = sem(ctx, "b1_T"), sem(ctx, "b1_ok")
    w1_hi, w1_lo, w2_hi, w2_lo = (sem(ctx, n, PIECES) for n in ("w1_hi", "w1_lo", "w2_hi", "w2_lo"))
    xh, xl = sem(ctx, "x_hi"), sem(ctx, "x_lo")
    u_full, g_ok, a_ok = (sem(ctx, n, PIECES * CH) for n in ("u_full", "gelu_ok", "act_ok"))
    ah, al = sem(ctx, "act_hi", PIECES), sem(ctx, "act_lo", PIECES)
    down_done, o_ok = sem(ctx, "down_done", PIECES), sem(ctx, "o_ok", 2)
    o_stored = sem(ctx, "o_stored", 32)
    w1x = w1.rearrange("k e (c p) (g h) -> (k e) p c g h", p=P, g=2)
    w2x = w2.rearrange("k e (c p) d -> (k e) p c d", p=P)
    b2x = b2.rearrange("k e d -> (k e) d")
    o_rows = o_dram.rearrange("(b k m e) d -> k e b m d", k=E1, m=M2, e=E2)
    slots_of = slots2T[:].rearrange("p c b (k m e) -> p c b m k e", k=E1, m=M2)

    def over_experts(eng, body):
        for e in range(E2):
            body(e, 0, e)
        with eng.Fori(1, E1 - 1) as k:
            for e in range(E2):
                body(k * E2 + e, k, e)
        for e in range(E2):
            body((E1 - 1) * E2 + e, E1 - 1, e)

    def is_last(x):
        return isinstance(x, int) and x == NX - 1

    with nc.Block() as block:
        @block.sync
        def _(sp):
            sp.dma_start(b1r[:], b1.rearrange("k e h -> (k e) h")).then_inc(b1_landed.sem, 16)

            def load(x, i):
                if past(x, 1):
                    sp.wait_ge(w1_lo.sem, w1_lo.at(x - 1, i + 1))
                for g in range(2):
                    sp.dma_start(raw1[i][:, :, g, :], w1x[bass.ds(x, 1), :, :, g, i * W:(i + 1) * W].rearrange(
                        "o p c h -> (o p) c h")).then_inc(raw1_landed[i].sem, 16)
                if past(x, 1):
                    sp.wait_ge(w2_lo.sem, w2_lo.at(x - 1, i + 1))
                sp.dma_start(raw2[i][:], w2x[bass.ds(x, 1), :, i * CH:(i + 1) * CH, :].rearrange(
                    "o p c d -> (o p) c d")).then_inc(raw2_landed[i].sem, 16)

            def load_b2(x, e):
                if past(x, 2):
                    sp.wait_ge(o_ok.sem, o_ok.at(x - 2, 2))
                sp.dma_start(b2r[e % 2][:], b2x[bass.ds(x, 1)].rearrange("o d -> (o d)").partition_broadcast(P)
                             ).then_inc(b2_landed[e % 2].sem, 16)

            def store(x, k, e):
                sp.wait_ge(o_ok.sem, o_ok.at(x, 2))
                for t in range(2):
                    sp.dma_start(o_rows[bass.ds(k, 1), e, t * NB // 2:(t + 1) * NB // 2].rearrange("o b m d -> (o b) m d"),
                                 o_sb[:, t, :]).then_inc(o_stored.sem, 16)

            def body(x, k, e):
                for i in range(PIECES):
                    load(x, i)
                    if i == 2:
                        if past(x, 2):
                            store(x - 2, k if e >= 2 else k - 1, (e - 2) % E2)
                        load_b2(x, e)
            over_experts(sp, body)
            for e in (E2 - 2, E2 - 1):
                store(NX - E2 + e, E1 - 1, e)
            sp.wait_ge(o_stored.sem, o_stored.n * NX)

        @block.tensor
        def _(pe):
            pe.wait_ge(b1_landed.sem, 16)
            for j in range(2 * HID // P):
                mm = pe.transpose(u_bank[0][:].rearrange("p a b -> p (a b)")[:, j * NX:(j + 1) * NX],
                                  b1r[:, j * P:(j + 1) * P], ident[0:NX, 0:NX])
            mm.then_inc(b1_T.sem, 1)
            pe.wait_ge(b1_ok.sem, 1)

            def up(x, e, i):
                if i == 0:
                    pe.wait_ge(xl.sem, xl.at(x, 1))
                pe.wait_ge(w1_lo.sem, w1_lo.at(x, i + 1))
                for c2 in range(CH):
                    n = i * CH + c2
                    if n >= BANKS:
                        pe.wait_ge(a_ok.sem, a_ok.at(x, n - BANKS + 1))
                    elif past(x, 1):
                        pe.wait_ge(a_ok.sem, a_ok.at(x - 1, PIECES * CH - BANKS + n + 1))
                    for g in range(2):
                        for c in range(DC):
                            for j, (a, b) in enumerate(((0, 0), (0, 1), (1, 0))):
                                mm = pe.matmul(u_bank[n % BANKS][:, g, :], w1s[i % 2][a][:, c, g, c2 * P:(c2 + 1) * P],
                                               xT[e % 2][b][:, c, :], start=c == 0 and j == 0, stop=c == DC - 1 and j == 2)
                    mm.then_inc(u_full.sem, 1)

            def down(x, e, i):
                pe.wait_ge(w2_lo.sem, w2_lo.at(x, i + 1))
                pe.wait_ge(al.sem, al.at(x, i + 1))
                if i == 0 and past(x, 2):
                    pe.wait_ge(o_ok.sem, o_ok.at(x - 2, 2))
                for t in range(2):
                    for c2 in range(CH):
                        for j, (a, b) in enumerate(((0, 0), (0, 1), (1, 0))):
                            mm = pe.matmul(o_bank[e % 2][t][:, 0:D], aTs[i % 2][a][:, c2, t * P:(t + 1) * P],
                                           w2s[i % 2][b][:, c2, :], start=i == 0 and c2 == 0 and j == 0,
                                           stop=i == PIECES - 1 and c2 == CH - 1 and j == 2)
                mm.then_inc(down_done.sem, 1)

            def body(x, k, e):
                up(x, e, 0)
                if past(x, 1):
                    down(x - 1, (e - 1) % E2, PIECES - 1)
                for i in range(1, PIECES):
                    up(x, e, i)
                    down(x, e, i - 1)
            over_experts(pe, body)
            down(NX - 1, E2 - 1, PIECES - 1)

        @block.scalar
        def _(act):
            act.wait_ge(b1_T.sem, 1)
            nc.scalar.copy(b1T[:].rearrange("p j x -> p (j x)"), u_bank[0][:].rearrange("p a b -> p (a b)")).then_inc(b1_ok.sem, 1)
            act.wait_ge(b1_ok.sem, 1)

            def split_w1(x, i):
                act.wait_ge(raw1_landed[i].sem, raw1_landed[i].at(x, 32))
                if i >= 2:
                    act.wait_ge(u_full.sem, u_full.at(x, (i - 1) * CH))
                elif past(x, 1):
                    act.wait_ge(u_full.sem, u_full.at(x - 1, (i + PIECES - 1) * CH))
                nc.scalar.copy(w1s[i % 2][0][:], raw1[i][:]).then_inc(w1_hi.sem, 1)

            def rows_hi(x, k, e):
                if past(x, 2):
                    act.wait_ge(u_full.sem, u_full.at(x - 2, PIECES * CH))
                src = slots_of[:, :, :, :, bass.ds(k, 1), e]
                nc.scalar.copy(xT[e % 2][0][:].rearrange("p c (b m) -> p c b m", m=M2),
                               src.rearrange("p c b m o -> p c b (m o)")).then_inc(xh.sem, 1)

            def gelu(x, i):
                for c2 in range(CH):
                    n = i * CH + c2
                    if n >= CH:
                        act.wait_ge(a_ok.sem, a_ok.at(x, n - CH + 1))
                    elif past(x, 1):
                        act.wait_ge(a_ok.sem, a_ok.at(x - 1, (PIECES - 1) * CH + n + 1))
                    act.wait_ge(u_full.sem, u_full.at(x, n + 1))
                    nc.scalar.activation(gel[:, c2, :], u_bank[n % BANKS][:, 1, :], ACT.Gelu_apprx_tanh,
                                         bias=b1T[:, HID // P + n, bass.ds(x, 1)]).then_inc(g_ok.sem, 1)

            def act_hi(x, i):
                act.wait_ge(a_ok.sem, a_ok.at(x, (i + 1) * CH))
                if i >= 2:
                    act.wait_ge(down_done.sem, down_done.at(x, i - 1))
                elif past(x, 1):
                    act.wait_ge(down_done.sem, down_done.at(x - 1, i + 3))
                nc.scalar.copy(aTs[i % 2][0][:], aT[i % 2][:]).then_inc(ah.sem, 1)

            def body(x, k, e):
                for i in range(PIECES):
                    gelu(x, i)
                    if i < 2:
                        split_w1(x, i + 2)
                    elif not is_last(x):
                        split_w1(x + 1, i - 2)
                    act_hi(x, i)
                    if i == 1 and not is_last(x):
                        rows_hi(x + 1, k if e < E2 - 1 else k + 1, (e + 1) % E2)
            rows_hi(0, 0, 0)
            for i in range(2):
                split_w1(0, i)
            over_experts(act, body)

        @block.vector
        def _(dve):
            dve.wait_ge(b1_ok.sem, 1)

            def split_w1(x, i):
                dve.wait_ge(w1_hi.sem, w1_hi.at(x, i + 1))
                nc.vector.tensor_tensor(w1s[i % 2][1][:], raw1[i][:], w1s[i % 2][0][:].bitcast(F32), ALU.subtract).then_inc(w1_lo.sem, 1)

            def split_w2(x, i):
                dve.wait_ge(raw2_landed[i].sem, raw2_landed[i].at(x, 16))
                if i >= 2:
                    dve.wait_ge(down_done.sem, down_done.at(x, i - 1))
                elif past(x, 1):
                    dve.wait_ge(down_done.sem, down_done.at(x - 1, i + 3))
                nc.vector.tensor_copy(w2s[i % 2][0][:], raw2[i][:]).then_inc(w2_hi.sem, 1)

            def rows_lo(x, k, e):
                dve.wait_ge(xh.sem, xh.at(x, 1))
                src = slots_of[:, :, :, :, bass.ds(k, 1), e].rearrange("p c b m o -> p c b (m o)")
                nc.vector.tensor_tensor(xT[e % 2][1][:].rearrange("p c (b m) -> p c b m", m=M2), src,
                                        xT[e % 2][0][:].bitcast(F32).rearrange("p c (b m) -> p c b m", m=M2),
                                        ALU.subtract).then_inc(xl.sem, 1)

            def gate(x, i):
                for c2 in range(CH):
                    n = i * CH + c2
                    if c2 == 0:
                        if i >= 2:
                            dve.wait_ge(al.sem, al.at(x, i - 1))
                        elif past(x, 1):
                            dve.wait_ge(al.sem, al.at(x - 1, i + 3))
                    dve.wait_ge(g_ok.sem, g_ok.at(x, n + 1))
                    nc.vector.scalar_tensor_tensor(out=aT[i % 2][:, c2, :], in0=u_bank[n % BANKS][:, 0, :],
                                                   scalar=b1T[:, n, bass.ds(x, 1)], in1=gel[:, c2, :],
                                                   op0=ALU.add, op1=ALU.mult).then_inc(a_ok.sem, 1)

            def rows_out(x, k, e):
                dve.wait_ge(down_done.sem, down_done.at(x, PIECES))
                dve.wait_ge(b2_landed[e % 2].sem, 16 * (k * (E2 // 2) + e // 2 + 1))
                if past(x, 1):
                    dve.wait_ge(o_stored.sem, o_stored.at(x - 1, 32))
                for t in range(2):
                    nc.vector.tensor_tensor(o_sb[:, t, :], o_bank[e % 2][t][:, 0:D], b2r[e % 2][:], ALU.add).then_inc(o_ok.sem, 1)

            def body(x, k, e):
                for i in range(PIECES):
                    gate(x, i)
                    if i < 2:
                        split_w1(x, i + 2)
                    elif not is_last(x):
                        split_w1(x + 1, i - 2)
                    if i == 0 and past(x, 1):
                        rows_out(x - 1, k if e else k - 1, (e - 1) % E2)
                    if i < PIECES - 1:
                        split_w2(x, i + 1)
                    elif not is_last(x):
                        split_w2(x + 1, 0)
                    if i == 1 and not is_last(x):
                        rows_lo(x + 1, k if e < E2 - 1 else k + 1, (e + 1) % E2)
            rows_lo(0, 0, 0)
            for i in range(2):
                split_w1(0, i)
            split_w2(0, 0)
            over_experts(dve, body)
            rows_out(NX - 1, E1 - 1, E2 - 1)

        @block.gpsimd
        def _(pool):
            def split_w2(x, i):
                pool.wait_ge(w2_hi.sem, w2_hi.at(x, i + 1))
                nc.gpsimd.tensor_tensor(w2s[i % 2][1][:], raw2[i][:], w2s[i % 2][0][:].bitcast(F32), ALU.subtract).then_inc(w2_lo.sem, 1)

            def act_lo(x, i):
                pool.wait_ge(ah.sem, ah.at(x, i + 1))
                nc.gpsimd.tensor_tensor(aTs[i % 2][1][:], aT[i % 2][:], aTs[i % 2][0][:].bitcast(F32), ALU.subtract).then_inc(al.sem, 1)

            def body(x, k, e):
                for i in range(PIECES):
                    act_lo(x, i)
                    if i < PIECES - 1:
                        split_w2(x, i + 1)
                    elif not is_last(x):
                        split_w2(x + 1, 0)
            split_w2(0, 0)
            over_experts(pool, body)


def combine(nc, ctx, sb, ps, sem, ct_dram, o_dram, res_dram, out):
    BUF = 4
    o_sb = [sb(ctx, f"c_o{i}", [P, D]) for i in range(BUF)]
    ct = [sb(ctx, f"c_ct{i}", [P, P]) for i in range(BUF)]
    res = [sb(ctx, f"c_res{i}", [P, D]) for i in range(BUF)]
    y = [sb(ctx, f"c_y{i}", [P, D]) for i in range(BUF)]
    bank = [ps(ctx, f"c_bank{i}", [P, 512]) for i in range(BUF)]
    landed = [sem(ctx, f"c_landed{i}", 48) for i in range(BUF)]
    stored = [sem(ctx, f"c_stored{i}", 16) for i in range(BUF)]
    full, added = sem(ctx, "c_full", BUF), sem(ctx, "c_added", BUF)
    out_rows = out.rearrange("b n d -> (b n) d")

    def loop(eng, body):
        for i in range(BUF):
            body(0, i)
        with eng.Fori(1, NB // BUF) as r:
            for i in range(BUF):
                body(r, i)

    with nc.Block() as block:
        @block.sync
        def _(sp):
            def body(r, i):
                if past(r, 1):
                    sp.wait_ge(added.sem, added.at(r - 1, i + 1))
                rows = bass.ds(r * BUF * P + i * P, P)
                sp.dma_start(o_sb[i][:], o_dram[rows, :]).then_inc(landed[i].sem, 16)
                sp.dma_start(ct[i][:], ct_dram[bass.ds(r * BUF + i, 1)].rearrange("o p n -> (o p) n")).then_inc(landed[i].sem, 16)
                sp.dma_start(res[i][:], res_dram[rows, :]).then_inc(landed[i].sem, 16)
            loop(sp, body)

        @block.tensor
        def _(pe):
            def body(r, i):
                pe.wait_ge(landed[i].sem, r * 48 + 48)
                if past(r, 1):
                    pe.wait_ge(added.sem, added.at(r - 1, i + 1))
                pe.matmul(bank[i][:, 0:D], ct[i][:], o_sb[i][:], start=True, stop=True).then_inc(full.sem, 1)
            loop(pe, body)

        @block.vector
        def _(dve):
            def body(r, i):
                dve.wait_ge(full.sem, full.at(r, i + 1))
                if past(r, 1):
                    dve.wait_ge(stored[i].sem, stored[i].at(r - 1, 16))
                nc.vector.tensor_tensor(y[i][:], bank[i][:, 0:D], res[i][:], ALU.add).then_inc(added.sem, 1)
            loop(dve, body)

        @block.scalar
        def _(act):
            def body(r, i):
                act.wait_ge(added.sem, added.at(r, i + 1))
                act.dma_start(out_rows[bass.ds(r * BUF * P + i * P, P), :], y[i][:]).then_inc(stored[i].sem, 16)
            loop(act, body)
            for s in stored:
                act.wait_ge(s.sem, 16 * NB // BUF)


_INS = ['x', 'adj', 'L0_gnn_wq', 'L0_gnn_bq', 'L0_gnn_wk', 'L0_gnn_bk', 'L0_gnn_wv', 'L0_gnn_bv', 'L0_gnn_wo',
        'L0_gnn_bo', 'L0_gnn_w1', 'L0_gnn_b1', 'L0_gnn_w2', 'L0_gnn_b2', 'L0_gnn_alpha1', 'L0_gnn_gamma1',
        'L0_gnn_alpha2', 'L0_gnn_gamma2', 'L0_ffn_gamma_in', 'L0_ffn_slots1', 'L0_ffn_gamma2', 'L0_ffn_w_slot2',
        'L0_ffn_w1', 'L0_ffn_b1', 'L0_ffn_w2', 'L0_ffn_b2']


def kernel(**inputs):
    import numpy as _np
    import concourse.bacc as _bacc
    from concourse import mybir as _mybir
    from concourse.bass_utils import run_bass_kernel_spmd as _run

    nc = _bacc.Bacc("TRN2", target_bir_lowering=False, num_devices=1, dynamic_dma_scratch_size=1024)
    arrays, args = {}, []
    for name in _INS:
        a = _np.ascontiguousarray(inputs[name])
        arrays[f"in_{name}_dram"] = a
        args.append(nc.dram_tensor(f"in_{name}_dram", a.shape, _mybir.dt.from_np(a.dtype), kind="ExternalInput").ap())
    args.append(nc.dram_tensor("out_0_dram", (NB, P, D), F32, kind="ExternalOutput").ap())
    build(nc, *args)
    r = _run(nc, [arrays], core_ids=[0])
    return r.results[0]["out_0_dram"]
```

```python
from contextlib import ExitStack

import concourse.bass as bass
from concourse import mybir

F32 = mybir.dt.float32
F32R = mybir.dt.float32r
BF16 = mybir.dt.bfloat16
ALU = mybir.AluOpType
ACT = mybir.ActivationFunctionType
X_AXIS = mybir.AxisListType.X

P = 128
D = 384
DC = D // P
NB = 64
H = 8
DH = D // H
HP = 64
FF = 1536
FC = FF // P
GT = 2
GN = GT * P
NG = NB // GT
PAIRS = FC // 2
E1, S1, E2, M2 = 8, 16, 4, 4
NS = S1 // E2
NX = E1 * E2
HID = 1024
XR = NB * M2
ROUND = 8
EARLY = (E1 - 1) * DC * NB * S1 // D // ROUND * ROUND
EPS_LN = 1e-5
EPS = 1e-6
SCALE = float(D) ** 0.5
MASKED = -1e30


class Signal:

    def __init__(self, sem, per_step):
        self.sem, self.n = sem, per_step

    def at(self, step, k):
        return step * self.n + k


def past(step, n):
    return not isinstance(step, int) or step >= n


def build(nc, x, adj, wq, bq, wk, bk, wv, bv, wo, bo, w1, b1, w2, b2, alpha1, gamma1, alpha2, gamma2,
          f_gamma_in, f_slots1, f_gamma2, f_w_slot2, f_w1, f_b1, f_w2, f_b2, out):
    names, taken = [0], []

    def dram(name, shape):
        return nc.dram_tensor(name, shape, F32, kind="Internal").ap()

    x_rows = x.rearrange("b n d -> (b n) d")
    res_dram = dram("residual", [NB * P, D])
    yn_dram = dram("yn", [NB, P, D])
    comb_dram = dram("comb1T", [NB, P, P])
    se_dram = dram("se2", [E1, NB * M2, E2 * D])
    ct_dram = dram("combT", [NB, P, P])
    o_dram = dram("expert_out", [NB * P, D])

    with ExitStack() as kernel_ctx:
        def sem(ctx, name, per_step=1):
            names[0] += 1
            handle = nc.alloc_semaphore(name=f"{name}_{names[0]}")
            taken.append(handle)
            return Signal(handle, per_step)

        def free_semaphores():
            nc.clear_and_free_semaphores(list(taken))
            taken.clear()
            nc.all_engine_barrier()

        def sb(ctx, name, shape, dt=F32):
            return ctx.enter_context(nc.sbuf_tensor(name, shape, dt))

        def ps(ctx, name, shape):
            return ctx.enter_context(nc.psum_tensor(name, shape, F32))

        ident = sb(kernel_ctx, "ident", [P, P])
        nhalf = sb(kernel_ctx, "nhalf", [P, 4])
        eps_ln = sb(kernel_ctx, "eps_ln", [P, 4])
        eps = sb(kernel_ctx, "eps", [P, 4])

        with ExitStack() as layer_ctx:
            setup_and_layer(nc, layer_ctx, sb, ps, sem, free_semaphores, ident, nhalf, eps_ln, eps, x_rows, adj, wq, bq, wk, bk, wv, bv,
                            wo, bo, w1, b1, w2, b2, alpha1, gamma1, alpha2, gamma2, f_gamma_in, f_slots1,
                            f_gamma2, res_dram, yn_dram, comb_dram)
        with ExitStack() as ctx:
            routes(nc, ctx, sb, ps, sem, ident, nhalf, eps, f_w_slot2, yn_dram, se_dram)
        with ExitStack() as experts_ctx:
            slots2T = sb(experts_ctx, "slots2T", [P, E1, DC, NB, S1])
            early = slots2T[:].rearrange("p k c b j -> p (k c b j)")[:, 0:EARLY * D].rearrange("p (g d) -> p g d", d=D)
            res_landed = sem(experts_ctx, "res_landed", 16)
            with ExitStack() as ctx:
                dispatch(nc, ctx, sb, ps, sem, ident, yn_dram, se_dram, comb_dram, ct_dram, slots2T)
            with ExitStack() as ctx:
                experts(nc, ctx, sb, ps, sem, ident, slots2T, f_w1, f_b1, f_w2, f_b2, o_dram, res_dram, early,
                        res_landed)
            with ExitStack() as ctx:
                combine(nc, ctx, sb, ps, sem, ct_dram, o_dram, res_dram, out, early, res_landed)


def setup_and_layer(nc, ctx, sb, ps, sem, free_semaphores, ident, nhalf, eps_ln, eps, x_rows, adj, wq, bq, wk, bk, wv, bv, wo, bo, w1, b1,
                    w2, b2, alpha1, gamma1, alpha2, gamma2, f_gamma_in, f_slots1, f_gamma2, res_dram,
                    yn_dram, comb_dram):
    def split_pair(name, shape):
        return [sb(ctx, name + "_hi", shape, F32R), sb(ctx, name + "_lo", shape, F32R)]

    wq_s = split_pair("wq", [P, DC, H * HP])
    wk_s = split_pair("wk", [P, DC, H * HP])
    wv_s = split_pair("wv", [P, DC, D])
    wo_s = split_pair("wo", [P, DC, D])
    w1_s = split_pair("w1", [P, DC, FF])
    w2_s = split_pair("w2", [P, FC, D])
    phiT = sb(ctx, "phiT", [P, DC, P])
    bqk = sb(ctx, "bqk", [P, 2, H // 2])
    b1c = sb(ctx, "b1c", [P, FC])
    rows = {n: sb(ctx, "row_" + n, [P, D]) for n in
            ("bv", "bo", "alpha1", "gamma1", "b2", "alpha2", "gamma2", "gin", "g2")}

    with ExitStack() as setup:
        stage = [sb(setup, f"stage{i}", [P, w]) for i, w in enumerate(
            (DC * H * HP, DC * H * HP, DC * D, DC * D, DC * FF, FC * D))]
        phi = sb(setup, "phi", [P, D])
        phi_sq = sb(setup, "phi_sq", [P, D])
        phi_ss = sb(setup, "phi_ss", [P, 4])
        tp = ps(setup, "tp", [P, DC, P])
        staged = [sem(setup, f"staged{i}") for i in range(len(stage))]
        zeroed = sem(setup, "zeroed")
        hi_done = sem(setup, "hi_done")
        lo_done = sem(setup, "lo_done")
        small = sem(setup, "small")
        pool_done = sem(setup, "pool_done")
        phi_done = sem(setup, "phi_done")
        phi_T = sem(setup, "phi_T")

        def padded(t):
            return t[:, 0:DC * H * HP].rearrange("p (c h e) -> p c h e", c=DC, h=H)

        weights = []
        for i, (w, parts) in enumerate(((wq, wq_s), (wk, wk_s), (wv, wv_s), (wo, wo_s), (w1, w1_s), (w2, w2_s))):
            s = stage[i]
            if i < 2:
                srcs = [(padded(s)[:, c, :, 0:DH], w[c * P:(c + 1) * P, :].rearrange("p (h e) -> p h e", h=H))
                        for c in range(DC)]
                flat = s[:, 0:DC * H * HP]
            else:
                n = w.shape[0] // P * w.shape[1]
                srcs = [(s[:, 0:n].rearrange("p (c f) -> p c f", c=w.shape[0] // P),
                         w.rearrange("(c p) f -> p c f", p=P))]
                flat = s[:, 0:n]
            weights.append((srcs, flat, [t[:].rearrange("p c f -> p (c f)") for t in parts]))

        n_small = [0]

        def small_load(eng, dst, src):
            eng.dma_start(dst, src).then_inc(small.sem, 16)
            n_small[0] += 16

        with nc.Block() as block:
            @block.sync
            def _(sp):
                for i, (srcs, _, _) in enumerate(weights):
                    if i < 2:
                        sp.wait_ge(zeroed.sem, i + 1)
                    for dst, src in srcs:
                        sp.dma_start(dst, src).then_inc(staged[i].sem, 16)
                small_load(sp, phi[:], f_slots1.rearrange("k s d -> (k s) d"))
                for name, src in (("bv", bv), ("bo", bo), ("alpha1", alpha1), ("gamma1", gamma1), ("b2", b2),
                                  ("alpha2", alpha2), ("gamma2", gamma2), ("gin", f_gamma_in)):
                    small_load(sp, rows[name][:], src.partition_broadcast(P))
                small_load(sp, rows["g2"][:], f_gamma2.rearrange("k (o d) -> k o d", o=1).broadcast_to([E1, S1, D]))
                sp.wait_ge(zeroed.sem, 3)
                for n, b in enumerate((bq, bk)):
                    for half in range(2):
                        src = b.rearrange("(m two e) -> two e m", two=2, e=DH)[half]
                        for m in range(H // 2):
                            small_load(sp, bqk[HP * half:HP * half + DH, n, m:m + 1], src[:, m:m + 1])
                for m in range(FC):
                    small_load(sp, b1c[:, m:m + 1], b1[m * P:(m + 1) * P].rearrange("(p o) -> p o", o=1))

            @block.scalar
            def _(act):
                for i, (_, flat, parts) in enumerate(weights):
                    act.wait_ge(staged[i].sem, 16 * len(weights[i][0]))
                    nc.scalar.copy(parts[0], flat).then_inc(hi_done.sem, 1)
                act.wait_ge(small.sem, n_small[0])
                nc.scalar.activation(phi_sq[:], phi[:], ACT.Square, accum_out=phi_ss[:, 0:1]).then_inc(phi_done.sem, 1)
                act.wait_ge(phi_T.sem, 1)
                nc.scalar.copy(phiT[:], tp[:]).then_inc(phi_done.sem, 1)

            @block.gpsimd
            def _(pool):
                nc.gpsimd.memset(ident[:], 0.0).then_inc(pool_done.sem, 1)
                nc.gpsimd.memset(eps_ln[:], EPS_LN)
                nc.gpsimd.memset(eps[:], EPS)
                nc.gpsimd.memset(nhalf[:], -0.5).then_inc(pool_done.sem, 1)
                pool.wait_ge(pool_done.sem, 2)
                nc.gpsimd.affine_select(out=ident[:], in_=ident[:], compare_op=ALU.not_equal, fill=1.0, base=0,
                                        pattern=[[-1, P]], channel_multiplier=1).then_inc(pool_done.sem, 1)
                pool.wait_ge(phi_done.sem, 1)
                nc.gpsimd.tensor_scalar(phi_ss[:, 1:2], phi_ss[:, 0:1], EPS, 1.0, ALU.add, ALU.mult).then_inc(pool_done.sem, 1)
                pool.wait_ge(pool_done.sem, 4)
                nc.gpsimd.tensor_tensor(phi_ss[:, 2:3], phi_ss[:, 1:2], nhalf[:, 0:1], ALU.pow).then_inc(pool_done.sem, 1)

            @block.vector
            def _(dve):
                for s in stage[0:2]:
                    nc.vector.memset(s[:, 0:DC * H * HP], 0.0).then_inc(zeroed.sem, 1)
                nc.vector.memset(bqk[:], 0.0).then_inc(zeroed.sem, 1)
                for i, (_, flat, parts) in enumerate(weights):
                    dve.wait_ge(hi_done.sem, i + 1)
                    nc.vector.tensor_tensor(parts[1], flat, parts[0].bitcast(F32), ALU.subtract).then_inc(lo_done.sem, 1)
                dve.wait_ge(small.sem, n_small[0])
                nc.vector.tensor_scalar(rows["gin"][:], rows["gin"][:], SCALE, None, ALU.mult)
                nc.vector.tensor_scalar(rows["g2"][:], rows["g2"][:], SCALE, None, ALU.mult)
                nc.vector.tensor_scalar(bqk[:, 0, :], bqk[:, 0, :], DH ** -0.5, None, ALU.mult)
                dve.wait_ge(pool_done.sem, 5)
                nc.vector.tensor_scalar(phi[:], phi[:], phi_ss[:, 2:3], SCALE, ALU.mult, ALU.mult).then_inc(lo_done.sem, 1)

            @block.tensor
            def _(pe):
                pe.wait_ge(pool_done.sem, 5)
                pe.wait_ge(lo_done.sem, len(weights) + 1)
                for c in range(DC):
                    mm = pe.transpose(tp[:, c, :], phi[:, c * P:(c + 1) * P], ident[:])
                mm.then_inc(phi_T.sem, 1)

    free_semaphores()

    t_sb = lambda name, shape, dt=F32: sb(ctx, name, shape, dt)
    x_in = t_sb("x_in", [P, GT, D])
    adj_sb = t_sb("adj_sb", [P, GT, P])
    z = t_sb("z", [P, GT, D])
    zT = [t_sb("zT_hi", [P, DC, GN], F32R), t_sb("zT_lo", [P, DC, GN], F32R)]
    qT = t_sb("qT", [P, H // 2, GN])
    kT = t_sb("kT", [P, H // 2, GN])
    v_sb = t_sb("v_sb", [P, GT, D])
    s_sb = [t_sb(f"s_sb{t}", [P, 2, H // 2, P]) for t in range(GT)]
    pT = t_sb("pT", [P, 2, H // 2, P])
    ctx_sb = t_sb("ctx_sb", [P, D])
    cT = [t_sb("cT_hi", [P, DC, P], F32R), t_sb("cT_lo", [P, DC, P], F32R)]
    y = t_sb("y", [P, GT, D])
    yT = [t_sb("yT_hi", [P, DC, GN], F32R), t_sb("yT_lo", [P, DC, GN], F32R)]
    yb = t_sb("yb", [P, GT, D])
    h_tmp = [t_sb(f"h_tmp{i}", [P, 2, GN]) for i in range(2)]
    hT = [[t_sb(f"hT_hi{i}", [P, 2, GN], F32R), t_sb(f"hT_lo{i}", [P, 2, GN], F32R)] for i in range(3)]
    f_sb = t_sb("f_sb", [P, GT, D])
    x_res = t_sb("x_res", [P, GT, D])
    xn = t_sb("xn", [P, GT, D])
    xnT = t_sb("xnT", [P, DC, GN])
    logit = t_sb("logit", [P, GT, P])
    comb = t_sb("comb", [P, GT, P])
    disp = t_sb("disp", [P, GT, P])
    dcT = t_sb("dcT", [P, 2, GT, P])
    yn = t_sb("yn_sb", [P, GT, D])
    squares = {n: t_sb("squares_" + n, [P, GT, D], BF16) for n in ("r", "f")}
    counts = t_sb("counts", [P, GT])
    st = t_sb("st", [P, GT, 6])
    mv = t_sb("mv", [P, GT, 2])
    rstd = t_sb("rstd", [P, 2, GT])
    nmax = t_sb("nmax", [P, GT, H])
    ssum = t_sb("ssum", [P, GT, H])
    rsum = t_sb("rsum", [P, GT, H])
    rms = t_sb("rms", [P, GT, 3])
    fms = t_sb("fms", [P, GT, 3])
    st2 = t_sb("st2", [P, GT, 6])
    mv2 = t_sb("mv2", [P, GT, 2])
    rstd2 = t_sb("rstd2", [P, 2, GT])
    zms = t_sb("zms", [P, GT, 3])
    lmx = t_sb("lmx", [P, 2, GT])
    lsum = t_sb("lsum", [P, 2, GT])
    lrec = t_sb("lrec", [P, 2, GT])
    sms = t_sb("sms", [P, GT, 3])

    a_bank = [ps(ctx, f"a_bank{i}", [P, 512]) for i in range(3)]
    m_bank = [ps(ctx, f"m_bank{i}", [P, 2, GN]) for i in range(2)]
    f_bank = [ps(ctx, f"f_bank{i}", [P, 512]) for i in range(GT)]
    r_bank = ps(ctx, "r_bank", [P, 512])

    S = lambda name, n: sem(ctx, name, n)
    x_landed, adj_landed = S("x_landed", 16), S("adj_landed", 16)
    stats, meanvar, ve, rstd_ok, z_ok = S("stats", 2), S("meanvar", 2), S("ve", 1), S("rstd_ok", 1), S("z_ok", 2)
    zh, zl = S("zT_hi", 2), S("zT_lo", 2)
    q_ok, k_ok, v_ok = S("q", 4), S("k", 4), S("v", 2)
    sc_ok, mx_ok, p_ok, rs_ok = S("scores", 4), S("row_max", 2), S("exp", 16), S("recip", 2)
    pt_ok, ctx_ok, ch, cl = S("pT", 4), S("ctx", 2), S("cT_hi", 2), S("cT_lo", 2)
    r_ok, rb_ok, rss, rve, rrs = S("r", 2), S("r_bias", 2), S("r_ss", 2), S("r_ve", 2), S("r_rs", 2)
    ys, y_ok, yh, yl = S("y_scaled", 2), S("y", 2), S("yT_hi", 2), S("yT_lo", 2)
    a_full, zt_full = S("a_bank_full", 22), S("zT_full", 2)
    res_landed = S("x_res_landed", 16)
    yb_ok, h_ok, hh, hl = S("yb", 2), S("h", 12), S("hT_hi", 6), S("hT_lo", 6)
    f_ok, fss, fve, frs = S("f", 2), S("f_ss", 2), S("f_ve", 2), S("f_rs", 2)
    fs, xg, xo = S("f_scaled", 2), S("x_plus_gamma", 2), S("layer_out", 2)
    m_full, f_full, h_used = S("m_bank_full", 6), S("f_bank_full", 2), S("h_used", PAIRS - 1)
    res_stored = S("res_stored", 16)
    st2_ok, mv2_ok, ve2, rstd2_ok, z2_ok = S("stats2", 2), S("meanvar2", 2), S("ve2", 1), S("rstd2_ok", 1), S("z2", 2)
    zss, zve, zrs, xn_ok = S("z_ss", 2), S("z_ve", 1), S("z_rs", 1), S("xn", 2)
    xt_ok, lg_ok, lm_ok, le_ok, lr_ok, cb_ok = S("xnT", 2), S("logit", 1), S("l_max", 1), S("l_exp", 2), S("l_recip", 1), S("comb", 2)
    dm_ok, de_ok, dr_ok, tt_ok = S("d_max", 1), S("d_exp", 2), S("d_recip", 1), S("dcT", 1)
    sl_ok, sss, sve, srs, yn_ok = S("slots", 2), S("s_ss", 2), S("s_ve", 2), S("s_rs", 2), S("yn", 2)
    r_full = S("r_bank_full", 7)
    yn_stored, comb_stored = S("yn_stored", 16), S("comb_stored", 16)

    U_Q, U_K, U_V, U_S = (0, 1), (2, 3), (4, 5), ((6, 7), (8, 9))
    U_PT, U_CTX, U_CT, U_WO, U_YT = ((10, 11), (13, 14)), (12, 16), (15, 18), (17, 19), (20, 21)
    A_BANK = [a_bank[u % 3] for u in range(20)] + [a_bank[0], a_bank[2]]
    ZT_BANK = [a_bank[2], a_bank[1]]

    def tok(t):
        return slice(t * P, (t + 1) * P)

    with nc.Block() as block:
        @block.sync
        def _(sp):
            def body(a, m, r, n):
                if n is not None:
                    if past(n, 1):
                        sp.wait_ge(z_ok.sem, z_ok.at(n - 1, 2))
                    sp.dma_start(x_in[:], x_rows[bass.ds(n * GN, GN), :].rearrange("(t p) d -> p t d", p=P)
                                 ).then_inc(x_landed.sem, 16)
                if a is not None:
                    if past(a, 1):
                        sp.wait_ge(sc_ok.sem, sc_ok.at(a - 1, 4))
                    sp.dma_start(adj_sb[:], adj[bass.ds(a * GT, GT)].rearrange("t q k -> q t k")
                                 ).then_inc(adj_landed.sem, 16)
                if m is not None:
                    if past(m, 1):
                        sp.wait_ge(xo.sem, xo.at(m - 1, 2))
                    sp.dma_start(x_res[:], x_rows[bass.ds(m * GN, GN), :].rearrange("(t p) d -> p t d", p=P)
                                 ).then_inc(res_landed.sem, 16)
                if r is not None:
                    sp.wait_ge(tt_ok.sem, tt_ok.at(r, 1))
                    sp.dma_start(comb_dram[bass.ds(r * GT, GT)].rearrange("t p n -> p t n"), dcT[:, 1, :, :]
                                 ).then_inc(comb_stored.sem, 16)
                    sp.wait_ge(yn_ok.sem, yn_ok.at(r, 2))
                    sp.dma_start(yn_dram[bass.ds(r * GT, GT)].rearrange("t p d -> p t d"), yn[:]
                                 ).then_inc(yn_stored.sem, 16)
                if m is not None:
                    sp.wait_ge(xo.sem, xo.at(m, 2))
                    sp.dma_start(res_dram[bass.ds(m * GN, GN), :].rearrange("(t p) d -> p t d", p=P), f_sb[:]
                                 ).then_inc(res_stored.sem, 16)

            run(sp, body)
            sp.wait_ge(res_stored.sem, 16 * NG)
            sp.wait_ge(yn_stored.sem, 16 * NG)
            sp.wait_ge(comb_stored.sem, 16 * NG)

        @block.tensor
        def _(pe):
            def split_mm(dst, lhs, rhs, start=True, stop=True):
                n = len(lhs)
                for c in range(n):
                    (lh, ll), (rh, rl) = lhs[c], rhs[c]
                    for j, (left, right) in enumerate(((lh, rh), (lh, rl), (ll, rh))):
                        mm = pe.matmul(dst, left, right, start=start and c == 0 and j == 0,
                                       stop=stop and c == n - 1 and j == 2)
                return mm

            def zT_step(g, t):
                pe.wait_ge(z_ok.sem, z_ok.at(g, t + 1))
                if past(g, 1):
                    pe.wait_ge(r_ok.sem, r_ok.at(g - 1, t + 1))
                for c in range(DC):
                    mm = pe.transpose(ZT_BANK[t][:, tok(c)], z[:, t, tok(c)], ident[:])
                mm.then_inc(zt_full.sem, 1)

            def project(g, uses, w, n):
                if w is wq_s and n == 0:
                    pe.wait_ge(zl.sem, zl.at(g, 2))
                    if past(g, 1):
                        pe.wait_ge(yl.sem, yl.at(g - 1, 1))
                if w is wk_s and n == 0:
                    if past(g, 1):
                        pe.wait_ge(yl.sem, yl.at(g - 1, 2))
                if w is wk_s and n == 1:
                    pe.wait_ge(q_ok.sem, q_ok.at(g, 2))
                bank = A_BANK[uses[n]]
                for half in range(2):
                    m = 2 * n + half
                    mm = split_mm(bank[:, half * GN:(half + 1) * GN],
                                  [[w[s][:, c, tok(m)] for s in range(2)] for c in range(DC)],
                                  [[zT[s][:, c, :] for s in range(2)] for c in range(DC)])
                mm.then_inc(a_full.sem, 1)

            def values(g, t):
                if t == 0:
                    pe.wait_ge(q_ok.sem, q_ok.at(g, 4))
                else:
                    pe.wait_ge(k_ok.sem, k_ok.at(g, 2))
                bank = A_BANK[U_V[t]]
                split_mm(bank[:, 0:D], [[zT[s][:, c, tok(t)] for s in range(2)] for c in range(DC)],
                         [[wv_s[s][:, c, :] for s in range(2)] for c in range(DC)]).then_inc(a_full.sem, 1)

            def scores(g, t):
                pe.wait_ge(q_ok.sem, q_ok.at(g, 4))
                pe.wait_ge(k_ok.sem, k_ok.at(g, 4))
                for par in range(2):
                    held, k = ((k_ok, 4), (v_ok, 1), (v_ok, 2), (sc_ok, 1))[2 * t + par]
                    pe.wait_ge(held.sem, held.at(g, k))
                    bank = A_BANK[U_S[t][par]]
                    r = slice(HP * par, HP * par + DH)
                    for m in range(H // 2):
                        mm = pe.matmul(bank[:, tok(m)], qT[r, m, tok(t)], kT[r, m, tok(t)], start=True, stop=True)
                    mm.then_inc(a_full.sem, 1)

            def prob_T(g, t):
                for par in range(2):
                    pe.wait_ge(p_ok.sem, p_ok.at(g, 8 * t + 4 * (par + 1)))
                    held, k = ((sc_ok, 2), (sc_ok, 3), (pt_ok, 1), (pt_ok, 2))[2 * t + par]
                    pe.wait_ge(held.sem, held.at(g, k))
                    bank = A_BANK[U_PT[t][par]]
                    for m in range(H // 2):
                        mm = pe.transpose(bank[:, tok(m)], s_sb[t][:, par, m, :], ident[:])
                    mm.then_inc(a_full.sem, 1)

            def context(g, t):
                pe.wait_ge(v_ok.sem, v_ok.at(g, t + 1))
                held, k = ((sc_ok, 4), (pt_ok, 3))[t]
                pe.wait_ge(held.sem, held.at(g, k))
                bank = A_BANK[U_CTX[t]]
                for par in range(2):
                    pe.wait_ge(pt_ok.sem, pt_ok.at(g, 2 * t + par + 1))
                    for m in range(H // 2):
                        h = 2 * m + par
                        mm = pe.matmul(bank[:, h * DH:(h + 1) * DH], pT[:, par, m, :],
                                       v_sb[:, t, h * DH:(h + 1) * DH], start=True, stop=True)
                mm.then_inc(a_full.sem, 1)

            def context_T(g, t):
                pe.wait_ge(ctx_ok.sem, ctx_ok.at(g, t + 1))
                if t:
                    pe.wait_ge(cl.sem, cl.at(g, 1))
                bank = A_BANK[U_CT[t]]
                for c in range(DC):
                    mm = pe.transpose(bank[:, tok(c)], ctx_sb[:, tok(c)], ident[:])
                mm.then_inc(a_full.sem, 1)

            def project_out(g, t):
                pe.wait_ge(cl.sem, cl.at(g, t + 1))
                held, k = ((pt_ok, 4), (ctx_ok, 2))[t]
                pe.wait_ge(held.sem, held.at(g, k))
                bank = A_BANK[U_WO[t]]
                split_mm(bank[:, 0:D], [[cT[s][:, c, :] for s in range(2)] for c in range(DC)],
                         [[wo_s[s][:, c, :] for s in range(2)] for c in range(DC)]).then_inc(a_full.sem, 1)

            def yT_step(g, t):
                pe.wait_ge(y_ok.sem, y_ok.at(g, t + 1))
                if t == 0:
                    pe.wait_ge(cl.sem, cl.at(g, 2))
                elif not (isinstance(g, int) and g == NG - 1):
                    pe.wait_ge(zl.sem, zl.at(g + 1, 1))
                bank = A_BANK[U_YT[t]]
                for c in range(DC):
                    mm = pe.transpose(bank[:, tok(c)], y[:, t, tok(c)], ident[:])
                mm.then_inc(a_full.sem, 1)

            def up(g, i):
                pe.wait_ge(yl.sem, yl.at(g, 2))
                if i >= 2:
                    pe.wait_ge(h_ok.sem, h_ok.at(g, 2 * (i - 1)))
                else:
                    if past(g, 1):
                        pe.wait_ge(h_ok.sem, h_ok.at(g - 1, 12 - 2 * (1 - i)))
                for half in range(2):
                    m = 2 * i + half
                    mm = split_mm(m_bank[i % 2][:, half, :],
                                  [[w1_s[s][:, c, tok(m)] for s in range(2)] for c in range(DC)],
                                  [[yT[s][:, c, :] for s in range(2)] for c in range(DC)])
                mm.then_inc(m_full.sem, 1)

            def down(g, i):
                pe.wait_ge(hh.sem, hh.at(g, i + 1))
                pe.wait_ge(hl.sem, hl.at(g, i + 1))
                for t in range(GT):
                    if i == 0:
                        if past(g, 1):
                            pe.wait_ge(f_ok.sem, f_ok.at(g - 1, t + 1))
                    mm = split_mm(f_bank[t][:, 0:D],
                                  [[hT[i % 3][s][:, half, tok(t)] for s in range(2)] for half in range(2)],
                                  [[w2_s[s][:, 2 * i + half, :] for s in range(2)] for half in range(2)],
                                  start=i == 0, stop=i == PAIRS - 1)
                    if i == PAIRS - 1:
                        mm.then_inc(f_full.sem, 1)
                if i < PAIRS - 1:
                    mm.then_inc(h_used.sem, 1)

            def xnT_step(g, t):
                pe.wait_ge(xn_ok.sem, xn_ok.at(g, t + 1))
                if t == 0:
                    if past(g, 1):
                        pe.wait_ge(sl_ok.sem, sl_ok.at(g - 1, 2))
                else:
                    pe.wait_ge(xt_ok.sem, xt_ok.at(g, 1))
                for c in range(DC):
                    mm = pe.transpose(r_bank[:, tok(c)], xn[:, t, tok(c)], ident[:])
                mm.then_inc(r_full.sem, 1)

            def logits(g):
                pe.wait_ge(xt_ok.sem, xt_ok.at(g, 2))
                for t in range(GT):
                    for c in range(DC):
                        mm = pe.matmul(r_bank[:, tok(t)], xnT[:, c, tok(t)], phiT[:, c, :], start=c == 0, stop=c == DC - 1)
                mm.then_inc(r_full.sem, 1)

            def logits_T(g):
                pe.wait_ge(lg_ok.sem, lg_ok.at(g, 1))
                for t in range(GT):
                    mm = pe.transpose(r_bank[:, tok(t)], logit[:, t, :], ident[:])
                mm.then_inc(r_full.sem, 1)

            def weights_T(g):
                pe.wait_ge(de_ok.sem, de_ok.at(g, 2))
                pe.wait_ge(cb_ok.sem, cb_ok.at(g, 2))
                for n, w in enumerate((disp, comb)):
                    for t in range(GT):
                        mm = pe.transpose(r_bank[:, tok(2 * n + t)], w[:, t, :], ident[:])
                mm.then_inc(r_full.sem, 1)

            def slots(g, t):
                if t == 0:
                    pe.wait_ge(tt_ok.sem, tt_ok.at(g, 1))
                else:
                    pe.wait_ge(sl_ok.sem, sl_ok.at(g, 1))
                pe.matmul(r_bank[:, 0:D], dcT[:, 0, t, :], xn[:, t, :], start=True, stop=True).then_inc(r_full.sem, 1)

            def body(a, m, r, n):
                A, M, R, N = (v is not None for v in (a, m, r, n))
                if A: project(a, U_Q, wq_s, 0); project(a, U_Q, wq_s, 1)
                if M: up(m, 0)
                if A: project(a, U_K, wk_s, 0); project(a, U_K, wk_s, 1)
                if M: up(m, 1)
                if A: values(a, 0); values(a, 1); scores(a, 0)
                if R: xnT_step(r, 0)
                if A: scores(a, 1)
                if R: xnT_step(r, 1)
                if M: down(m, 0)
                if A: prob_T(a, 0)
                if R: logits(r)
                if M: down(m, 1)
                if A: context(a, 0); prob_T(a, 1)
                if R: logits_T(r)
                if M: up(m, 2)
                if A: context_T(a, 0); context(a, 1)
                if M: up(m, 3)
                if A: project_out(a, 0); context_T(a, 1)
                if R: weights_T(r)
                if M: down(m, 2)
                if A: project_out(a, 1)
                if M: up(m, 4); down(m, 3)
                if N: zT_step(n, 0)
                if R: slots(r, 0)
                if M: up(m, 5)
                if A: yT_step(a, 0)
                if N: zT_step(n, 1)
                if M: down(m, 4)
                if A: yT_step(a, 1)
                if R: slots(r, 1)
                if M: down(m, 5)

            run(pe, body)

        @block.scalar
        def _(act):
            def hi_zT(g, t):
                act.wait_ge(zt_full.sem, zt_full.at(g, t + 1))
                if past(g, 1):
                    act.wait_ge(a_full.sem, a_full.at(g - 1, U_V[1] + 1))
                nc.scalar.copy(zT[0][:, :, tok(t)], ZT_BANK[t][:, 0:D].rearrange("p (c n) -> p c n", c=DC)).then_inc(zh.sem, 1)

            def hi_yT(g, t):
                if past(g, 1):
                    act.wait_ge(m_full.sem, m_full.at(g - 1, PAIRS))
                hi_T(g, t, U_YT, yT[0][:, :, tok(t)], yh)

            def hi_T(g, t, use, dst, sig):
                act.wait_ge(a_full.sem, a_full.at(g, use[t] + 1))
                nc.scalar.copy(dst, A_BANK[use[t]][:, 0:D].rearrange("p (c n) -> p c n", c=DC)).then_inc(sig.sem, 1)

            def query(g, half):
                for m in (2 * half, 2 * half + 1):
                    if m % 2 == 0:
                        act.wait_ge(a_full.sem, a_full.at(g, U_Q[m // 2] + 1))
                    bank = A_BANK[U_Q[m // 2]]
                    nc.scalar.activation(qT[:, m, :], bank[:, (m % 2) * GN:(m % 2 + 1) * GN], ACT.Identity,
                                         bias=bqk[:, 0, m:m + 1], scale=DH ** -0.5).then_inc(q_ok.sem, 1)

            def exps(g, t):
                act.wait_ge(mx_ok.sem, mx_ok.at(g, t + 1))
                for par in range(2):
                    for m in range(H // 2):
                        h = par * (H // 2) + m
                        s = s_sb[t][:, par, m, :]
                        nc.scalar.activation(s, s, ACT.Exp, bias=nmax[:, t, h:h + 1],
                                             accum_out=ssum[:, t, h:h + 1]).then_inc(p_ok.sem, 1)

            def prob_T(g, t):
                act.wait_ge(a_full.sem, a_full.at(g, U_PT[t][0] + 1))
                if t:
                    act.wait_ge(ctx_ok.sem, ctx_ok.at(g, t))
                else:
                    if past(g, 1):
                        act.wait_ge(ctx_ok.sem, ctx_ok.at(g - 1, 2))
                for par in range(2):
                    act.wait_ge(a_full.sem, a_full.at(g, U_PT[t][par] + 1))
                    nc.scalar.copy(pT[:, par, :, :], A_BANK[U_PT[t][par]][:].rearrange("p (m n) -> p m n", n=P)
                                   ).then_inc(pt_ok.sem, 1)

            def square(g, t, name, sig_in, src, dst, sig, scale=1.0):
                act.wait_ge(sig_in.sem, sig_in.at(g, t + 1))
                out, rows_in = squares[name][:, t, :] if name in squares else None, src[:, t, :]
                if name == "z":
                    out, rows_in = xnT[:, :, tok(t)], rows_in.rearrange("p (c n) -> p c n", c=DC)
                if name == "s":
                    out = (comb, disp)[t][:].rearrange("p t n -> p (t n)").bitcast(BF16)[:, 0:D]
                nc.scalar.activation(out, rows_in, ACT.Square, scale=scale, accum_out=dst[:, t, 0:1]).then_inc(sig.sem, 1)

            def silu(g, i):
                act.wait_ge(m_full.sem, m_full.at(g, i + 1))
                if i >= 2:
                    act.wait_ge(hl.sem, hl.at(g, i - 1))
                else:
                    if past(g, 1):
                        act.wait_ge(hl.sem, hl.at(g - 1, PAIRS - 1 + i))
                for half in range(2):
                    nc.scalar.activation(h_tmp[i % 2][:, half, :], m_bank[i % 2][:, half, :], ACT.Silu,
                                         bias=b1c[:, 2 * i + half:2 * i + half + 1]).then_inc(h_ok.sem, 1)

            def xnT_step(g, t):
                act.wait_ge(r_full.sem, r_full.at(g, t + 1))
                nc.scalar.copy(xnT[:, :, tok(t)], r_bank[:, 0:D].rearrange("p (c n) -> p c n", c=DC)).then_inc(xt_ok.sem, 1)

            def logits(g):
                act.wait_ge(r_full.sem, r_full.at(g, 3))
                nc.scalar.copy(logit[:], r_bank[:, 0:GN].rearrange("p (t n) -> p t n", t=GT)).then_inc(lg_ok.sem, 1)

            def comb_exp(g):
                act.wait_ge(lm_ok.sem, lm_ok.at(g, 1))
                for t in range(GT):
                    nc.scalar.activation(comb[:, t, :], logit[:, t, :], ACT.Exp, bias=lmx[:, 0, t:t + 1],
                                         accum_out=lsum[:, 0, t:t + 1]).then_inc(le_ok.sem, 1)

            def disp_exp(g):
                act.wait_ge(dm_ok.sem, dm_ok.at(g, 1))
                for t in range(GT):
                    nc.scalar.activation(disp[:, t, :], r_bank[:, tok(t)], ACT.Exp, bias=lmx[:, 1, t:t + 1],
                                         accum_out=lsum[:, 1, t:t + 1]).then_inc(de_ok.sem, 1)

            def weights_T(g):
                act.wait_ge(r_full.sem, r_full.at(g, 5))
                if past(g, 1):
                    act.wait_ge(comb_stored.sem, comb_stored.at(g - 1, 16))
                nc.scalar.copy(dcT[:].rearrange("p n t k -> p (n t k)"), r_bank[:]).then_inc(tt_ok.sem, 1)

            def body(a, m, r, n):
                A, M, R, N = (v is not None for v in (a, m, r, n))
                if A: query(a, 0); query(a, 1)
                if M: silu(m, 0)
                if R: square(r, 0, "z", z2_ok, xn, zms, zss); square(r, 1, "z", z2_ok, xn, zms, zss)
                if M: silu(m, 1)
                if R: xnT_step(r, 0)
                if A: exps(a, 0)
                if R: xnT_step(r, 1)
                if A: exps(a, 1); prob_T(a, 0)
                if R: logits(r); comb_exp(r)
                if A: prob_T(a, 1)
                if R: disp_exp(r)
                if A: hi_T(a, 0, U_CT, cT[0][:], ch)
                if M: silu(m, 2); silu(m, 3)
                if A: hi_T(a, 1, U_CT, cT[0][:], ch)
                if R: weights_T(r)
                if A: square(a, 0, "r", rb_ok, y, rms, rss, D ** -0.5)
                if M: silu(m, 4)
                if A: square(a, 1, "r", rb_ok, y, rms, rss, D ** -0.5)
                if N: hi_zT(n, 0)
                if R: square(r, 0, "s", sl_ok, yn, sms, sss)
                if M: silu(m, 5)
                if A: hi_yT(a, 0)
                if N: hi_zT(n, 1)
                if A: hi_yT(a, 1)
                if R: square(r, 1, "s", sl_ok, yn, sms, sss)
                if M: square(m, 0, "f", f_ok, f_sb, fms, fss, D ** -0.5); square(m, 1, "f", f_ok, f_sb, fms, fss, D ** -0.5)

            run(act, body)

        @block.vector
        def _(dve):
            def norm_stats(g, landed, k, src, s, v, sig_s, sig_v):
                for t in range(GT):
                    if t == 0 or k < 16:
                        dve.wait_ge(landed.sem, landed.at(g, k + t if k < 16 else k))
                    nc.vector.bn_stats(s[:, t, :], src[:, t, :]).then_inc(sig_s.sem, 1)
                dve.wait_ge(sig_s.sem, sig_s.at(g, GT))
                nc.vector.tensor_copy(counts[:], s[:, :, 0])
                for t in range(GT):
                    nc.vector.bn_aggr(v[:, t, :], s[:, t, :]).then_inc(sig_v.sem, 1)

            def centre(g, t, src, dst, v, r, sig_r, sig):
                dve.wait_ge(sig_r.sem, sig_r.at(g, 1))
                nc.vector.tensor_scalar(dst[:, t, :], src[:, t, :], v[:, t, 0:1], r[:, 1, t:t + 1],
                                        ALU.subtract, ALU.mult).then_inc(sig.sem, 1)

            def z_step(g, t):
                if past(g, 1):
                    dve.wait_ge(r_ok.sem, r_ok.at(g - 1, t + 1))
                dve.wait_ge(x_landed.sem, x_landed.at(g, 16))
                centre(g, t, x_in, z, mv, rstd, rstd_ok, z_ok)

            def lo_zT(g, t):
                dve.wait_ge(zh.sem, zh.at(g, t + 1))
                nc.vector.tensor_tensor(zT[1][:, :, tok(t)], ZT_BANK[t][:, 0:D].rearrange("p (c n) -> p c n", c=DC),
                                        zT[0][:, :, tok(t)].bitcast(F32), ALU.subtract).then_inc(zl.sem, 1)

            def lo_T(g, t, use, hi, lo, sig_hi, sig):
                dve.wait_ge(sig_hi.sem, sig_hi.at(g, t + 1))
                nc.vector.tensor_tensor(lo, A_BANK[use[t]][:, 0:D].rearrange("p (c n) -> p c n", c=DC),
                                        hi.bitcast(F32), ALU.subtract).then_inc(sig.sem, 1)

            def key(g, half):
                for m in (2 * half, 2 * half + 1):
                    if m % 2 == 0:
                        dve.wait_ge(a_full.sem, a_full.at(g, U_K[m // 2] + 1))
                    bank = A_BANK[U_K[m // 2]]
                    nc.vector.tensor_scalar(kT[:, m, :], bank[:, (m % 2) * GN:(m % 2 + 1) * GN],
                                            bqk[:, 1, m:m + 1], None, ALU.add).then_inc(k_ok.sem, 1)

            def values(g, t):
                dve.wait_ge(a_full.sem, a_full.at(g, U_V[t] + 1))
                nc.vector.tensor_tensor(v_sb[:, t, :], A_BANK[U_V[t]][:, 0:D], rows["bv"][:], ALU.add).then_inc(v_ok.sem, 1)

            def scores(g, t):
                if t == 0:
                    dve.wait_ge(adj_landed.sem, adj_landed.at(g, 16))
                for par in range(2):
                    dve.wait_ge(a_full.sem, a_full.at(g, U_S[t][par] + 1))
                    nc.vector.tensor_tensor(s_sb[t][:, par, :, :], A_BANK[U_S[t][par]][:].rearrange("p (m n) -> p m n", n=P),
                                            adj_sb[:, t, :].unsqueeze(1).broadcast_to([P, H // 2, P]), ALU.add).then_inc(sc_ok.sem, 1)
                dve.wait_ge(sc_ok.sem, sc_ok.at(g, 2 * t + 2))
                nc.vector.tensor_reduce(nmax[:, t, :], s_sb[t][:].rearrange("p a m n -> p (a m) n"), X_AXIS, ALU.max,
                                        negate=True).then_inc(mx_ok.sem, 1)

            def recips(g, t):
                dve.wait_ge(p_ok.sem, p_ok.at(g, 8 * (t + 1)))
                nc.vector.reciprocal(rsum[:, t, :], ssum[:, t, :]).then_inc(rs_ok.sem, 1)

            def context(g, t):
                dve.wait_ge(a_full.sem, a_full.at(g, U_CTX[t] + 1))
                dve.wait_ge(rs_ok.sem, rs_ok.at(g, t + 1))
                if t:
                    dve.wait_ge(a_full.sem, a_full.at(g, U_CT[0] + 1))
                else:
                    if past(g, 1):
                        dve.wait_ge(a_full.sem, a_full.at(g - 1, U_CT[1] + 1))
                nc.vector.tensor_tensor(
                    ctx_sb[:].rearrange("p (m a e) -> p m a e", a=2, e=DH),
                    A_BANK[U_CTX[t]][:, 0:D].rearrange("p (m a e) -> p m a e", a=2, e=DH),
                    rsum[:, t, :].rearrange("p (a m) -> p m a", a=2).unsqueeze(3).broadcast_to([P, H // 2, 2, DH]),
                    ALU.mult).then_inc(ctx_ok.sem, 1)

            def residual(g, t):
                dve.wait_ge(a_full.sem, a_full.at(g, U_WO[t] + 1))
                if past(g, 1):
                    dve.wait_ge(yb_ok.sem, yb_ok.at(g - 1, t + 1))
                nc.vector.tensor_tensor(y[:, t, :], A_BANK[U_WO[t]][:, 0:D], z[:, t, :], ALU.add).then_inc(r_ok.sem, 1)

            def y_scale(g, t):
                dve.wait_ge(rrs.sem, rrs.at(g, t + 1))
                dve.wait_ge(rb_ok.sem, rb_ok.at(g, t + 1))
                nc.vector.scalar_tensor_tensor(out=y[:, t, :], in0=y[:, t, :], scalar=rms[:, t, 2:3],
                                               in1=rows["alpha1"][:], op0=ALU.mult, op1=ALU.mult).then_inc(ys.sem, 1)

            def h_hi(g, i):
                dve.wait_ge(h_ok.sem, h_ok.at(g, 2 * i + 2))
                if i >= 3:
                    dve.wait_ge(h_used.sem, h_used.at(g, i - 2))
                else:
                    if past(g, 1):
                        dve.wait_ge(f_full.sem, f_full.at(g - 1, 2))
                nc.vector.tensor_copy(hT[i % 3][0][:], h_tmp[i % 2][:]).then_inc(hh.sem, 1)

            def f_sum(g, t):
                dve.wait_ge(f_full.sem, f_full.at(g, t + 1))
                dve.wait_ge(yb_ok.sem, yb_ok.at(g, t + 1))
                if past(g, 1):
                    dve.wait_ge(res_stored.sem, res_stored.at(g - 1, 16))
                nc.vector.tensor_tensor(f_sb[:, t, :], f_bank[t][:, 0:D], yb[:, t, :], ALU.add).then_inc(f_ok.sem, 1)

            def f_scale(g, t):
                dve.wait_ge(frs.sem, frs.at(g, t + 1))
                dve.wait_ge(f_ok.sem, f_ok.at(g, t + 1))
                nc.vector.scalar_tensor_tensor(out=f_sb[:, t, :], in0=f_sb[:, t, :], scalar=fms[:, t, 2:3],
                                               in1=rows["alpha2"][:], op0=ALU.mult, op1=ALU.mult).then_inc(fs.sem, 1)
                dve.wait_ge(fs.sem, fs.at(g, t + 1))
                dve.wait_ge(xg.sem, xg.at(g, t + 1))
                nc.vector.tensor_tensor(f_sb[:, t, :], f_sb[:, t, :], x_res[:, t, :], ALU.add).then_inc(xo.sem, 1)

            def r_scale(g):
                dve.wait_ge(zrs.sem, zrs.at(g, 1))
                dve.wait_ge(z2_ok.sem, z2_ok.at(g, 2))
                for t in range(GT):
                    nc.vector.scalar_tensor_tensor(out=xn[:, t, :], in0=xn[:, t, :], scalar=zms[:, t, 2:3],
                                                   in1=rows["gin"][:], op0=ALU.mult, op1=ALU.mult).then_inc(xn_ok.sem, 1)

            def row_max(g):
                dve.wait_ge(lg_ok.sem, lg_ok.at(g, 1))
                nc.vector.tensor_reduce(lmx[:, 0, :], logit[:], X_AXIS, ALU.max, negate=True).then_inc(lm_ok.sem, 1)

            def comb_norm(g):
                dve.wait_ge(le_ok.sem, le_ok.at(g, 2))
                nc.vector.reciprocal(lrec[:, 0, :], lsum[:, 0, :]).then_inc(lr_ok.sem, 1)
                dve.wait_ge(lr_ok.sem, lr_ok.at(g, 1))
                for t in range(GT):
                    nc.vector.tensor_scalar(comb[:, t, :], comb[:, t, :], lrec[:, 0, t:t + 1], None, ALU.mult).then_inc(cb_ok.sem, 1)

            def slot_max(g):
                dve.wait_ge(r_full.sem, r_full.at(g, 4))
                nc.vector.tensor_reduce(lmx[:, 1, :], r_bank[:, 0:GN].rearrange("p (t n) -> p t n", t=GT), X_AXIS,
                                        ALU.max, negate=True).then_inc(dm_ok.sem, 1)

            def disp_recip(g):
                dve.wait_ge(de_ok.sem, de_ok.at(g, 2))
                nc.vector.reciprocal(lrec[:, 1, :], lsum[:, 1, :]).then_inc(dr_ok.sem, 1)

            def slot_rows(g, t):
                dve.wait_ge(r_full.sem, r_full.at(g, 6 + t))
                dve.wait_ge(dr_ok.sem, dr_ok.at(g, 1))
                if past(g, 1):
                    dve.wait_ge(yn_stored.sem, yn_stored.at(g - 1, 16))
                nc.vector.tensor_scalar(yn[:, t, :], r_bank[:, 0:D], lrec[:, 1, t:t + 1], None, ALU.mult).then_inc(sl_ok.sem, 1)

            def yn_scale(g, t):
                dve.wait_ge(srs.sem, srs.at(g, t + 1))
                dve.wait_ge(sl_ok.sem, sl_ok.at(g, t + 1))
                nc.vector.scalar_tensor_tensor(out=yn[:, t, :], in0=yn[:, t, :], scalar=sms[:, t, 2:3],
                                               in1=rows["g2"][:], op0=ALU.mult, op1=ALU.mult).then_inc(yn_ok.sem, 1)

            def body(a, m, r, n):
                A, M, R, N = (v is not None for v in (a, m, r, n))
                if R:
                    norm_stats(r, xo, 1, f_sb, st2, mv2, st2_ok, mv2_ok)
                    if past(r, 1):
                        dve.wait_ge(r_full.sem, r_full.at(r - 1, 7))
                    for t in range(GT): centre(r, t, f_sb, xn, mv2, rstd2, rstd2_ok, z2_ok)
                if A: key(a, 0)
                if M: h_hi(m, 0)
                if A: key(a, 1)
                if R: r_scale(r)
                if M: h_hi(m, 1)
                if A: values(a, 0); values(a, 1); scores(a, 0); scores(a, 1); recips(a, 0)
                if N: norm_stats(n, x_landed, 16, x_in, st, mv, stats, meanvar)
                if R: row_max(r)
                if A: context(a, 0); recips(a, 1)
                if R: slot_max(r); comb_norm(r)
                if A: lo_T(a, 0, U_CT, cT[0][:], cT[1][:], ch, cl)
                if R: disp_recip(r)
                if M: h_hi(m, 2)
                if A: context(a, 1)
                if M: h_hi(m, 3)
                if A: residual(a, 0); lo_T(a, 1, U_CT, cT[0][:], cT[1][:], ch, cl)
                if N: z_step(n, 0)
                if A: y_scale(a, 0); residual(a, 1)
                if N: z_step(n, 1)
                if M: h_hi(m, 4)
                if A: y_scale(a, 1)
                if N: lo_zT(n, 0)
                if R: slot_rows(r, 0)
                if M: h_hi(m, 5)
                if A: lo_T(a, 0, U_YT, yT[0][:, :, tok(0)], yT[1][:, :, tok(0)], yh, yl)
                if N: lo_zT(n, 1)
                if R: yn_scale(r, 0)
                if A: lo_T(a, 1, U_YT, yT[0][:, :, tok(1)], yT[1][:, :, tok(1)], yh, yl)
                if R: slot_rows(r, 1)
                if M: f_sum(m, 0); f_sum(m, 1)
                if R: yn_scale(r, 1)
                if M: f_scale(m, 0); f_scale(m, 1)

            run(dve, body)

        @block.gpsimd
        def _(pool):
            def power(g, k, sig_in, src, small, mid, dst, sig_mid, sig_out, kk):
                n = src.shape[1]
                pool.wait_ge(sig_in.sem, sig_in.at(g, k))
                nc.gpsimd.tensor_tensor(mid, src, small[:, 0:n], ALU.add).then_inc(sig_mid.sem, 1)
                pool.wait_ge(sig_mid.sem, sig_mid.at(g, kk))
                nc.gpsimd.tensor_tensor(dst, mid, nhalf[:, 0:n], ALU.pow).then_inc(sig_out.sem, 1)

            def h_lo(g, i):
                pool.wait_ge(hh.sem, hh.at(g, i + 1))
                nc.gpsimd.tensor_tensor(hT[i % 3][1][:], h_tmp[i % 2][:], hT[i % 3][0][:].bitcast(F32),
                                        ALU.subtract).then_inc(hl.sem, 1)

            def r_bias(g, t):
                pool.wait_ge(r_ok.sem, r_ok.at(g, t + 1))
                nc.gpsimd.tensor_tensor(y[:, t, :], y[:, t, :], rows["bo"][:], ALU.add).then_inc(rb_ok.sem, 1)

            def y_shift(g, t):
                pool.wait_ge(ys.sem, ys.at(g, t + 1))
                nc.gpsimd.tensor_tensor(y[:, t, :], y[:, t, :], rows["gamma1"][:], ALU.add).then_inc(y_ok.sem, 1)

            def body(a, m, r, n):
                A, M, R, N = (v is not None for v in (a, m, r, n))
                if R: power(r, 2, mv2_ok, mv2[:, :, 1], eps_ln, rstd2[:, 0, :], rstd2[:, 1, :], ve2, rstd2_ok, 1)
                if M:
                    for t in range(GT):
                        pool.wait_ge(y_ok.sem, y_ok.at(m, t + 1))
                        if past(m, 1):
                            pool.wait_ge(f_ok.sem, f_ok.at(m - 1, t + 1))
                        nc.gpsimd.tensor_tensor(yb[:, t, :], y[:, t, :], rows["b2"][:], ALU.add).then_inc(yb_ok.sem, 1)
                if R: power(r, 2, zss, zms[:, :, 0], eps, zms[:, :, 1], zms[:, :, 2], zve, zrs, 1)
                if M:
                    h_lo(m, 0); h_lo(m, 1)
                    pool.wait_ge(res_landed.sem, res_landed.at(m, 16))
                    for t in range(GT):
                        nc.gpsimd.tensor_tensor(x_res[:, t, :], x_res[:, t, :], rows["gamma2"][:], ALU.add).then_inc(xg.sem, 1)
                if N: power(n, 2, meanvar, mv[:, :, 1], eps_ln, rstd[:, 0, :], rstd[:, 1, :], ve, rstd_ok, 1)
                if M: h_lo(m, 2); h_lo(m, 3)
                if A:
                    r_bias(a, 0)
                    power(a, 1, rss, rms[:, 0, 0:1], eps, rms[:, 0, 1:2], rms[:, 0, 2:3], rve, rrs, 1)
                    y_shift(a, 0)
                    r_bias(a, 1)
                    power(a, 2, rss, rms[:, 1, 0:1], eps, rms[:, 1, 1:2], rms[:, 1, 2:3], rve, rrs, 2)
                if M: h_lo(m, 4)
                if A: y_shift(a, 1)
                if R: power(r, 1, sss, sms[:, 0, 0:1], eps, sms[:, 0, 1:2], sms[:, 0, 2:3], sve, srs, 1)
                if M: h_lo(m, 5)
                if R: power(r, 2, sss, sms[:, 1, 0:1], eps, sms[:, 1, 1:2], sms[:, 1, 2:3], sve, srs, 2)
                if M:
                    for t in range(GT):
                        power(m, t + 1, fss, fms[:, t, 0:1], eps, fms[:, t, 1:2], fms[:, t, 2:3], fve, frs, t + 1)

            run(pool, body)


def run(eng, body):
    body(None, None, None, 0)
    body(0, None, None, 1)
    body(1, 0, None, 2)
    with eng.Fori(2, NG - 1) as g:
        body(g, g - 1, g - 2, g + 1)
    body(NG - 1, NG - 2, NG - 3, None)
    body(None, NG - 1, NG - 2, None)
    body(None, None, NG - 1, None)


def routes(nc, ctx, sb, ps, sem, ident, nhalf, eps, w_slot2, yn_dram, se_dram):
    HB = 2
    QC = E2 * D // 4
    NP = HB * E2
    BANKS = 4
    raw = [sb(ctx, f"ws_raw{i}", [P, DC, E2 * D]) for i in range(2)]
    ws = [[sb(ctx, f"ws_{i}_{s}", [P, DC, E2 * D], F32R) for s in range(2)] for i in range(2)]
    yk = [[sb(ctx, f"yk{j}{i}", [P, NS, D]) for i in range(HB)] for j in range(2)]
    mean = [sb(ctx, f"mean{i}", [P, D]) for i in range(HB)]
    mT = [[sb(ctx, f"mT_{i}_{s}", [P, DC, HB, P], F32R) for s in range(2)] for i in range(2)]
    se = [sb(ctx, f"se{i}", [P, E2, D]) for i in range(HB)]
    squares = sb(ctx, "se_squares", [P, HB, E2, D], BF16)
    ms = sb(ctx, "r_ms", [P, 3, NP])
    t_bank = [ps(ctx, f"rt_bank{i}", [P, DC, P]) for i in range(HB)]
    bank = [ps(ctx, f"rs_bank{i}", [P, 512]) for i in range(BANKS)]
    w_landed = [sem(ctx, f"ws_landed{i}", 16) for i in range(2)]
    y_landed = [[sem(ctx, f"yk_landed{j}{i}", 16) for i in range(HB)] for j in range(2)]
    w_hi, w_lo = sem(ctx, "ws_hi", 4), sem(ctx, "ws_lo", 4)
    added, t_full, m_hi, m_lo = sem(ctx, "added", 3 * HB), sem(ctx, "mT_full", HB), sem(ctx, "mT_hi", HB), sem(ctx, "mT_lo", HB)
    full, sq, ve, rs, scaled = (sem(ctx, n, NP) for n in ("se_full", "se_ss", "se_ve", "se_rs", "se_ok"))
    stored = [sem(ctx, f"se_stored{i}", 16) for i in range(HB)]
    yn_by_k = yn_dram.rearrange("b (k m n) d -> b k m (n d)", k=E1, n=NS)

    def over_experts(eng, body):
        for k in range(2):
            body(k, k, 0, k + 1)
        with eng.Fori(1, E1 // 2 - 1) as h:
            for j in range(2):
                body(2 * h + j, j, h, 2 * h + j + 1)
        body(E1 - 2, 0, E1 // 2 - 1, E1 - 1)
        body(E1 - 1, 1, E1 // 2 - 1, None)

    with nc.Block() as block:
        @block.sync
        def _(sp):
            def load(k, j):
                if past(k, 2):
                    sp.wait_ge(w_lo.sem, w_lo.at(k - 2, 4))
                sp.dma_start(raw[j][:], w_slot2[bass.ds(k, 1)].rearrange("o (c p) f -> p (o c) f", p=P)).then_inc(w_landed[j].sem, 16)
                for i in range(HB):
                    if past(k, 2):
                        sp.wait_ge(added.sem, added.at(k - 2, 3 * (i + 1)))
                    sp.dma_start(yk[j][i][:].rearrange("p n d -> p (n d)"),
                                 yn_by_k[i * NB // HB:(i + 1) * NB // HB, bass.ds(k, 1)].rearrange("b o m q -> (b o) m q")
                                 ).then_inc(y_landed[j][i].sem, 16)

            def body(k, j, h, nxt):
                if not isinstance(k, int) or k < E1 - 2:
                    load(k + 2, j)
                for i in range(HB):
                    sp.wait_ge(scaled.sem, scaled.at(k, E2 * (i + 1)))
                    sp.dma_start(se_dram[bass.ds(k, 1), i * P:(i + 1) * P, :].rearrange("o r q -> (o r) q"),
                                 se[i][:].rearrange("p e d -> p (e d)")).then_inc(stored[i].sem, 16)

            load(0, 0)
            load(1, 1)
            over_experts(sp, body)
            for s in stored:
                sp.wait_ge(s.sem, 16 * E1)

        @block.tensor
        def _(pe):
            def means_T(k):
                for i in range(HB):
                    pe.wait_ge(added.sem, added.at(k, 3 * (i + 1)))
                    if past(k, 1):
                        pe.wait_ge(m_lo.sem, m_lo.at(k - 1, i + 1))
                    for c in range(DC):
                        mm = pe.transpose(t_bank[i][:, c, :], mean[i][:, c * P:(c + 1) * P], ident[:])
                    mm.then_inc(t_full.sem, 1)

            def body(k, j, h, nxt):
                for n in range(NP):
                    i, e = divmod(n, E2)
                    if i == 0:
                        pe.wait_ge(w_lo.sem, w_lo.at(k, e + 1))
                    if e == 0:
                        pe.wait_ge(m_lo.sem, m_lo.at(k, i + 1))
                    if n >= BANKS:
                        pe.wait_ge(scaled.sem, scaled.at(k, n - BANKS + 1))
                    elif past(k, 1):
                        pe.wait_ge(scaled.sem, scaled.at(k - 1, NP - BANKS + n + 1))
                    for c in range(DC):
                        for q, (x, w) in enumerate(((0, 0), (0, 1), (1, 0))):
                            mm = pe.matmul(bank[n % BANKS][:, 0:D], mT[j][x][:, c, i, :], ws[j][w][:, c, e * D:(e + 1) * D],
                                           start=c == 0 and q == 0, stop=c == DC - 1 and q == 2)
                    mm.then_inc(full.sem, 1)
                    if n == NP - 3 and nxt is not None:
                        means_T(nxt)

            means_T(0)
            over_experts(pe, body)

        @block.scalar
        def _(act):
            def split(k, j, h, q):
                if q == 0:
                    act.wait_ge(w_landed[j].sem, w_landed[j].at(h, 16))
                    if past(k, 2):
                        act.wait_ge(full.sem, full.at(k - 2, NP))
                nc.scalar.copy(ws[j][0][:, :, q * QC:(q + 1) * QC], raw[j][:, :, q * QC:(q + 1) * QC]).then_inc(w_hi.sem, 1)

            def means_hi(k, j):
                if past(k, 2):
                    act.wait_ge(full.sem, full.at(k - 2, NP))
                for i in range(HB):
                    act.wait_ge(t_full.sem, t_full.at(k, i + 1))
                    nc.scalar.activation(mT[j][0][:, :, i, :], t_bank[i][:], ACT.Identity, scale=1.0 / NS).then_inc(m_hi.sem, 1)

            def body(k, j, h, nxt):
                for n in range(NP):
                    i, e = divmod(n, E2)
                    act.wait_ge(full.sem, full.at(k, n + 1))
                    if past(k, 1):
                        act.wait_ge(ve.sem, ve.at(k - 1, n + 1))
                    nc.scalar.activation(squares[:, i, e, :], bank[n % BANKS][:, 0:D], ACT.Square, accum_out=ms[:, 0, n:n + 1]).then_inc(sq.sem, 1)
                    if nxt is not None:
                        if n < 4:
                            split(nxt, 1 - j, h + j, n)
                        elif n == NP - 2:
                            means_hi(nxt, 1 - j)

            for q in range(4):
                split(0, 0, 0, q)
            means_hi(0, 0)
            over_experts(act, body)

        @block.vector
        def _(dve):
            def split(k, j, q):
                dve.wait_ge(w_hi.sem, w_hi.at(k, q + 1))
                nc.vector.tensor_tensor(ws[j][1][:, :, q * QC:(q + 1) * QC], raw[j][:, :, q * QC:(q + 1) * QC],
                                        ws[j][0][:, :, q * QC:(q + 1) * QC].bitcast(F32), ALU.subtract).then_inc(w_lo.sem, 1)

            def means_lo(k, j):
                for i in range(HB):
                    dve.wait_ge(m_hi.sem, m_hi.at(k, i + 1))
                    nc.vector.scalar_tensor_tensor(out=mT[j][1][:, :, i, :], in0=t_bank[i][:], scalar=1.0 / NS,
                                                   in1=mT[j][0][:, :, i, :].bitcast(F32), op0=ALU.mult,
                                                   op1=ALU.subtract).then_inc(m_lo.sem, 1)

            def scale(k, n):
                i, e = divmod(n, E2)
                if e == 0 and past(k, 1):
                    dve.wait_ge(stored[i].sem, stored[i].at(k - 1, 16))
                dve.wait_ge(rs.sem, rs.at(k, n + 1))
                nc.vector.tensor_scalar(se[i][:, e, :], bank[n % BANKS][:, 0:D], ms[:, 2, n:n + 1], SCALE,
                                        ALU.mult, ALU.mult).then_inc(scaled.sem, 1)

            def body(k, j, h, nxt):
                for n in range(NP):
                    dve.wait_ge(sq.sem, sq.at(k, n + 1))
                    nc.vector.tensor_tensor(ms[:, 1, n:n + 1], ms[:, 0, n:n + 1], eps[:, 0:1], ALU.add).then_inc(ve.sem, 1)
                    if n:
                        scale(k, n - 1)
                    if nxt is not None:
                        if n < 4:
                            split(nxt, 1 - j, n)
                        elif n == NP - 2:
                            means_lo(nxt, 1 - j)
                scale(k, NP - 1)

            for q in range(4):
                split(0, 0, q)
            means_lo(0, 0)
            over_experts(dve, body)

        @block.gpsimd
        def _(pool):
            def add(k, j, h, i, n):
                if n == 0:
                    pool.wait_ge(y_landed[j][i].sem, y_landed[j][i].at(h, 16))
                    if past(k, 1):
                        pool.wait_ge(t_full.sem, t_full.at(k - 1, i + 1))
                else:
                    pool.wait_ge(added.sem, added.at(k, 3 * i + n))
                nc.gpsimd.tensor_tensor(mean[i][:], mean[i][:] if n else yk[j][i][:, 0, :], yk[j][i][:, n + 1, :],
                                        ALU.add).then_inc(added.sem, 1)

            def body(k, j, h, nxt):
                for n in range(NP):
                    pool.wait_ge(ve.sem, ve.at(k, n + 1))
                    nc.gpsimd.tensor_tensor(ms[:, 2, n:n + 1], ms[:, 1, n:n + 1], nhalf[:, 0:1], ALU.pow).then_inc(rs.sem, 1)
                    if nxt is not None and n < 3:
                        for q in (2 * n, 2 * n + 1):
                            add(nxt, 1 - j, h + j, q // 3, q % 3)

            for n in range(6):
                add(0, 0, 0, n // 3, n % 3)
            over_experts(pool, body)


def dispatch(nc, ctx, sb, ps, sem, ident, yn_dram, se_dram, comb_dram, ct_dram, slots2T):
    G = 2
    NP = NB // G
    RING = 4
    yn = [sb(ctx, f"d_yn{i}", [P, G, D]) for i in range(RING)]
    se = [sb(ctx, f"d_se{i}", [P, G, D]) for i in range(RING)]
    cb = [sb(ctx, f"d_cb{i}", [P, G, P]) for i in range(RING)]
    ynT = [sb(ctx, f"d_ynT{i}", [P, G, D]) for i in range(2)]
    seT = [sb(ctx, f"d_seT{i}", [P, G, D]) for i in range(2)]
    lm = sb(ctx, "d_lm", [P, G, P])
    lg = [sb(ctx, f"d_lg{i}", [P, G, 2, P]) for i in range(2)]
    dT = [sb(ctx, f"d_dT{i}", [P, G, P]) for i in range(2)]
    ct = [sb(ctx, f"d_ct{i}", [P, G, P]) for i in range(2)]
    mx = sb(ctx, "d_mx", [P, 2, G, 2])
    sm = sb(ctx, "d_sm", [P, 2, G, 2])
    rc = sb(ctx, "d_rc", [P, 2, G, 2])
    mask = sb(ctx, "d_mask", [P, P])
    yb = ps(ctx, "d_yb", [P, 512])
    eb = ps(ctx, "d_eb", [P, 512])
    lb = ps(ctx, "d_lb", [P, G, P])
    tb = ps(ctx, "d_tb", [P, G, P])
    wb = ps(ctx, "d_wb", [P, G, P])
    ob = [ps(ctx, f"d_ob{g}", [P, 512]) for g in range(G)]
    landed = [sem(ctx, f"d_landed{i}", 64) for i in range(RING)]
    stored = [sem(ctx, f"d_stored{i}", 16) for i in range(2)]
    y_full, e_full, l_full, t_full, w_full, s_full, c_full = (sem(ctx, n, c) for n, c in (
        ("d_y_full", G), ("d_e_full", G), ("d_l_full", 1), ("d_t_full", 1), ("d_w_full", 1), ("d_s_full", G),
        ("d_c_full", 1)))
    ynT_ok, seT_ok, lg_ok, mx_ok, cmx_ok, ex_ok, cex_ok, rc_ok, nm_ok, dT_ok, s_ok, ct_ok, mask_ok = (
        sem(ctx, n, c) for n, c in (
            ("d_ynT", G), ("d_seT", G), ("d_lg", 1), ("d_row_max", 1), ("d_col_max", 1), ("d_row_exp", G),
            ("d_col_exp", G), ("d_recip", 1), ("d_norm", 1), ("d_dT", 1), ("d_s", G), ("d_ct", 1), ("d_mask", 1)))
    se_by_b = se_dram.rearrange("k (b m) (e d) -> b k (m e) d", m=M2, e=E2)

    def over_steps(eng, body):
        for i in range(RING):
            body(0, i)
        with eng.Fori(1, NP // RING) as r:
            for i in range(RING):
                body(r, i)
        for i in range(2):
            body(NP // RING, i)

    def before(r, i, lag):
        pair = (r, i - lag) if i >= lag else (r - 1, i - lag + RING)
        there = not isinstance(r, int) or 0 <= pair[0] * RING + pair[1] < NP
        return pair if there else None

    with nc.Block() as block:
        @block.sync
        def _(sp):
            def load(r, i):
                first = r * (RING * G) + i * G
                if past(r, 1):
                    sp.wait_ge(s_full.sem, s_full.at(r * RING - RING + i, G))
                sp.dma_start(yn[i][:], yn_dram[bass.ds(first, G)].rearrange("g p d -> p g d")).then_inc(landed[i].sem, 16)
                for g in range(G):
                    sp.dma_start(se[i][:, g, :], se_by_b[bass.ds(first + g, 1)].rearrange("o k r d -> (o k) r d")
                                 ).then_inc(landed[i].sem, 16)
                if past(r, 1):
                    sp.wait_ge(c_full.sem, c_full.at(r * RING - RING + i, 1))
                sp.dma_start(cb[i][:], comb_dram[bass.ds(first, G)].rearrange("g p d -> p g d")).then_inc(landed[i].sem, 16)

            def store(r, i):
                sp.wait_ge(ct_ok.sem, ct_ok.at(r * RING + i, 1))
                sp.dma_start(ct_dram[bass.ds(r * (RING * G) + i * G, G)].rearrange("g p d -> p g d"), ct[i % 2][:]
                             ).then_inc(stored[i % 2].sem, 16)

            for i in range(RING):
                load(0, i)
            with sp.Fori(1, NP // RING) as r:
                for i in range(RING):
                    load(r, i)
                    store(r - 1, i)
            for i in range(RING):
                store(NP // RING - 1, i)
            for s in stored:
                sp.wait_ge(s.sem, 16 * NP // 2)

        @block.gpsimd
        def _(pool):
            nc.gpsimd.memset(mask[:], 0.0).then_inc(mask_ok.sem, 1)
            pool.wait_ge(mask_ok.sem, 1)
            blocks = mask[:].rearrange("p (k j) -> p k j", k=E1)
            nc.gpsimd.affine_select(out=blocks, in_=blocks, compare_op=ALU.is_ge, fill=MASKED, base=0,
                                    pattern=[[-S1, E1], [0, S1]], channel_multiplier=1).then_inc(mask_ok.sem, 1)
            pool.wait_ge(mask_ok.sem, 2)
            nc.gpsimd.affine_select(out=blocks, in_=blocks, compare_op=ALU.is_ge, fill=MASKED, base=S1 - 1,
                                    pattern=[[S1, E1], [0, S1]], channel_multiplier=-1).then_inc(mask_ok.sem, 1)

        @block.tensor
        def _(pe):
            def turn(r, i, g, src, bank, full, read):
                n = r * RING + i
                if g == 0:
                    pe.wait_ge(landed[i].sem, landed[i].at(r, 64))
                if g:
                    pe.wait_ge(read.sem, read.at(n, g))
                elif past(n, 1):
                    pe.wait_ge(read.sem, read.at(n - 1, G))
                for c in range(DC):
                    mm = pe.transpose(bank[:, c * P:(c + 1) * P], src[i][:, g, c * P:(c + 1) * P], ident[:])
                mm.then_inc(full.sem, 1)

            def logits(r, i, g):
                n = r * RING + i
                if g == 0:
                    pe.wait_ge(ynT_ok.sem, ynT_ok.at(n, G))
                    pe.wait_ge(seT_ok.sem, seT_ok.at(n, G))
                    if past(n, 1):
                        pe.wait_ge(lg_ok.sem, lg_ok.at(n - 1, 1))
                for c in range(DC):
                    mm = pe.matmul(lb[:, g, :], ynT[i % 2][:, g, c * P:(c + 1) * P], seT[i % 2][:, g, c * P:(c + 1) * P],
                                   start=c == 0, stop=c == DC - 1)
                if g == G - 1:
                    mm.then_inc(l_full.sem, 1)

            def logits_T(r, i):
                n = r * RING + i
                pe.wait_ge(lg_ok.sem, lg_ok.at(n, 1))
                if past(n, 1):
                    pe.wait_ge(cex_ok.sem, cex_ok.at(n - 1, G))
                for g in range(G):
                    mm = pe.transpose(tb[:, g, :], lm[:, g, :], ident[:])
                mm.then_inc(t_full.sem, 1)

            def disp_T(r, i):
                n = r * RING + i
                pe.wait_ge(nm_ok.sem, nm_ok.at(n, 1))
                if past(n, 1):
                    pe.wait_ge(ct_ok.sem, ct_ok.at(n - 1, 1))
                for g in range(G):
                    mm = pe.transpose(wb[:, g, :], lg[i % 2][:, g, 1, :], ident[:])
                mm.then_inc(w_full.sem, 1)

            def back(r, i):
                n = r * RING + i
                pe.wait_ge(dT_ok.sem, dT_ok.at(n, 1))
                for g in range(G):
                    mm = pe.matmul(wb[:, g, :], lg[i % 2][:, g, 0, :], cb[i][:, g, :], start=True, stop=True)
                mm.then_inc(c_full.sem, 1)
                for g in range(G):
                    if past(n, 1):
                        pe.wait_ge(s_ok.sem, s_ok.at(n - 1, g + 1))
                    for c in range(DC):
                        mm = pe.matmul(ob[g][:, c * P:(c + 1) * P], yn[i][:, g, c * P:(c + 1) * P], dT[i % 2][:, g, :],
                                       start=True, stop=True)
                    mm.then_inc(s_full.sem, 1)

            def body(r, i):
                this, last, last2 = before(r, i, 0), before(r, i, 1), before(r, i, 2)
                if this:
                    turn(*this, 0, yn, yb, y_full, ynT_ok)
                    turn(*this, 0, se, eb, e_full, seT_ok)
                if last:
                    logits(*last, 0)
                if last2:
                    disp_T(*last2)
                if last:
                    logits(*last, 1)
                if this:
                    turn(*this, 1, yn, yb, y_full, ynT_ok)
                    turn(*this, 1, se, eb, e_full, seT_ok)
                if last:
                    logits_T(*last)
                if last2:
                    back(*last2)

            over_steps(pe, body)

        @block.scalar
        def _(act):
            def turn(r, i, g):
                n = r * RING + i
                act.wait_ge(y_full.sem, y_full.at(n, g + 1))
                if past(n, 2):
                    act.wait_ge(l_full.sem, l_full.at(n - 2, 1))
                nc.scalar.copy(ynT[i % 2][:, g, :], yb[:, 0:D]).then_inc(ynT_ok.sem, 1)

            def row_exps(r, i):
                n = r * RING + i
                act.wait_ge(mx_ok.sem, mx_ok.at(n, 1))
                if past(n, 2):
                    act.wait_ge(c_full.sem, c_full.at(n - 2, 1))
                for g in range(G):
                    nc.scalar.activation(lg[i % 2][:, g, 0, :], lm[:, g, :], ACT.Exp, bias=mx[:, i % 2, 0, g:g + 1],
                                         accum_out=sm[:, i % 2, g, 0:1]).then_inc(ex_ok.sem, 1)

            def col_exps(r, i):
                n = r * RING + i
                act.wait_ge(cmx_ok.sem, cmx_ok.at(n, 1))
                for g in range(G):
                    nc.scalar.activation(lg[i % 2][:, g, 1, :], tb[:, g, :], ACT.Exp, bias=mx[:, i % 2, 1, g:g + 1],
                                         accum_out=sm[:, i % 2, g, 1:2]).then_inc(cex_ok.sem, 1)

            def disp_T(r, i):
                n = r * RING + i
                act.wait_ge(w_full.sem, w_full.at(n, 1))
                if past(n, 2):
                    act.wait_ge(s_full.sem, s_full.at(n - 2, G))
                nc.scalar.copy(dT[i % 2][:], wb[:]).then_inc(dT_ok.sem, 1)

            def back(r, i):
                n = r * RING + i
                for g in range(G):
                    act.wait_ge(s_full.sem, s_full.at(n, g + 1))
                    nc.scalar.copy(slots2T[:, :, :, bass.ds(n * G + g, 1), :].rearrange("p k c o j -> p c k (o j)"),
                                   ob[g][:, 0:D].rearrange("p (c k j) -> p c k j", c=DC, k=E1)).then_inc(s_ok.sem, 1)

            def body(r, i):
                this, last, last2 = before(r, i, 0), before(r, i, 1), before(r, i, 2)
                if this:
                    turn(*this, 0)
                if last2:
                    disp_T(*last2)
                if this:
                    turn(*this, 1)
                if last:
                    row_exps(*last)
                    col_exps(*last)
                if last2:
                    back(*last2)

            over_steps(act, body)

        @block.vector
        def _(dve):
            def turn(r, i, g):
                n = r * RING + i
                dve.wait_ge(e_full.sem, e_full.at(n, g + 1))
                if past(n, 2):
                    dve.wait_ge(l_full.sem, l_full.at(n - 2, 1))
                nc.vector.tensor_copy(seT[i % 2][:, g, :], eb[:, 0:D]).then_inc(seT_ok.sem, 1)

            def logits(r, i):
                n = r * RING + i
                dve.wait_ge(l_full.sem, l_full.at(n, 1))
                if past(n, 1):
                    dve.wait_ge(t_full.sem, t_full.at(n - 1, 1))
                    dve.wait_ge(ex_ok.sem, ex_ok.at(n - 1, G))
                nc.vector.tensor_tensor(lm[:], lb[:], mask[:].unsqueeze(1).broadcast_to([P, G, P]), ALU.add
                                        ).then_inc(lg_ok.sem, 1)
                dve.wait_ge(lg_ok.sem, lg_ok.at(n, 1))
                nc.vector.tensor_reduce(mx[:, i % 2, 0], lm[:], X_AXIS, ALU.max, negate=True).then_inc(mx_ok.sem, 1)

            def col_max(r, i):
                n = r * RING + i
                dve.wait_ge(t_full.sem, t_full.at(n, 1))
                nc.vector.tensor_reduce(mx[:, i % 2, 1], tb[:], X_AXIS, ALU.max, negate=True).then_inc(cmx_ok.sem, 1)

            def norms(r, i):
                n = r * RING + i
                dve.wait_ge(ex_ok.sem, ex_ok.at(n, G))
                dve.wait_ge(cex_ok.sem, cex_ok.at(n, G))
                nc.vector.reciprocal(rc[:, i % 2].rearrange("p g k -> p (g k)"),
                                     sm[:, i % 2].rearrange("p g k -> p (g k)")).then_inc(rc_ok.sem, 1)
                dve.wait_ge(rc_ok.sem, rc_ok.at(n, 1))
                flat = lg[i % 2][:].rearrange("p g k n -> p (g k) n")
                nc.vector.tensor_tensor(flat, flat, rc[:, i % 2].rearrange("p g k -> p (g k)").unsqueeze(2).broadcast_to(
                    [P, 2 * G, P]), ALU.mult).then_inc(nm_ok.sem, 1)

            def back(r, i):
                n = r * RING + i
                dve.wait_ge(c_full.sem, c_full.at(n, 1))
                if past(n, 2):
                    dve.wait_ge(stored[i % 2].sem, 16 * (r * (RING // 2) + i // 2))
                nc.vector.tensor_copy(ct[i % 2][:], wb[:]).then_inc(ct_ok.sem, 1)

            def body(r, i):
                this, last, last2 = before(r, i, 0), before(r, i, 1), before(r, i, 2)
                if last2:
                    norms(*last2)
                if this:
                    turn(*this, 0)
                if last:
                    logits(*last)
                if this:
                    turn(*this, 1)
                if last:
                    col_max(*last)
                if last2:
                    back(*last2)

            dve.wait_ge(mask_ok.sem, 3)
            over_steps(dve, body)


def experts(nc, ctx, sb, ps, sem, ident, slots2T, w1, b1, w2, b2, o_dram, res_dram, early, res_landed):
    PIECES = 4
    CH = HID // P // PIECES
    W = CH * P
    BANKS = 4
    raw1 = [sb(ctx, f"raw1_{i}", [P, DC, 2, W]) for i in range(PIECES)]
    raw2 = [sb(ctx, f"raw2_{i}", [P, CH, D]) for i in range(PIECES)]
    w1s = [[sb(ctx, f"x_w1_{i}_{s}", [P, DC, 2, W], F32R) for s in range(2)] for i in range(2)]
    w2s = [[sb(ctx, f"x_w2_{i}_{s}", [P, CH, D], F32R) for s in range(2)] for i in range(2)]
    xT = [[sb(ctx, f"x_in_{i}_{s}", [P, DC, XR], F32R) for s in range(2)] for i in range(2)]
    gel = sb(ctx, "x_gelu", [P, CH, XR])
    aT = [sb(ctx, f"x_act_{i}", [P, CH, XR]) for i in range(2)]
    aTs = [[sb(ctx, f"x_aT_{i}_{s}", [P, CH, XR], F32R) for s in range(2)] for i in range(2)]
    o_sb = sb(ctx, "x_o", [P, 2, D])
    b1r = sb(ctx, "x_b1r", [NX, 2 * HID])
    b1T = sb(ctx, "x_b1T", [P, 2 * HID // P, NX])
    b2r = [sb(ctx, f"x_b2r{i}", [P, D]) for i in range(2)]
    u_bank = [ps(ctx, f"u_bank{i}", [P, 2, XR]) for i in range(BANKS)]
    o_bank = [[ps(ctx, f"o_bank{i}{t}", [P, 512]) for t in range(2)] for i in range(2)]

    raw1_landed = [sem(ctx, f"raw1_landed{i}", 32) for i in range(PIECES)]
    raw2_landed = [sem(ctx, f"raw2_landed{i}", 16) for i in range(PIECES)]
    b1_landed, b2_landed = sem(ctx, "b1_landed", 16), [sem(ctx, f"b2_landed{i}", 16) for i in range(2)]
    b1_T, b1_ok = sem(ctx, "b1_T"), sem(ctx, "b1_ok")
    w1_hi, w1_lo, w2_hi, w2_lo = (sem(ctx, n, PIECES) for n in ("w1_hi", "w1_lo", "w2_hi", "w2_lo"))
    xh, xl = sem(ctx, "x_hi"), sem(ctx, "x_lo")
    u_full, g_ok, a_ok = (sem(ctx, n, PIECES * CH) for n in ("u_full", "gelu_ok", "act_ok"))
    ah, al = sem(ctx, "act_hi", PIECES), sem(ctx, "act_lo", PIECES)
    down_done, o_ok = sem(ctx, "down_done", PIECES), sem(ctx, "o_ok", 2)
    o_stored = sem(ctx, "o_stored", 32)
    w1x = w1.rearrange("k e (c p) (g h) -> (k e) p c g h", p=P, g=2)
    w2x = w2.rearrange("k e (c p) d -> (k e) p c d", p=P)
    b2x = b2.rearrange("k e d -> (k e) d")
    o_rows = o_dram.rearrange("(b k m e) d -> k e b m d", k=E1, m=M2, e=E2)
    slots_of = slots2T[:].rearrange("p k c b (m e) -> p k c b m e", m=M2)

    def over_experts(eng, body):
        for e in range(E2):
            body(e, 0, e)
        with eng.Fori(1, E1 - 1) as k:
            for e in range(E2):
                body(k * E2 + e, k, e)
        for e in range(E2):
            body((E1 - 1) * E2 + e, E1 - 1, e)

    def is_last(x):
        return isinstance(x, int) and x == NX - 1

    with nc.Block() as block:
        @block.sync
        def _(sp):
            sp.dma_start(b1r[:], b1.rearrange("k e h -> (k e) h")).then_inc(b1_landed.sem, 16)

            def load(x, i):
                if past(x, 1):
                    sp.wait_ge(w1_lo.sem, w1_lo.at(x - 1, i + 1))
                for g in range(2):
                    sp.dma_start(raw1[i][:, :, g, :], w1x[bass.ds(x, 1), :, :, g, i * W:(i + 1) * W].rearrange(
                        "o p c h -> (o p) c h")).then_inc(raw1_landed[i].sem, 16)
                if past(x, 1):
                    sp.wait_ge(w2_lo.sem, w2_lo.at(x - 1, i + 1))
                sp.dma_start(raw2[i][:], w2x[bass.ds(x, 1), :, i * CH:(i + 1) * CH, :].rearrange(
                    "o p c d -> (o p) c d")).then_inc(raw2_landed[i].sem, 16)

            def load_b2(x, e):
                if past(x, 2):
                    sp.wait_ge(o_ok.sem, o_ok.at(x - 2, 2))
                sp.dma_start(b2r[e % 2][:], b2x[bass.ds(x, 1)].rearrange("o d -> (o d)").partition_broadcast(P)
                             ).then_inc(b2_landed[e % 2].sem, 16)

            def store(x, k, e):
                sp.wait_ge(o_ok.sem, o_ok.at(x, 2))
                for t in range(2):
                    sp.dma_start(o_rows[bass.ds(k, 1), e, t * NB // 2:(t + 1) * NB // 2].rearrange("o b m d -> (o b) m d"),
                                 o_sb[:, t, :]).then_inc(o_stored.sem, 16)

            def load_early(e):
                sp.wait_ge(xl.sem, xl.at(NX - E2 - 1, 1))
                for n in range(e, EARLY // ROUND, E2):
                    sp.dma_start(early[:, n * ROUND:(n + 1) * ROUND, :],
                                 res_dram[n * ROUND * P:(n + 1) * ROUND * P, :].rearrange("(g p) d -> p g d", p=P)
                                 ).then_inc(res_landed.sem, 16)

            def body(x, k, e):
                for i in range(PIECES):
                    load(x, i)
                    if i == 2:
                        if past(x, 2):
                            store(x - 2, k if e >= 2 else k - 1, (e - 2) % E2)
                        load_b2(x, e)
                if isinstance(k, int) and k == E1 - 1:
                    load_early(e)
            over_experts(sp, body)
            for e in (E2 - 2, E2 - 1):
                store(NX - E2 + e, E1 - 1, e)
            sp.wait_ge(o_stored.sem, o_stored.n * NX)
            sp.wait_ge(res_landed.sem, 16 * (EARLY // ROUND))

        @block.tensor
        def _(pe):
            pe.wait_ge(b1_landed.sem, 16)
            for j in range(2 * HID // P):
                mm = pe.transpose(u_bank[0][:].rearrange("p a b -> p (a b)")[:, j * NX:(j + 1) * NX],
                                  b1r[:, j * P:(j + 1) * P], ident[0:NX, 0:NX])
            mm.then_inc(b1_T.sem, 1)
            pe.wait_ge(b1_ok.sem, 1)

            def up(x, e, i):
                if i == 0:
                    pe.wait_ge(xl.sem, xl.at(x, 1))
                pe.wait_ge(w1_lo.sem, w1_lo.at(x, i + 1))
                for c2 in range(CH):
                    n = i * CH + c2
                    if n >= BANKS:
                        pe.wait_ge(a_ok.sem, a_ok.at(x, n - BANKS + 1))
                    elif past(x, 1):
                        pe.wait_ge(a_ok.sem, a_ok.at(x - 1, PIECES * CH - BANKS + n + 1))
                    for g in range(2):
                        for c in range(DC):
                            for j, (a, b) in enumerate(((0, 0), (0, 1), (1, 0))):
                                mm = pe.matmul(u_bank[n % BANKS][:, g, :], w1s[i % 2][a][:, c, g, c2 * P:(c2 + 1) * P],
                                               xT[e % 2][b][:, c, :], start=c == 0 and j == 0, stop=c == DC - 1 and j == 2)
                    mm.then_inc(u_full.sem, 1)

            def down(x, e, i):
                pe.wait_ge(w2_lo.sem, w2_lo.at(x, i + 1))
                pe.wait_ge(al.sem, al.at(x, i + 1))
                if i == 0 and past(x, 2):
                    pe.wait_ge(o_ok.sem, o_ok.at(x - 2, 2))
                for t in range(2):
                    for c2 in range(CH):
                        for j, (a, b) in enumerate(((0, 0), (0, 1), (1, 0))):
                            mm = pe.matmul(o_bank[e % 2][t][:, 0:D], aTs[i % 2][a][:, c2, t * P:(t + 1) * P],
                                           w2s[i % 2][b][:, c2, :], start=i == 0 and c2 == 0 and j == 0,
                                           stop=i == PIECES - 1 and c2 == CH - 1 and j == 2)
                mm.then_inc(down_done.sem, 1)

            def body(x, k, e):
                up(x, e, 0)
                if past(x, 1):
                    down(x - 1, (e - 1) % E2, PIECES - 1)
                for i in range(1, PIECES):
                    up(x, e, i)
                    down(x, e, i - 1)
            over_experts(pe, body)
            down(NX - 1, E2 - 1, PIECES - 1)

        @block.scalar
        def _(act):
            act.wait_ge(b1_T.sem, 1)
            nc.scalar.copy(b1T[:].rearrange("p j x -> p (j x)"), u_bank[0][:].rearrange("p a b -> p (a b)")).then_inc(b1_ok.sem, 1)
            act.wait_ge(b1_ok.sem, 1)

            def split_w1(x, i):
                act.wait_ge(raw1_landed[i].sem, raw1_landed[i].at(x, 32))
                if i >= 2:
                    act.wait_ge(u_full.sem, u_full.at(x, (i - 1) * CH))
                elif past(x, 1):
                    act.wait_ge(u_full.sem, u_full.at(x - 1, (i + PIECES - 1) * CH))
                nc.scalar.copy(w1s[i % 2][0][:], raw1[i][:]).then_inc(w1_hi.sem, 1)

            def rows_hi(x, k, e):
                if past(x, 2):
                    act.wait_ge(u_full.sem, u_full.at(x - 2, PIECES * CH))
                src = slots_of[:, bass.ds(k, 1), :, :, :, e]
                nc.scalar.copy(xT[e % 2][0][:].rearrange("p c (b m) -> p c b m", m=M2),
                               src.rearrange("p o c b m -> p (o c) b m")).then_inc(xh.sem, 1)

            def gelu(x, i):
                for c2 in range(CH):
                    n = i * CH + c2
                    if n >= CH:
                        act.wait_ge(a_ok.sem, a_ok.at(x, n - CH + 1))
                    elif past(x, 1):
                        act.wait_ge(a_ok.sem, a_ok.at(x - 1, (PIECES - 1) * CH + n + 1))
                    act.wait_ge(u_full.sem, u_full.at(x, n + 1))
                    nc.scalar.activation(gel[:, c2, :], u_bank[n % BANKS][:, 1, :], ACT.Gelu_apprx_tanh,
                                         bias=b1T[:, HID // P + n, bass.ds(x, 1)]).then_inc(g_ok.sem, 1)

            def act_hi(x, i):
                act.wait_ge(a_ok.sem, a_ok.at(x, (i + 1) * CH))
                if i >= 2:
                    act.wait_ge(down_done.sem, down_done.at(x, i - 1))
                elif past(x, 1):
                    act.wait_ge(down_done.sem, down_done.at(x - 1, i + 3))
                nc.scalar.copy(aTs[i % 2][0][:], aT[i % 2][:]).then_inc(ah.sem, 1)

            def body(x, k, e):
                for i in range(PIECES):
                    gelu(x, i)
                    if i < 2:
                        split_w1(x, i + 2)
                    elif not is_last(x):
                        split_w1(x + 1, i - 2)
                    act_hi(x, i)
                    if i == 1 and not is_last(x):
                        rows_hi(x + 1, k if e < E2 - 1 else k + 1, (e + 1) % E2)
            rows_hi(0, 0, 0)
            for i in range(2):
                split_w1(0, i)
            over_experts(act, body)

        @block.vector
        def _(dve):
            dve.wait_ge(b1_ok.sem, 1)

            def split_w1(x, i):
                dve.wait_ge(w1_hi.sem, w1_hi.at(x, i + 1))
                nc.vector.tensor_tensor(w1s[i % 2][1][:], raw1[i][:], w1s[i % 2][0][:].bitcast(F32), ALU.subtract).then_inc(w1_lo.sem, 1)

            def split_w2(x, i):
                dve.wait_ge(raw2_landed[i].sem, raw2_landed[i].at(x, 16))
                if i >= 2:
                    dve.wait_ge(down_done.sem, down_done.at(x, i - 1))
                elif past(x, 1):
                    dve.wait_ge(down_done.sem, down_done.at(x - 1, i + 3))
                nc.vector.tensor_copy(w2s[i % 2][0][:], raw2[i][:]).then_inc(w2_hi.sem, 1)

            def rows_lo(x, k, e):
                dve.wait_ge(xh.sem, xh.at(x, 1))
                src = slots_of[:, bass.ds(k, 1), :, :, :, e].rearrange("p o c b m -> p (o c) b m")
                nc.vector.tensor_tensor(xT[e % 2][1][:].rearrange("p c (b m) -> p c b m", m=M2), src,
                                        xT[e % 2][0][:].bitcast(F32).rearrange("p c (b m) -> p c b m", m=M2),
                                        ALU.subtract).then_inc(xl.sem, 1)

            def gate(x, i):
                for c2 in range(CH):
                    n = i * CH + c2
                    if c2 == 0:
                        if i >= 2:
                            dve.wait_ge(al.sem, al.at(x, i - 1))
                        elif past(x, 1):
                            dve.wait_ge(al.sem, al.at(x - 1, i + 3))
                    dve.wait_ge(g_ok.sem, g_ok.at(x, n + 1))
                    nc.vector.scalar_tensor_tensor(out=aT[i % 2][:, c2, :], in0=u_bank[n % BANKS][:, 0, :],
                                                   scalar=b1T[:, n, bass.ds(x, 1)], in1=gel[:, c2, :],
                                                   op0=ALU.add, op1=ALU.mult).then_inc(a_ok.sem, 1)

            def rows_out(x, k, e):
                dve.wait_ge(down_done.sem, down_done.at(x, PIECES))
                dve.wait_ge(b2_landed[e % 2].sem, 16 * (k * (E2 // 2) + e // 2 + 1))
                if past(x, 1):
                    dve.wait_ge(o_stored.sem, o_stored.at(x - 1, 32))
                for t in range(2):
                    nc.vector.tensor_tensor(o_sb[:, t, :], o_bank[e % 2][t][:, 0:D], b2r[e % 2][:], ALU.add).then_inc(o_ok.sem, 1)

            def body(x, k, e):
                for i in range(PIECES):
                    gate(x, i)
                    if i < 2:
                        split_w1(x, i + 2)
                    elif not is_last(x):
                        split_w1(x + 1, i - 2)
                    if i == 0 and past(x, 1):
                        rows_out(x - 1, k if e else k - 1, (e - 1) % E2)
                    if i < PIECES - 1:
                        split_w2(x, i + 1)
                    elif not is_last(x):
                        split_w2(x + 1, 0)
                    if i == 1 and not is_last(x):
                        rows_lo(x + 1, k if e < E2 - 1 else k + 1, (e + 1) % E2)
            rows_lo(0, 0, 0)
            for i in range(2):
                split_w1(0, i)
            split_w2(0, 0)
            over_experts(dve, body)
            rows_out(NX - 1, E1 - 1, E2 - 1)

        @block.gpsimd
        def _(pool):
            def split_w2(x, i):
                pool.wait_ge(w2_hi.sem, w2_hi.at(x, i + 1))
                nc.gpsimd.tensor_tensor(w2s[i % 2][1][:], raw2[i][:], w2s[i % 2][0][:].bitcast(F32), ALU.subtract).then_inc(w2_lo.sem, 1)

            def act_lo(x, i):
                pool.wait_ge(ah.sem, ah.at(x, i + 1))
                nc.gpsimd.tensor_tensor(aTs[i % 2][1][:], aT[i % 2][:], aTs[i % 2][0][:].bitcast(F32), ALU.subtract).then_inc(al.sem, 1)

            def body(x, k, e):
                for i in range(PIECES):
                    act_lo(x, i)
                    if i < PIECES - 1:
                        split_w2(x, i + 1)
                    elif not is_last(x):
                        split_w2(x + 1, 0)
            split_w2(0, 0)
            over_experts(pool, body)


def combine(nc, ctx, sb, ps, sem, ct_dram, o_dram, res_dram, out, early, res_landed):
    G = 2
    BUF = ROUND // G
    ROUNDS = NB // ROUND
    o_sb = [sb(ctx, f"c_o{i}", [P, G, D]) for i in range(BUF)]
    ct = [sb(ctx, f"c_ct{i}", [P, G, P]) for i in range(BUF)]
    late = sb(ctx, "c_late", [P, NB - EARLY, D])
    y = [sb(ctx, f"c_y{i}", [P, G, D]) for i in range(BUF)]
    bank = [[ps(ctx, f"c_bank{i}{g}", [P, 512]) for g in range(G)] for i in range(BUF)]
    landed = [sem(ctx, f"c_landed{i}", 32) for i in range(BUF)]
    stored = [sem(ctx, f"c_stored{i}", 16) for i in range(BUF)]
    full, added = sem(ctx, "c_full", ROUND), sem(ctx, "c_added", ROUND)
    out_rows = out.rearrange("b n d -> (b n) d")

    def loop(eng, body):
        for i in range(BUF):
            body(0, i)
        with eng.Fori(1, EARLY // ROUND) as r:
            for i in range(BUF):
                body(r, i)
        for r in range(EARLY // ROUND, ROUNDS):
            for i in range(BUF):
                body(r, i)

    def rows_of(t, r, i):
        return t[bass.ds(r * (ROUND * P) + i * G * P, G * P), :].rearrange("(g p) d -> p g d", p=P)

    with nc.Block() as block:
        @block.sync
        def _(sp):
            def body(r, i):
                if past(r, 1):
                    sp.wait_ge(full.sem, full.at(r - 1, G * (i + 1)))
                sp.dma_start(o_sb[i][:], rows_of(o_dram, r, i)).then_inc(landed[i].sem, 16)
                sp.dma_start(ct[i][:], ct_dram[bass.ds(r * ROUND + i * G, G)].rearrange("g p n -> p g n")).then_inc(landed[i].sem, 16)
                if isinstance(r, int) and r == 0 and i == BUF - 1:
                    sp.dma_start(late[:], res_dram[EARLY * P:NB * P, :].rearrange("(g p) d -> p g d", p=P)
                                 ).then_inc(res_landed.sem, 16)
            loop(sp, body)

        @block.tensor
        def _(pe):
            def body(r, i):
                pe.wait_ge(landed[i].sem, landed[i].at(r, 32))
                for g in range(G):
                    if past(r, 1):
                        pe.wait_ge(added.sem, added.at(r - 1, G * i + g + 1))
                    pe.matmul(bank[i][g][:, 0:D], ct[i][:, g, :], o_sb[i][:, g, :], start=True, stop=True).then_inc(full.sem, 1)
            loop(pe, body)

        @block.vector
        def _(dve):
            def body(r, i):
                if past(r, 1):
                    dve.wait_ge(stored[i].sem, stored[i].at(r - 1, 16))
                for g in range(G):
                    if isinstance(r, int) and r * ROUND >= EARLY:
                        dve.wait_ge(res_landed.sem, 16 * (EARLY // ROUND + 1))
                        x_of = late[:, r * ROUND + i * G + g - EARLY, :]
                    else:
                        x_of = early[:, bass.ds(r * ROUND + i * G + g, 1), :].rearrange("p o d -> p (o d)")
                    dve.wait_ge(full.sem, full.at(r, G * i + g + 1))
                    nc.vector.tensor_tensor(y[i][:, g, :], bank[i][g][:, 0:D], x_of, ALU.add).then_inc(added.sem, 1)
            loop(dve, body)

        @block.scalar
        def _(act):
            def body(r, i):
                act.wait_ge(added.sem, added.at(r, G * (i + 1)))
                act.dma_start(rows_of(out_rows, r, i), y[i][:]).then_inc(stored[i].sem, 16)
            loop(act, body)
            for s in stored:
                act.wait_ge(s.sem, 16 * ROUNDS)


_INS = ['x', 'adj', 'L0_gnn_wq', 'L0_gnn_bq', 'L0_gnn_wk', 'L0_gnn_bk', 'L0_gnn_wv', 'L0_gnn_bv', 'L0_gnn_wo',
        'L0_gnn_bo', 'L0_gnn_w1', 'L0_gnn_b1', 'L0_gnn_w2', 'L0_gnn_b2', 'L0_gnn_alpha1', 'L0_gnn_gamma1',
        'L0_gnn_alpha2', 'L0_gnn_gamma2', 'L0_ffn_gamma_in', 'L0_ffn_slots1', 'L0_ffn_gamma2', 'L0_ffn_w_slot2',
        'L0_ffn_w1', 'L0_ffn_b1', 'L0_ffn_w2', 'L0_ffn_b2']


def kernel(**inputs):
    import numpy as _np
    import concourse.bacc as _bacc
    from concourse import mybir as _mybir
    from concourse.bass_utils import run_bass_kernel_spmd as _run

    nc = _bacc.Bacc("TRN2", target_bir_lowering=False, num_devices=1, dynamic_dma_scratch_size=1024)
    arrays, args = {}, []
    for name in _INS:
        a = _np.ascontiguousarray(inputs[name])
        arrays[f"in_{name}_dram"] = a
        args.append(nc.dram_tensor(f"in_{name}_dram", a.shape, _mybir.dt.from_np(a.dtype), kind="ExternalInput").ap())
    args.append(nc.dram_tensor("out_0_dram", (NB, P, D), F32, kind="ExternalOutput").ap())
    build(nc, *args)
    r = _run(nc, [arrays], core_ids=[0])
    return r.results[0]["out_0_dram"]
```
